# Optimizing a Trainium2 kernel written in Bass

```python
import numpy as np
import jax
import jax.numpy as jnp

def _softmax(x, axis=-1):
    return jax.nn.softmax(x, axis=axis)

def _gelu(x):
    return jax.nn.gelu(x, approximate=True)

def _silu(x):
    return jax.nn.silu(x)

def _sigmoid(x):
    return jax.nn.sigmoid(x)

def _layernorm(x, axis=-1, eps=1e-05):
    m = jnp.mean(x, axis=axis, keepdims=True)
    v = jnp.var(x, axis=axis, keepdims=True)
    return (x - m) / jnp.sqrt(v + eps)

def _scatter_add(tgt, idx, src, axis=0):
    return tgt.at[idx].add(src)

def _segment_sum(src, seg, n):
    return jax.ops.segment_sum(src, seg, n)
kernel_name = 'mk_early_fusion_d1_tok_img768_r4_ad33c6'

def setup_inputs(seed: int=0):
    np.random.seed(seed)
    _w = jnp.asarray

    def _rec_inputs():
        import jax
        import jax.numpy as jnp
        _rk = jax.random.key(seed)
        x = -0.000596345 + 1.00056 * jax.random.normal(jax.random.fold_in(_rk, 1), (4, 3, 64, 64), jnp.float32)
        txt = -0.000190561 + 0.886117 * jax.random.normal(jax.random.fold_in(_rk, 2), (4, 128, 192), jnp.float32)
        return (x, txt)
    x, txt = _rec_inputs()

    def _L0_tok_setup():
        import jax, jax.numpy as jnp
        import numpy as np
        B = 16
        IMG = 64
        CH = 3
        EMBED = 64
        GP = 16
        PRE = [1, 2, 4]
        N_LEVELS = 3
        FUSED = EMBED * N_LEVELS

        def hilbert_flat_indices(n):
            t = np.arange(n * n, dtype=np.int64)
            x = np.zeros(n * n, dtype=np.int64)
            y = np.zeros(n * n, dtype=np.int64)
            s = 1
            while s < n:
                rx = 1 & t // 2
                ry = 1 & (t ^ rx)
                swap = ry == 0
                flip = swap & (rx == 1)
                x = np.where(flip, s - 1 - x, x)
                y = np.where(flip, s - 1 - y, y)
                x2 = np.where(swap, y, x)
                y2 = np.where(swap, x, y)
                x, y = (x2, y2)
                x = x + s * rx
                y = y + s * ry
                t = t // 4
                s *= 2
            return y * n + x

        def _level(x, idx, W, b, p, gp):
            Bsz, C, H, _ = x.shape
            h = H // p
            t = x.reshape(Bsz, C, h, p, h, p).transpose(0, 2, 4, 3, 5, 1).reshape(Bsz, h * h, p * p * C)
            t = t[:, idx]
            t = t.reshape(Bsz, h * h // gp, gp * p * p * C)
            return t @ W.T + b

        def _interp_linear(x, n_out):
            L = x.shape[1]
            pos = (jnp.arange(n_out, dtype=jnp.float32) + 0.5) * (L / n_out) - 0.5
            pos = jnp.clip(pos, 0.0, L - 1)
            i0 = jnp.floor(pos).astype(jnp.int32)
            i1 = jnp.minimum(i0 + 1, L - 1)
            w = (pos - i0).astype(x.dtype)
            return x[:, i0] * (1.0 - w)[None, :, None] + x[:, i1] * w[None, :, None]
        key = jax.random.key(seed)
        ks = jax.random.split(key, 9)
        inp = {'x': jax.random.normal(ks[0], (B, CH, IMG, IMG), jnp.float32)}
        for i, p in enumerate(PRE):
            din = CH * p * p * GP
            inp[f'W{i}'] = jax.random.normal(ks[1 + 2 * i], (EMBED, din), jnp.float32) * din ** (-0.5)
            inp[f'b{i}'] = jax.random.normal(ks[2 + 2 * i], (EMBED,), jnp.float32) * 0.02
        inp['Wf'] = jax.random.normal(ks[7], (FUSED, FUSED), jnp.float32) * FUSED ** (-0.5)
        inp['bf'] = jax.random.normal(ks[8], (FUSED,), jnp.float32) * 0.02
        for i, p in enumerate(PRE):
            inp[f'idx{i}'] = jnp.asarray(hilbert_flat_indices(IMG // p), jnp.int32)
        return inp
    _L0_tok_all = _L0_tok_setup()
    _L0_tok_in = {k: v for k, v in _L0_tok_all.items() if k in ('W0', 'b0', 'W1', 'b1', 'W2', 'b2', 'Wf', 'bf', 'idx0', 'idx1', 'idx2')}
    del _L0_tok_all

    def _L0_attn_setup():
        import jax, jax.numpy as jnp
        import numpy as np
        BATCH, SEQ, D_MODEL, D_STATE, K = (2, 512, 192, 16, 4)

        def _block(x, in_proj_w, conv_w, conv_b, dt_w, dt_b, B_w, C_w, A_log, D_param, out_w, ln_g, ln_b):
            B, L, D = x.shape
            residual = x
            xz = x @ in_proj_w.T
            x_branch, z = jnp.split(xz, 2, axis=-1)
            xc = jnp.transpose(x_branch, (0, 2, 1))
            xc = jax.lax.conv_general_dilated(xc, conv_w, (1,), [(3, 3)], feature_group_count=D, dimension_numbers=('NCH', 'OIH', 'NCH'))
            xc = xc[:, :, :L] + conv_b[None, :, None]
            u = jnp.transpose(jax.nn.silu(xc), (0, 2, 1))
            dt = jax.nn.softplus(u @ dt_w.T + dt_b)
            Bv = u @ B_w.T
            Cv = u @ C_w.T
            A = -jnp.exp(A_log)
            dA = jnp.exp(dt[..., None] * A)
            dBu = dt[..., None] * Bv[:, :, None, :] * u[..., None]

            def step(h, ins):
                dA_t, dBu_t, C_t = ins
                h = dA_t * h + dBu_t
                return (h, jnp.einsum('bdn,bn->bd', h, C_t))
            h0 = jnp.zeros((B, D, A.shape[1]), u.dtype)
            _, ys = jax.lax.scan(step, h0, (jnp.transpose(dA, (1, 0, 2, 3)), jnp.transpose(dBu, (1, 0, 2, 3)), jnp.transpose(Cv, (1, 0, 2))))
            y = jnp.transpose(ys, (1, 0, 2))
            y = y + D_param * u
            y = y * jax.nn.silu(z)
            y = y @ out_w.T
            r = y + residual
            mu = jnp.mean(r, axis=-1, keepdims=True)
            var = jnp.var(r, axis=-1, keepdims=True)
            return (r - mu) / jnp.sqrt(var + 1e-05) * ln_g + ln_b
        key = jax.random.key(seed)
        ks = jax.random.split(key, 8)
        s = 0.02
        x = jax.random.normal(ks[0], (BATCH, SEQ, D_MODEL), jnp.float32)
        in_proj_w = jax.random.normal(ks[1], (2 * D_MODEL, D_MODEL), jnp.float32) * s
        conv_w = jax.random.normal(ks[2], (D_MODEL, 1, K), jnp.float32) * 0.25
        conv_b = jnp.zeros((D_MODEL,), jnp.float32)
        dt_w = jax.random.normal(ks[3], (D_MODEL, D_MODEL), jnp.float32) * s
        dt_b = jnp.full((D_MODEL,), -4.0, jnp.float32)
        B_w = jax.random.normal(ks[4], (D_STATE, D_MODEL), jnp.float32) * s
        C_w = jax.random.normal(ks[5], (D_STATE, D_MODEL), jnp.float32) * s
        A_log = jnp.broadcast_to(jnp.log(jnp.arange(1, D_STATE + 1, dtype=jnp.float32)), (D_MODEL, D_STATE)) + 0.0
        D_param = jnp.ones((D_MODEL,), jnp.float32)
        out_w = jax.random.normal(ks[6], (D_MODEL, D_MODEL), jnp.float32) * s
        ln_g = jnp.ones((D_MODEL,), jnp.float32)
        ln_b = jnp.zeros((D_MODEL,), jnp.float32)
        return {'x': x, 'in_proj_w': in_proj_w, 'conv_w': conv_w, 'conv_b': conv_b, 'dt_w': dt_w, 'dt_b': dt_b, 'B_w': B_w, 'C_w': C_w, 'A_log': A_log, 'D_param': D_param, 'out_w': out_w, 'ln_g': ln_g, 'ln_b': ln_b}
    _L0_attn_all = _L0_attn_setup()
    _L0_attn_in = {k: v for k, v in _L0_attn_all.items() if k in ('in_proj_w', 'conv_w', 'conv_b', 'dt_w', 'dt_b', 'B_w', 'C_w', 'A_log', 'D_param', 'out_w', 'ln_g', 'ln_b')}
    del _L0_attn_all

    def _L0_ffn_setup():
        import jax, jax.numpy as jnp
        import numpy as np
        B, S, H, F, E, TOP_K = (4, 512, 192, 768, 8, 2)
        key = jax.random.key(seed)
        ks = jax.random.split(key, 6)
        x = jax.random.normal(ks[0], (B, S, H), dtype=jnp.float32)
        Wr = jax.random.normal(ks[1], (E, H), dtype=jnp.float32) * 0.02
        Wi = jax.random.normal(ks[2], (E, F, H), dtype=jnp.float32) * 0.02
        bi = jnp.zeros((E, F), dtype=jnp.float32)
        Wo = jax.random.normal(ks[3], (E, H, F), dtype=jnp.float32) * 0.02
        bo = jnp.zeros((E, H), dtype=jnp.float32)
        return {'x': x, 'Wr': Wr, 'Wi': Wi, 'bi': bi, 'Wo': Wo, 'bo': bo}
    _L0_ffn_all = _L0_ffn_setup()
    _L0_ffn_in = {k: v for k, v in _L0_ffn_all.items() if k in ('Wr', 'Wi', 'bi', 'Wo', 'bo')}
    del _L0_ffn_all
    return {'x': x, 'txt': txt, 'L0_tok_W0': _L0_tok_in['W0'], 'L0_tok_b0': _L0_tok_in['b0'], 'L0_tok_W1': _L0_tok_in['W1'], 'L0_tok_b1': _L0_tok_in['b1'], 'L0_tok_W2': _L0_tok_in['W2'], 'L0_tok_b2': _L0_tok_in['b2'], 'L0_tok_Wf': _L0_tok_in['Wf'], 'L0_tok_bf': _L0_tok_in['bf'], 'L0_tok_idx0': _L0_tok_in['idx0'], 'L0_tok_idx1': _L0_tok_in['idx1'], 'L0_tok_idx2': _L0_tok_in['idx2'], 'L0_attn_in_proj_w': _L0_attn_in['in_proj_w'], 'L0_attn_conv_w': _L0_attn_in['conv_w'], 'L0_attn_conv_b': _L0_attn_in['conv_b'], 'L0_attn_dt_w': _L0_attn_in['dt_w'], 'L0_attn_dt_b': _L0_attn_in['dt_b'], 'L0_attn_B_w': _L0_attn_in['B_w'], 'L0_attn_C_w': _L0_attn_in['C_w'], 'L0_attn_A_log': _L0_attn_in['A_log'], 'L0_attn_D_param': _L0_attn_in['D_param'], 'L0_attn_out_w': _L0_attn_in['out_w'], 'L0_attn_ln_g': _L0_attn_in['ln_g'], 'L0_attn_ln_b': _L0_attn_in['ln_b'], 'L0_ffn_Wr': _L0_ffn_in['Wr'], 'L0_ffn_Wi': _L0_ffn_in['Wi'], 'L0_ffn_bi': _L0_ffn_in['bi'], 'L0_ffn_Wo': _L0_ffn_in['Wo'], 'L0_ffn_bo': _L0_ffn_in['bo']}

def reference(x, txt, L0_tok_W0, L0_tok_b0, L0_tok_W1, L0_tok_b1, L0_tok_W2, L0_tok_b2, L0_tok_Wf, L0_tok_bf, L0_tok_idx0, L0_tok_idx1, L0_tok_idx2, L0_attn_in_proj_w, L0_attn_conv_w, L0_attn_conv_b, L0_attn_dt_w, L0_attn_dt_b, L0_attn_B_w, L0_attn_C_w, L0_attn_A_log, L0_attn_D_param, L0_attn_out_w, L0_attn_ln_g, L0_attn_ln_b, L0_ffn_Wr, L0_ffn_Wi, L0_ffn_bi, L0_ffn_Wo, L0_ffn_bo):
    import jax
    import jax.numpy as jnp

    def _L0_tok_ref(x, W0, b0, W1, b1, W2, b2, Wf, bf, idx0, idx1, idx2):
        import jax, jax.numpy as jnp
        import numpy as np
        B = 16
        IMG = 64
        CH = 3
        EMBED = 64
        GP = 16
        PRE = [1, 2, 4]
        N_LEVELS = 3
        FUSED = EMBED * N_LEVELS

        def hilbert_flat_indices(n):
            t = np.arange(n * n, dtype=np.int64)
            x = np.zeros(n * n, dtype=np.int64)
            y = np.zeros(n * n, dtype=np.int64)
            s = 1
            while s < n:
                rx = 1 & t // 2
                ry = 1 & (t ^ rx)
                swap = ry == 0
                flip = swap & (rx == 1)
                x = np.where(flip, s - 1 - x, x)
                y = np.where(flip, s - 1 - y, y)
                x2 = np.where(swap, y, x)
                y2 = np.where(swap, x, y)
                x, y = (x2, y2)
                x = x + s * rx
                y = y + s * ry
                t = t // 4
                s *= 2
            return y * n + x

        def _level(x, idx, W, b, p, gp):
            Bsz, C, H, _ = x.shape
            h = H // p
            t = x.reshape(Bsz, C, h, p, h, p).transpose(0, 2, 4, 3, 5, 1).reshape(Bsz, h * h, p * p * C)
            t = t[:, idx]
            t = t.reshape(Bsz, h * h // gp, gp * p * p * C)
            return t @ W.T + b

        def _interp_linear(x, n_out):
            L = x.shape[1]
            pos = (jnp.arange(n_out, dtype=jnp.float32) + 0.5) * (L / n_out) - 0.5
            pos = jnp.clip(pos, 0.0, L - 1)
            i0 = jnp.floor(pos).astype(jnp.int32)
            i1 = jnp.minimum(i0 + 1, L - 1)
            w = (pos - i0).astype(x.dtype)
            return x[:, i0] * (1.0 - w)[None, :, None] + x[:, i1] * w[None, :, None]
        Ws = [(idx0, W0, b0, PRE[0]), (idx1, W1, b1, PRE[1]), (idx2, W2, b2, PRE[2])]
        outs = [_level(x, idx, W, b, p, GP) for idx, W, b, p in Ws]
        n_tokens = outs[0].shape[1]
        outs = [outs[0]] + [_interp_linear(o, n_tokens) for o in outs[1:]]
        y = jnp.concatenate(outs, axis=-1)
        return y @ Wf.T + bf

    def _L0_attn_ref(x, in_proj_w, conv_w, conv_b, dt_w, dt_b, B_w, C_w, A_log, D_param, out_w, ln_g, ln_b):
        import jax, jax.numpy as jnp
        import numpy as np
        BATCH, SEQ, D_MODEL, D_STATE, K = (2, 512, 192, 16, 4)

        def _block(x, in_proj_w, conv_w, conv_b, dt_w, dt_b, B_w, C_w, A_log, D_param, out_w, ln_g, ln_b):
            B, L, D = x.shape
            residual = x
            xz = x @ in_proj_w.T
            x_branch, z = jnp.split(xz, 2, axis=-1)
            xc = jnp.transpose(x_branch, (0, 2, 1))
            xc = jax.lax.conv_general_dilated(xc, conv_w, (1,), [(3, 3)], feature_group_count=D, dimension_numbers=('NCH', 'OIH', 'NCH'))
            xc = xc[:, :, :L] + conv_b[None, :, None]
            u = jnp.transpose(jax.nn.silu(xc), (0, 2, 1))
            dt = jax.nn.softplus(u @ dt_w.T + dt_b)
            Bv = u @ B_w.T
            Cv = u @ C_w.T
            A = -jnp.exp(A_log)
            dA = jnp.exp(dt[..., None] * A)
            dBu = dt[..., None] * Bv[:, :, None, :] * u[..., None]

            def step(h, ins):
                dA_t, dBu_t, C_t = ins
                h = dA_t * h + dBu_t
                return (h, jnp.einsum('bdn,bn->bd', h, C_t))
            h0 = jnp.zeros((B, D, A.shape[1]), u.dtype)
            _, ys = jax.lax.scan(step, h0, (jnp.transpose(dA, (1, 0, 2, 3)), jnp.transpose(dBu, (1, 0, 2, 3)), jnp.transpose(Cv, (1, 0, 2))))
            y = jnp.transpose(ys, (1, 0, 2))
            y = y + D_param * u
            y = y * jax.nn.silu(z)
            y = y @ out_w.T
            r = y + residual
            mu = jnp.mean(r, axis=-1, keepdims=True)
            var = jnp.var(r, axis=-1, keepdims=True)
            return (r - mu) / jnp.sqrt(var + 1e-05) * ln_g + ln_b
        return _block(x, in_proj_w, conv_w, conv_b, dt_w, dt_b, B_w, C_w, A_log, D_param, out_w, ln_g, ln_b)

    def _L0_ffn_ref(x, Wr, Wi, bi, Wo, bo):
        import jax, jax.numpy as jnp
        import numpy as np
        B, S, H, F, E, TOP_K = (4, 512, 192, 768, 8, 2)
        xf = x.reshape(-1, x.shape[-1])
        router_logits = jnp.einsum('th,eh->te', xf, Wr)
        topk_vals, topk_idx = jax.lax.top_k(router_logits, TOP_K)
        routing_weights = jax.nn.softmax(topk_vals, axis=-1)
        h = jnp.einsum('th,efh->etf', xf, Wi) + bi[:, None, :]
        h = jax.nn.gelu(h, approximate=False)
        expert_out = jnp.einsum('etf,ehf->eth', h, Wo) + bo[:, None, :]
        expert_out = jnp.transpose(expert_out, (1, 0, 2))
        gathered = jnp.take_along_axis(expert_out, topk_idx[:, :, None], axis=1)
        out = jnp.einsum('tk,tkh->th', routing_weights, gathered)
        return out.reshape(x.shape)
    h = _L0_tok_ref(x, L0_tok_W0, L0_tok_b0, L0_tok_W1, L0_tok_b1, L0_tok_W2, L0_tok_b2, L0_tok_Wf, L0_tok_bf, L0_tok_idx0, L0_tok_idx1, L0_tok_idx2)
    h = jnp.concatenate([h, txt], axis=1)
    h = h + _L0_attn_ref(_layernorm(h, axis=-1), L0_attn_in_proj_w, L0_attn_conv_w, L0_attn_conv_b, L0_attn_dt_w, L0_attn_dt_b, L0_attn_B_w, L0_attn_C_w, L0_attn_A_log, L0_attn_D_param, L0_attn_out_w, L0_attn_ln_g, L0_attn_ln_b)
    h = h + _L0_ffn_ref(_layernorm(h, axis=-1), L0_ffn_Wr, L0_ffn_Wi, L0_ffn_bi, L0_ffn_Wo, L0_ffn_bo)
    return h

_drawn_inputs = setup_inputs


def setup_inputs(seed=0):
    import zlib

    import numpy as np

    out = dict(_drawn_inputs(seed))
    spreads = {'L0_attn_conv_b': (0.0, 0.8),
     'L0_attn_dt_b': (-4.0, 0.6),
     'L0_attn_D_param': (1.0, 0.6),
     'L0_attn_ln_g': (1.0, 0.2),
     'L0_attn_ln_b': (0.0, 0.1),
     'L0_ffn_bi': (0.0, 0.757),
     'L0_ffn_bo': (0.0, 0.1)}
    factors = {'L0_tok_b0': 4.997,
     'L0_tok_b1': 5.188,
     'L0_tok_b2': 4.796,
     'L0_tok_bf': 2.755,
     'L0_attn_in_proj_w': 8.0,
     'L0_attn_conv_w': 8.0,
     'L0_attn_dt_w': 8.0,
     'L0_attn_B_w': 8.0,
     'L0_attn_C_w': 8.0,
     'L0_attn_A_log': 8.0,
     'L0_attn_out_w': 8.0}
    for name, (base, spread) in spreads.items():
        noise = np.random.default_rng([zlib.crc32(name.encode()), seed]).standard_normal(out[name].shape)
        drawn = base * np.exp(spread * noise) if base else spread * noise
        out[name] = jnp.asarray(drawn.astype(out[name].dtype))
    for name, factor in factors.items():
        out[name] = (out[name] * factor).astype(out[name].dtype)
    return out
```

```python
from contextlib import ExitStack

import concourse.bass as bass
import numpy as np
from concourse import mybir

F32 = mybir.dt.float32
BF16 = mybir.dt.bfloat16
I32 = mybir.dt.int32
U32 = mybir.dt.uint32
ALU = mybir.AluOpType
ACT = mybir.ActivationFunctionType
AX_X = mybir.AxisListType.X

P = 128
NB = 4
C = 192
CB = C - P
NJ = 3
L = NJ * P
NT = NJ * NB
EMB = 64
GROUP = 16
PATCH = [3, 12, 48]
N_IMG = 256
G0, G1, G2 = 32, 8, 2
S = 16
K = 4
U = 2 * L
E = 8
F = 768
FC = F // P
FH = F // 2
TOPK = 2
NTOK = NB * L
MT = (TOPK * NTOK + E * (P - 1)) // P
EPS = 1e-5
LOG1P = [0.9999999659255084, -0.4999944497632982, 0.33318121707353093, -0.2483539898720075, 0.19076880730853912,
         -0.13602247612385465, 0.0775160866235987, -0.029074064606579537, 0.0051261021233726485]

C_ID = 0
C_UP = C_ID + P
C_ROW = C_UP + P
C_NEG = C_ROW + 2 * S
C_E8 = C_NEG + 2
C_M12 = C_E8 + E
C_MASK = C_M12 + NT
C_T31 = C_MASK + E * NT
C_EPS = C_T31 + MT
N_CST = C_EPS + 1

H_W, H_CB, H_DTB, H_D, H_A = 0, 4, 5, 6, 7
N_CH = H_A + S


def constants():
    c = np.zeros((P, N_CST), np.float32)
    c[:, C_ID:C_ID + P] = np.eye(P)
    c[:, C_UP:C_UP + P] = np.triu(np.ones((P, P)), 1)
    for pair in range(2):
        for part in range(3):
            for s in range(S):
                c[64 * pair + S * part + s, C_ROW + S * pair + s] = 1
        c[64 * pair + S:64 * pair + 3 * S, C_NEG] = -1
        c[64 * pair + 2 * S:64 * pair + 3 * S, C_NEG + 1] = -1
    c[:, C_E8:C_E8 + E] = np.arange(E)
    c[:, C_M12:C_M12 + NT] = P * np.arange(NT)
    c[:, C_MASK:C_MASK + E * NT] = (np.arange(E * NT) % NT != 0)
    c[:, C_T31:C_T31 + MT] = np.arange(MT)
    c[:, C_EPS] = EPS
    return c


def interpolation(n_in, copies):
    pos = np.clip((np.arange(N_IMG) + 0.5) * (n_in / N_IMG) - 0.5, 0, n_in - 1)
    lo = np.floor(pos).astype(int)
    hi = np.minimum(lo + 1, n_in - 1)
    m = np.zeros((n_in, N_IMG), np.float32)
    m[lo, np.arange(N_IMG)] += 1 - (pos - lo)
    m[hi, np.arange(N_IMG)] += pos - lo
    out = np.zeros((copies, n_in, copies, N_IMG), np.float32)
    for k in range(copies):
        out[k, :, k] = m
    return out.reshape(copies * n_in, copies, N_IMG)


def build(nc, d, out):
    with ExitStack() as ctx:
        def sb(name, shape, dt=F32):
            return ctx.enter_context(nc.sbuf_tensor(name, shape, dt))

        def sem(name):
            return ctx.enter_context(nc.semaphore(name))

        cst = sb("cst", [P, N_CST])
        gidx = sb("gidx", [P, G0 + G1 + G2], I32)
        chan = sb("chan", [P, 2, N_CH])
        ln_gb = sb("ln_gb", [P, 2, C])
        b12 = sb("b12", [P, 1])
        b0 = sb("b0", [EMB, 1])
        ip_a = sb("ip_a", [P, 2 * C])
        ip_b = sb("ip_b", [CB, 2 * C])
        dw = sb("dw", [P, 2, C])
        bc = sb("bc", [P, 2, 2, 64])
        ow = sb("ow", [P, 2, C])
        wr = sb("wr", [P, 2, E])
        bo = sb("bo", [1, E * C])
        wi_a = sb("wi_a", [P, E * F])
        wi_b = sb("wi_b", [CB + 1, E * F])
        wo = sb("wo", [P, E * FC * C])

        h_tok = sb("h_tok", [P, NJ, NB, C])
        xn = sb("xn", [P, NJ, NB, C])
        x_cm = sb("x_cm", [P, 6 * (L + K - 1)])
        u_cm = sb("u_cm", [P, 6 * L])
        z_cm = sb("z_cm", [P, 6 * L])
        dt_cm = sb("dt_cm", [P, 6 * L])
        dtu_cm = sb("dtu_cm", [P, 6 * L])
        y_cm = sb("y_cm", [P, 6 * L])
        decay = sb("decay", [P, 2, 2, L])
        drive = sb("drive", [P, 2, L])
        state = sb("state", [P, 2, L])
        hc = sb("hc", [P, 2, L])
        pick = sb("pick", [P, 3, S, P], BF16)
        b_parts = sb("b_parts", [P, 2, L], BF16)
        c_parts = sb("c_parts", [P, 2, L], BF16)
        a_neg = sb("a_neg", [P, 2, S])
        ones_row = sb("ones_row", [1, P])
        ones_sq = sb("ones_sq", [P, P])
        stats = sb("stats", [P, NB, 6])
        mv = sb("mv", [P, NB, 2])
        std = sb("std", [P, NB])
        rstd = sb("rstd", [P, NB])
        gate = sb("gate", [P, TOPK, NT])
        gtmp = sb("gtmp", [P, 2, NT])
        tiles = sb("tiles", [P, E])
        ends = sb("ends", [P, E])
        first = sb("first", [P, E])
        slot = sb("slot", [P, TOPK, NT], I32)
        texi = sb("texi", [1, MT], I32)

        g0 = y_cm[:, 0:G0 * 12].rearrange("p (d r) -> p d r", d=G0)
        g1 = y_cm[:, 384:768].rearrange("p (d r) -> p d r", d=G1)
        g2 = y_cm[:, 768:1152].rearrange("p (d r) -> p d r", d=G2)
        r0 = y_cm[:, 1152:1536]
        r1 = y_cm[:, 1536:1920]
        t0 = dt_cm[0:48, 0:1024]
        t1 = dt_cm[0:96, 1024:1536]
        t2 = dtu_cm[0:48, 0:1024]
        y1 = dtu_cm[:, 1024:1152]
        y2 = dtu_cm[0:64, 1152:1216]
        i1 = u_cm[:, 0:512]
        i2 = u_cm[0:64, 512:1536]
        ycat_hi = decay[:, :, :, :].rearrange("p a b c -> p (a b c)")[:, 0:1024]
        ycat_lo = dt_cm[0:EMB + 1, 1536:2048]
        w2T = dtu_cm[0:PATCH[2], 1216:2240].rearrange("p (k e) -> p k e", k=GROUP)
        hcf = hc[:, :, :].rearrange("p a c -> p (a c)")
        w0T = hcf[0:PATCH[0] * GROUP, 0:EMB]
        w1T = hcf[0:96, EMB:3 * EMB].rearrange("p (k e) -> p k e", k=2)
        wf_hi = hcf[:, 192:384]
        wf_lo = hcf[0:EMB + 1, 384:576]
        xt_a = drive[:, :, :].rearrange("p a c -> p (a c)")[:, 0:512]
        xt_b = state[:, :, :].rearrange("p a c -> p (a c)")[0:CB, 0:512]
        decay_f = decay[:, :, :, :].rearrange("p a b c -> p (a b c)")
        used = 0

        def table(parts, *dims):
            nonlocal used
            t = decay_f[0:parts, used:used + int(np.prod(dims))]
            used += int(np.prod(dims))
            if len(dims) == 1:
                return t
            names = "abc"[:len(dims)]
            return t.rearrange(f"p ({' '.join(names)}) -> p {' '.join(names)}", **dict(zip(names, dims)))

        logit = table(P, NT, E)
        top_v = table(P, NT, 8)
        top_i = table(P, NT, 8).bitcast(U32)
        idf = table(P, NT, TOPK)
        hot = table(P, TOPK, NT, E)
        cnt = table(P, E, NT)
        run = table(P, E, NT)
        cmp12 = table(P, E, NT)
        pos = table(P, NT, E)
        pos_k = table(P, TOPK, NT, E)
        slot_f = table(P, TOPK, NT)
        tcmp = table(1, MT, E)
        tex = table(1, MT)
        xf = dt_cm[:, :].rearrange("p (t c) -> p t c", t=NT)
        rr = dtu_cm[:, 0:768].rearrange("p (t c) -> p t c", t=NB)
        xft_a = dtu_cm[:, 768:1280]
        xft_b = dtu_cm[0:CB, 1280:1792]
        zero = drive[:, :, :].rearrange("p a c -> p (a c)")[:, 0:C]
        x_in = u_cm[:, 0:2 * C].rearrange("p (n c) -> p n c", n=2)
        xe_a = u_cm[:, 384:640].rearrange("p (n c) -> p n c", n=2)
        xe_b = u_cm[0:CB + 1, 640:896].rearrange("p (n c) -> p n c", n=2)
        hid = u_cm[:, 896:1664]
        y_out = u_cm[:, 1664:2048].rearrange("p (n c) -> p n c", n=2)
        hid_t = y_cm[:, 0:F]
        got_y = [z_cm[:, 0:NT * C].rearrange("p (t c) -> p t c", t=NT),
                 x_cm[:, 0:NT * C].rearrange("p (t c) -> p t c", t=NT)]

        ps = ctx.enter_context(nc.psum_tensor("ps", [P, 8, 512], F32))

        def q3(t):
            return t[:, :].rearrange("p (q n) -> p q n", q=6)

        x3, u3, z3, dt3, dtu3, y3 = (q3(t) for t in (x_cm, u_cm, z_cm, dt_cm, dtu_cm, y_cm))
        ident = cst[:, C_ID:C_ID + P]
        xs_dram = nc.dram_tensor("xs_dram", [MT * P, C], F32, kind="Internal").ap()
        ys_dram = nc.dram_tensor("ys_dram", [MT * P, C], F32, kind="Internal").ap()

        ld_idx = sem("ld_idx")
        ld_cst = sem("ld_cst")
        ld_tok = sem("ld_tok")
        ld_mix = sem("ld_mix")
        ld_exp = sem("ld_exp")
        gath12 = sem("gath12")
        gath0 = [sem("gath0_0"), sem("gath0_1")]
        dve_set = sem("dve_set")
        rearr = sem("rearr")
        pe_tok = sem("pe_tok")
        ev_tok = sem("ev_tok")
        h_ready = sem("h_ready")
        ln_step = sem("ln_step")
        std_rdy = sem("std_rdy")
        xn_ready = sem("xn_ready")
        xt_ps = sem("xt_ps")
        xt_ready = sem("xt_ready")
        xz_ps = sem("xz_ps")
        xz_out = sem("xz_out")
        conv_step = sem("conv_step")
        u_ready = sem("u_ready")
        z_ready = sem("z_ready")
        dt_ps = sem("dt_ps")
        bc_ps = sem("bc_ps")
        bc_step = sem("bc_step")
        sp_abs = sem("sp_abs")
        sp_act = sem("sp_act")
        sp_dve = sem("sp_dve")
        log_step = sem("log_step")
        a_exp = sem("a_exp")
        decay_rdy = sem("decay_rdy")
        b_wide = sem("b_wide")
        c_wide = sem("c_wide")
        driven = sem("driven")
        scanned = sem("scanned")
        hc_rdy = sem("hc_rdy")
        summed = sem("summed")
        y_step = sem("y_step")
        attn_ps = sem("attn_ps")
        post = sem("post")
        mixed_free = sem("tops")
        xf_rdy = sem("xf_rdy")
        xft_ps = sem("xft_ps")
        xft_rdy = sem("xft_rdy")
        logit_ps = sem("logit_ps")
        route = sem("route")
        gate_e = sem("gate_e")
        cnt_ps = sem("cnt_ps")
        zeroed = sem("zeroed")
        sent = sem("sent")
        xin_l = [sem("xin_l0"), sem("xin_l1")]
        xe_ps = sem("xe_ps")
        xe_rdy = sem("xe_rdy")
        up_ps = sem("up_ps")
        hid_rdy = sem("hid_rdy")
        hidt_ps = sem("hidt_ps")
        hidt_rdy = sem("hidt_rdy")
        down_ps = sem("down_ps")
        y_rdy = sem("y_rdy")
        stored = [sem("stored0"), sem("stored1")]
        fetched = [sem(f"fetched{t}") for t in range(NT)]
        mixed = sem("mixed")
        out_st = sem("out_st")

        N_TOK, N_MIX, N_EXP = 10, 8, 4
        JS = [2, 0, 1]
        US = [2, 0, 1]

        def chan_group(u):
            return 1 if u == 2 else 0

        def unit(t, u, lo=0, n=L):
            return t[:, 2 * u:2 * u + 2, lo:lo + n]

        def bank2(b, n=L):
            return ps[:, b:b + 2, 0:n]

        block = ctx.enter_context(nc.Block())

        def expert_loop(eng, step):
            step(0, 0)
            step(1, 1)
            with eng.Fori(1, (MT - 3) // 2) as m:
                step(2 * m, 0)
                step(2 * m + 1, 1)
            for i in range(2 * ((MT - 3) // 2), MT):
                step(i, i % 2)

        def is_at_least(i, n):
            return not isinstance(i, int) or i >= n

        def is_below(i, n):
            return not isinstance(i, int) or i < n

        T_T1, T_T2, T_L12, T_UP = 1, 2, 3, 4
        V_T1, V_T2, V_L12, V_UP = 1, 3, 4, 6
        ROUTE_TOP = NT
        ROUTE_SLOT = NT + 20

        @block.sync
        def _(sp):
            sp.dma_start(gidx[:, :], d["gidx"]).then_inc(ld_idx, 16)
            sp.dma_start(h_tok[:, 2, :, :], d["txt"].rearrange("b p c -> p b c")).then_inc(h_ready, 16)
            sp.dma_start(cst[:, :], d["cst"]).then_inc(ld_cst, 16)
            for dst, name in ((w0T, "w0T"), (w1T, "w1T"), (w2T, "w2T"), (b12[:, :], "b12"),
                              (b0[:, :], "b0"), (wf_hi, "wf_hi"), (wf_lo, "wf_lo"), (i1, "i1"), (i2, "i2"),
                              (chan[:, :, :], "chan")):
                sp.dma_start(dst, d[name]).then_inc(ld_tok, 16)
            for dst, name in ((ip_a[:, :], "ip_a"), (ip_b[:, :], "ip_b"), (dw[:, :, :], "dw"), (bc[:, :, :, :], "bc"),
                              (ow[:, :, :], "ow"), (wr[:, :, :], "wr"), (bo[:, :], "bo")):
                sp.dma_start(dst, d[name]).then_inc(ld_mix, 16)
            sp.dma_start(ln_gb[:, :, :], d["ln_gb"].to_broadcast([P, 2, C])).then_inc(ld_mix, 16)
            for dst, name in ((wi_a[:, :], "wi_a"), (wi_b[:, :], "wi_b"), (wo[:, :], "wo")):
                sp.dma_start(dst, d[name]).then_inc(ld_exp, 16)
            sp.wait_ge(zeroed, 1)
            sp.dma_start(xs_dram.rearrange("(n p) c -> p n c", p=P),
                         zero.rearrange("p (n c) -> p n c", n=1).to_broadcast([P, MT, C])).then_inc(ld_exp, 16)

            sp.wait_ge(sent, 16 * TOPK * NT)

            def load_tokens(i, p):
                if is_at_least(i, 2):
                    sp.wait_ge(xe_ps, i - 1)
                sp.dma_start(x_in[:, p, :], xs_dram[bass.ds(i * P, P), :]).then_inc(xin_l[p], 16)
            expert_loop(sp, load_tokens)

            for t in range(NT):
                j, b = t // NB, t % NB
                sp.wait_ge(mixed, TOPK * (t + 1))
                sp.dma_start(out[b, j * P:(j + 1) * P, :], h_tok[:, j, b, :]).then_inc(out_st, 16)
            sp.wait_ge(out_st, 16 * NT)

        @block.gpsimd
        def _(pool):
            pool.wait_ge(ld_idx, 16)

            def gather(dst, table, col, signal):
                pool.indirect_dma_start(dst, None, d[table], bass.IndirectOffsetOnAxis(
                    ap=gidx[:, col:col + 1].bitcast(U32), axis=0)).then_inc(signal, 16)

            for n in range(G2):
                gather(g2[:, n, :], "pix2", G0 + G1 + n, gath12)
            for n in range(G1):
                gather(g1[:, n, :], "pix1", G0 + n, gath12)
            for n in range(G0):
                gather(g0[:, n, :], "pix0", n, gath0[n // GROUP])
            pool.wait_ge(route, ROUTE_SLOT)
            pool.wait_ge(ld_exp, 16 * N_EXP)
            pool.wait_ge(xf_rdy, NJ)
            for t in range(NT):
                for k in range(TOPK):
                    pool.indirect_dma_start(xs_dram, bass.IndirectOffsetOnAxis(
                        ap=slot[:, k, t:t + 1].bitcast(U32), axis=0), xf[:, t, :], None).then_inc(sent, 16)
            for p in range(2):
                pool.wait_ge(stored[p], 16 * ((MT + 1 - p) // 2))
            for t in range(NT):
                for k in range(TOPK):
                    pool.indirect_dma_start(got_y[k][:, t, :], None, ys_dram, bass.IndirectOffsetOnAxis(
                        ap=slot[:, k, t:t + 1].bitcast(U32), axis=0)).then_inc(fetched[t], 16)

        @block.tensor
        def _(pe):
            pe.wait_ge(ld_cst, 16)
            pe.wait_ge(ld_tok, 16 * N_TOK)
            pe.wait_ge(rearr, 1)
            for b in range(NB):
                mm = nc.tensor.transpose(ps[0:96, 0, P * b:P * b + P], r1[:, 96 * b:96 * b + 96], ident)
            mm.then_inc(pe_tok, 1)
            for n in range(G2):
                for b in range(NB):
                    mm = nc.tensor.transpose(ps[0:48, 1 + n, P * b:P * b + P], g2[:, n, 48 * b:48 * b + 48], ident)
            mm.then_inc(pe_tok, 1)
            pe.wait_ge(ev_tok, V_T2)
            for half in range(2):
                for kh in range(2):
                    mm = nc.tensor.matmul(ps[:, 3, EMB * half:EMB * half + EMB], t1[:, 256 * kh + P * half:256 * kh + P * half + P],
                                          w1T[:, kh, :], start=(kh == 0), stop=(kh == 1))
            for k in range(GROUP):
                mm = nc.tensor.matmul(ps[0:64, 4, 0:EMB], t2[:, 64 * k:64 * k + 64], w2T[:, k, :],
                                      start=(k == 0), stop=(k == GROUP - 1))
            mm.then_inc(pe_tok, 1)
            pe.wait_ge(ev_tok, V_L12)
            for b in range(NB):
                o = ps[:, 5 + b // 2, N_IMG * (b % 2):N_IMG * (b % 2) + N_IMG]
                nc.tensor.matmul(o[0:64, :], y1[:, EMB * (b // 2):EMB * (b // 2) + EMB],
                                 i1[:, N_IMG * (b % 2):N_IMG * (b % 2) + N_IMG], start=True, stop=True)
                mm = nc.tensor.matmul(o[64:128, :], y2, i2[:, N_IMG * b:N_IMG * b + N_IMG], start=True, stop=True)
            mm.then_inc(pe_tok, 1)

            def tokens_from_patches(jt):
                base_v = 3 * jt
                pe.wait_ge(rearr, 2 + jt)
                for b in range(NB):
                    mm = nc.tensor.transpose(ps[0:48, 0, P * b:P * b + P],
                                             r0[:, 48 * (NB * jt + b):48 * (NB * jt + b) + 48], ident)
                mm.then_inc(pe_tok, 1)
                pe.wait_ge(ev_tok, V_UP + 1 + base_v)
                nc.tensor.matmul(ps[0:EMB, 1, :], w0T, t0[:, 512 * jt:512 * jt + 512],
                                 start=True, stop=True).then_inc(pe_tok, 1)
                pe.wait_ge(ev_tok, V_UP + 2 + base_v)
                for b in range(NB):
                    o = ps[:, 2 + b // 2, 256 * (b % 2):256 * (b % 2) + C]
                    c0 = N_IMG * b + P * jt
                    nc.tensor.matmul(o, ycat_hi[:, c0:c0 + P], wf_hi, start=True, stop=False)
                    mm = nc.tensor.matmul(o, ycat_lo[:, P * b:P * b + P], wf_lo,
                                          start=False, stop=True)
                mm.then_inc(pe_tok, 1)

            def in_projection(n):
                pe.wait_ge(xn_ready, n + 1)
                j = JS[n]
                if n >= 1:
                    pe.wait_ge(xt_ready, 2 * n)
                for b in range(NB):
                    nc.tensor.transpose(ps[:, 7, P * b:P * b + P], xn[:, j, b, 0:P], ident)
                mm = None
                for b in range(NB):
                    mm = nc.tensor.transpose(ps[0:CB, 4, P * b:P * b + P], xn[:, j, b, P:C], ident)
                mm.then_inc(xt_ps, 1)
                pe.wait_ge(xt_ready, 2 * n + 2)
                nc.tensor.matmul(ps[:, 5, :], ip_a[:, 0:P], xt_a, start=True, stop=False)
                nc.tensor.matmul(ps[:, 5, :], ip_b[:, 0:P], xt_b, start=False, stop=True).then_inc(xz_ps, 1)
                nc.tensor.matmul(ps[:, 6, :], ip_a[:, C:C + P], xt_a, start=True, stop=False)
                nc.tensor.matmul(ps[:, 6, :], ip_b[:, C:C + P], xt_b, start=False, stop=True).then_inc(xz_ps, 1)
                for half in range(2):
                    for xz in range(2):
                        o = ps[64 * half:64 * half + 64, 4, 256 * xz:256 * xz + 256]
                        w = slice(C * xz + P, C * xz + C)
                        c = slice(256 * half, 256 * half + 256)
                        nc.tensor.matmul(o, ip_a[:, w], xt_a[:, c], start=True, stop=False)
                        mm = nc.tensor.matmul(o, ip_b[:, w], xt_b[:, c], start=False, stop=True)
                mm.then_inc(xz_ps, 1)

            pe.wait_ge(ld_mix, 16 * N_MIX)
            pe.wait_ge(ev_tok, V_UP)
            in_projection(0)
            tokens_from_patches(0)
            pe.wait_ge(xz_out, 4)
            in_projection(1)
            tokens_from_patches(1)
            pe.wait_ge(xz_out, 8)
            in_projection(2)
            pe.wait_ge(xz_out, 12)

            def from_u(o, wa, wb, b, start_ok=True):
                hb = 64 * (b // 2)
                nc.tensor.matmul(o, wa, u3[:, b, :], start=True, stop=False)
                return nc.tensor.matmul(o, wb[hb:hb + 64], u3[hb:hb + 64, 4 + b % 2, :], start=False, stop=True)

            pe.wait_ge(u_ready, 3)
            for w in range(2):
                if w == 1:
                    pe.wait_ge(bc_step, 2)
                for b in range(NB):
                    mm = from_u(ps[64 * (b // 2):64 * (b // 2) + 64, 6 + b % 2, 0:L], bc[:, 0, w, :], bc[:, 1, w, :], b)
                mm.then_inc(bc_ps, 1)
                if w == 0:
                    for u in US:
                        if u == 2:
                            for b in range(NB):
                                mm = from_u(ps[64 * (b // 2):64 * (b // 2) + 64, 4 + b % 2, 0:L],
                                            dw[:, 0, P:C], dw[:, 1, P:C], b)
                        else:
                            for b in (2 * u, 2 * u + 1):
                                mm = from_u(ps[:, b, 0:L], dw[:, 0, 0:P], dw[:, 1, 0:P], b)
                        mm.then_inc(dt_ps, 1)
            pe.wait_ge(dve_set, 3)
            pe.wait_ge(bc_step, 10)
            pe.wait_ge(sp_dve, 9)
            for n, u in enumerate(US):
                yb = 4 + 2 * (n % 2)
                if n == 2:
                    pe.wait_ge(y_step, 2)

                def spread(s, parts, bank, signal):
                    for i in range(2):
                        mm = nc.tensor.matmul(ps[:, bank + i, 0:L], pick[:, u, bass.ds(s, 1), :].rearrange("p o c -> p (o c)"),
                                              parts[:, i, :], start=True, stop=True)
                    mm.then_inc(signal, 1)

                def sum_states(s, start, stop):
                    pe.wait_ge(hc_rdy, S * n + s + 1)
                    for i in range(2):
                        mm = nc.tensor.matmul(ps[:, yb + i, 0:L], ident, hc[:, i, :], start=start, stop=stop)
                    mm.then_inc(summed, 1)

                if n:
                    pe.wait_ge(driven, S * n)
                spread(0, b_parts, 0, b_wide)
                if n:
                    pe.wait_ge(hc_rdy, S * n)
                spread(0, c_parts, 2, c_wide)
                pe.wait_ge(driven, S * n + 1)
                spread(1, b_parts, 0, b_wide)
                pe.wait_ge(hc_rdy, S * n + 1)
                spread(1, c_parts, 2, c_wide)
                sum_states(0, True, False)
                with pe.Fori(2, S) as s:
                    pe.wait_ge(driven, s + S * n)
                    spread(s, b_parts, 0, b_wide)
                    pe.wait_ge(hc_rdy, s + S * n)
                    spread(s, c_parts, 2, c_wide)
                    sum_states(s - 1, False, False)
                sum_states(S - 1, False, True)
            pe.wait_ge(y_step, 6)
            for j in range(NJ):
                if j:
                    pe.wait_ge(post, 13 * (j - 1) + 1)
                for b in range(NB):
                    o = ps[:, b // 2, 256 * (b % 2):256 * (b % 2) + C]
                    hb = 64 * (b // 2)
                    nc.tensor.matmul(o, y3[:, b, P * j:P * j + P], ow[:, 0, :], start=True, stop=False)
                    mm = nc.tensor.matmul(o, y3[hb:hb + 64, 4 + b % 2, P * j:P * j + P], ow[hb:hb + 64, 1, :],
                                          start=False, stop=True)
                mm.then_inc(attn_ps, 1)
                pe.wait_ge(xf_rdy, j + 1)
                for b in range(NB):
                    nc.tensor.transpose(ps[:, 2, P * b:P * b + P], xf[:, NB * j + b, 0:P], ident)
                for b in range(NB):
                    mm = nc.tensor.transpose(ps[0:CB, 3, P * b:P * b + P], xf[:, NB * j + b, P:C], ident)
                mm.then_inc(xft_ps, 1)
                pe.wait_ge(xft_rdy, 2 * j + 2)
                for b in range(NB):
                    o = ps[:, 4, E * (NB * j + b):E * (NB * j + b) + E]
                    nc.tensor.matmul(o, xft_a[:, P * b:P * b + P], wr[:, 0, :], start=True, stop=False)
                    mm = nc.tensor.matmul(o, xft_b[:, P * b:P * b + P], wr[0:CB, 1, :], start=False, stop=True)
                mm.then_inc(logit_ps, 1)
            pe.wait_ge(route, ROUTE_TOP + 3)
            cv = cnt[:, :, :].rearrange("p e t -> p (e t)")
            nc.tensor.matmul(ps[:, 5, 0:E * NT], cst[:, C_UP:C_UP + P], cv, start=True, stop=True)
            nc.tensor.matmul(ps[:, 6, 0:E * NT], ones_sq[:, :], cv, start=True, stop=True).then_inc(cnt_ps, 1)

            pe.wait_ge(route, ROUTE_SLOT + 3)
            pe.wait_ge(ld_exp, 16 * N_EXP)

            def x_transposed(i, p):
                pe.wait_ge(xin_l[p], 16 * (i // 2 + 1) if isinstance(i, int) else i * 8 + (16 if p == 0 else 8))
                if is_at_least(i, 2):
                    pe.wait_ge(xe_rdy, 2 * i - 2)
                nc.tensor.transpose(ps[:, p, 0:P], x_in[:, p, 0:P], ident)
                nc.tensor.transpose(ps[0:CB, p, P:2 * P], x_in[:, p, P:C], ident).then_inc(xe_ps, 1)

            def up(i, p):
                e = pe.value_load(texi[0:1, bass.ds(i, 1)], min_val=0, max_val=E - 1)
                pe.wait_ge(xe_rdy, 2 * i + 2)
                if is_at_least(i, 1):
                    pe.wait_ge(hid_rdy, i)
                for h in range(2):
                    nc.tensor.matmul(ps[:, 2 + h, 0:FH], xe_a[:, p, :], wi_a[:, bass.ds(e * F + h * FH, FH)],
                                     start=True, stop=False)
                    mm = nc.tensor.matmul(ps[:, 2 + h, 0:FH], xe_b[:, p, :], wi_b[:, bass.ds(e * F + h * FH, FH)],
                                          start=False, stop=True)
                mm.then_inc(up_ps, 1)

            def hidden_transposed(i):
                pe.wait_ge(hid_rdy, i + 1)
                if is_at_least(i, 1):
                    pe.wait_ge(hidt_rdy, i)
                for f in range(FC):
                    mm = nc.tensor.transpose(ps[:, 4 + f // 3, P * (f % 3):P * (f % 3) + P], hid[:, P * f:P * f + P], ident)
                mm.then_inc(hidt_ps, 1)

            def down(i, p):
                e = pe.value_load(texi[0:1, bass.ds(i, 1)], min_val=0, max_val=E - 1)
                pe.wait_ge(hidt_rdy, i + 1)
                if is_at_least(i, 2):
                    pe.wait_ge(y_rdy, i - 1)
                nc.tensor.matmul(ps[:, 6 + p, 0:C], ones_row[:, :], bo[:, bass.ds(e * C, C)], start=True, stop=False)
                for f in range(FC):
                    mm = nc.tensor.matmul(ps[:, 6 + p, 0:C], hid_t[:, P * f:P * f + P],
                                          wo[:, bass.ds(e * (FC * C) + f * C, C)], start=False, stop=(f == FC - 1))
                mm.then_inc(down_ps, 1)

            x_transposed(0, 0)
            x_transposed(1, 1)
            up(0, 0)

            def expert_tile(i, p):
                hidden_transposed(i)
                if is_below(i, MT - 2):
                    x_transposed(i + 2, p)
                if is_below(i, MT - 1):
                    up(i + 1, 1 - p)
                down(i, p)
            expert_loop(pe, expert_tile)

        @block.scalar
        def _(act):
            act.wait_ge(gath12, 16 * (G2 + G1))
            nc.scalar.activation(r1.rearrange("p (b d c) -> p d b c", b=NB, d=G1),
                                 g1.rearrange("p d (b c) -> p d b c", b=NB), ACT.Copy).then_inc(rearr, 1)
            act.wait_ge(pe_tok, T_T1)
            nc.scalar.activation(t1.rearrange("p (k b t) -> p b k t", k=2, b=NB),
                                 ps[0:96, 0, :].rearrange("p (b k t) -> p b k t", b=NB, k=2), ACT.Copy).then_inc(ev_tok, 1)
            act.wait_ge(pe_tok, T_T2)
            for n in range(G2):
                nc.scalar.activation(t2[:, 512 * n:512 * n + 512].rearrange("p (k b t) -> p b k t", k=8, b=NB),
                                     ps[0:48, 1 + n, :].rearrange("p (b k t) -> p b k t", b=NB, k=8), ACT.Copy).then_inc(ev_tok, 1)
            act.wait_ge(pe_tok, T_L12)
            nc.scalar.activation(y1, ps[:, 3, 0:2 * EMB], ACT.Copy)
            nc.scalar.activation(y2, ps[0:64, 4, 0:EMB], ACT.Copy).then_inc(ev_tok, 1)
            act.wait_ge(pe_tok, T_UP)
            act.wait_ge(ld_tok, 16 * N_TOK)
            for h in range(2):
                nc.scalar.activation(ycat_hi[:, 512 * h:512 * h + 512], ps[:, 5 + h, :], ACT.Identity,
                                     bias=b12[:, 0:1]).then_inc(ev_tok, 1)

            def tokens_from_patches(jt):
                act.wait_ge(gath0[jt], 16 * GROUP)
                nc.scalar.activation(
                    r0[:, 192 * jt:192 * jt + 192].rearrange("p (b k c) -> p k b c", b=NB, k=GROUP),
                    g0[:, GROUP * jt:GROUP * jt + GROUP, :].rearrange("p k (b c) -> p k b c", b=NB),
                    ACT.Copy).then_inc(rearr, 1)
                act.wait_ge(pe_tok, T_UP + 1 + 3 * jt)
                nc.scalar.activation(t0[:, 512 * jt:512 * jt + 512], ps[0:48, 0, :], ACT.Copy).then_inc(ev_tok, 1)
                act.wait_ge(pe_tok, T_UP + 2 + 3 * jt)
                nc.scalar.activation(ycat_lo[0:EMB, :], ps[0:EMB, 1, :], ACT.Identity,
                                     bias=b0[:, 0:1]).then_inc(ev_tok, 1)
                act.wait_ge(pe_tok, T_UP + 3 + 3 * jt)
                for h in range(2):
                    ins = nc.scalar.activation(h_tok[:, jt, 2 * h:2 * h + 2, :],
                                               ps[:, 2 + h, :].rearrange("p (b c) -> p b c", b=2)[:, :, 0:C], ACT.Copy)
                ins.then_inc(ev_tok, 1)

            def deviation(n):
                act.wait_ge(ln_step, 9 * n + 8)
                nc.scalar.activation(std[:, :], mv[:, :, 1], ACT.Sqrt, bias=cst[:, C_EPS:C_EPS + 1]).then_inc(std_rdy, 1)

            def in_projection(n):
                j = JS[n]
                deviation(n)
                act.wait_ge(xt_ps, n + 1)
                nc.scalar.activation(xt_a, ps[:, 7, :], ACT.Copy).then_inc(xt_ready, 1)
                nc.scalar.activation(xt_b, ps[0:CB, 4, :], ACT.Copy).then_inc(xt_ready, 1)
                t = slice(K - 1 + P * j, K - 1 + P * j + P)
                act.wait_ge(xz_ps, 3 * n + 1)
                nc.scalar.activation(x3[:, 0:NB, t], ps[:, 5, :].rearrange("p (b t) -> p b t", b=NB),
                                     ACT.Copy).then_inc(xz_out, 1)
                act.wait_ge(xz_ps, 3 * n + 2)
                nc.scalar.activation(z3[:, 0:NB, P * j:P * j + P], ps[:, 6, :].rearrange("p (b t) -> p b t", b=NB),
                                     ACT.Copy).then_inc(xz_out, 1)
                act.wait_ge(xz_ps, 3 * n + 3)
                nc.scalar.activation(x3[:, NB:6, t], ps[:, 4, 0:256].rearrange("p (b t) -> p b t", b=2),
                                     ACT.Copy).then_inc(xz_out, 1)
                nc.scalar.activation(z3[:, NB:6, P * j:P * j + P], ps[:, 4, 256:512].rearrange("p (b t) -> p b t", b=2),
                                     ACT.Copy).then_inc(xz_out, 1)

            in_projection(0)
            tokens_from_patches(0)
            in_projection(1)
            tokens_from_patches(1)
            in_projection(2)
            act.wait_ge(xz_out, 12)
            nc.scalar.activation(z_cm[:, :], z_cm[:, :], ACT.Silu).then_inc(z_ready, 1)
            for n, u in enumerate(US):
                act.wait_ge(conv_step, K * (n + 1))
                g = chan_group(u)
                nc.scalar.activation(unit(u3, u), unit(y3, u), ACT.Silu, bias=chan[:, g, H_CB:H_CB + 1]).then_inc(u_ready, 1)
            act.wait_ge(bc_ps, 1)
            nc.scalar.activation(a_neg[:, :, :], chan[:, :, H_A:H_A + S], ACT.Exp).then_inc(a_exp, 1)
            for n, u in enumerate(US):
                g = chan_group(u)
                act.wait_ge(dt_ps, n + 1)
                nc.scalar.activation(unit(dt3, u), bank2(2 * u), ACT.Abs, bias=chan[:, g, H_DTB:H_DTB + 1]).then_inc(sp_act, 1)
            for n, u in enumerate(US):
                act.wait_ge(sp_act, 3 + n)
                nc.scalar.activation(unit(dt3, u), unit(dt3, u), ACT.Exp, scale=-1.0).then_inc(sp_act, 1)
            act.wait_ge(a_exp, 2)
            for n, u in enumerate(US):
                act.wait_ge(sp_dve, 3 * n + 3)
                g = chan_group(u)
                with act.Fori(0, S // 2) as m:
                    for p in range(2):
                        act.wait_ge(scanned, m * 2 + (S * n + p + 1))
                        nc.scalar.activation(decay[:, p, :, 1:L], unit(dt3, u, 1, L - 1), ACT.Exp,
                                             scale=a_neg[:, g, bass.ds(m * 2 + p, 1)]).then_inc(decay_rdy, 1)
            for j in range(NJ):
                deviation(NJ + 2 * j)
                deviation(NJ + 2 * j + 1)
                act.wait_ge(xft_ps, j + 1)
                if j:
                    act.wait_ge(logit_ps, j)
                nc.scalar.activation(xft_a, ps[:, 2, :], ACT.Copy).then_inc(xft_rdy, 1)
                nc.scalar.activation(xft_b, ps[0:CB, 3, :], ACT.Copy).then_inc(xft_rdy, 1)
            act.wait_ge(route, ROUTE_TOP + 4)
            nc.scalar.activation(gtmp[:, 0, :], gtmp[:, 0, :], ACT.Exp).then_inc(gate_e, 1)

            def expert_tile(i, p):
                act.wait_ge(up_ps, i + 1)
                if is_at_least(i, 1):
                    act.wait_ge(hidt_ps, i)
                nc.scalar.activation(hid.rearrange("p (h f) -> p h f", h=2), ps[:, 2:4, 0:FH],
                                     ACT.Gelu).then_inc(hid_rdy, 1)
                act.wait_ge(down_ps, i + 1)
                if is_at_least(i, 2):
                    act.wait_ge(stored[p], 16 * (i // 2) if isinstance(i, int) else i * 8 - 8 * p)
                nc.scalar.activation(y_out[:, p, :], ps[:, 6 + p, 0:C], ACT.Copy).then_inc(y_rdy, 1)
                act.wait_ge(y_rdy, i + 1)
                act.dma_start(ys_dram[bass.ds(i * P, P), :], y_out[:, p, :]).then_inc(stored[p], 16)
            expert_loop(act, expert_tile)

        @block.vector
        def _(dve):
            v = nc.vector
            dve.wait_ge(ld_cst, 16)
            rows = cst[:, C_ROW:C_ROW + 2 * S].rearrange("p (u s) -> p u s", u=2)
            v.tensor_copy(pick[:, 0:2, :, :].rearrange("p u s c -> p (u s) c"),
                          cst[:, C_ROW:C_ROW + 2 * S].rearrange("p (n o) -> p n o", o=1).to_broadcast([P, 2 * S, P]))\
                .then_inc(dve_set, 1)
            for half in range(2):
                v.tensor_copy(pick[:, 2, :, 64 * half:64 * half + 64],
                              rows[:, half, :].rearrange("p (s o) -> p s o", o=1).to_broadcast([P, S, 64]))\
                    .then_inc(dve_set, 1)
            v.memset(ones_row[:, :], 1.0).then_inc(dve_set, 1)
            v.memset(ones_sq[:, :], 1.0).then_inc(dve_set, 1)
            v.memset(ycat_lo[EMB:EMB + 1, :], 1.0).then_inc(dve_set, 1)
            v.memset(x3[:, :, 0:K - 1], 0.0).then_inc(dve_set, 1)

            def norm_stats(src, signal, at):
                for b in range(NB):
                    v.bn_stats(stats[:, b, :], src[:, b, :]).then_inc(signal, 1)
                dve.wait_ge(signal, at + 4)
                for b in range(NB):
                    v.bn_aggr(mv[:, b, :], stats[:, b, :]).then_inc(signal, 1)
                dve.wait_ge(signal, at + 8)
                dve.wait_ge(std_rdy, at // 9 + 1)
                v.reciprocal(rstd[:, :], std[:, :]).then_inc(signal, 1)
                dve.wait_ge(signal, at + 9)

            def normalise(dst, src, b):
                return v.tensor_scalar(dst, src, mv[:, b, 0:1], rstd[:, b:b + 1], ALU.subtract, ALU.mult)

            for n, j in enumerate(JS):
                if n == 0:
                    dve.wait_ge(h_ready, 16)
                else:
                    dve.wait_ge(ev_tok, V_UP + 3 * n)
                norm_stats(h_tok[:, j, :, :], ln_step, 9 * n)
                for b in range(NB):
                    ins = normalise(xn[:, j, b, :], h_tok[:, j, b, :], b)
                ins.then_inc(xn_ready, 1)
                dve.wait_ge(xn_ready, n + 1)

            dve.wait_ge(xz_out, 12)
            dve.wait_ge(dve_set, 7)
            for n, u in enumerate(US):
                g = chan_group(u)
                v.tensor_scalar(unit(y3, u), unit(x3, u, K - 1), chan[:, g, H_W + K - 1:H_W + K], None,
                                ALU.mult).then_inc(conv_step, 1)
                for k in range(K - 1):
                    dve.wait_ge(conv_step, K * n + k + 1)
                    v.scalar_tensor_tensor(unit(y3, u), unit(x3, u, k), chan[:, g, H_W + k:H_W + k + 1],
                                           unit(y3, u), ALU.mult, ALU.add).then_inc(conv_step, 1)
            hi = drive[:, :, :]
            for w, parts in enumerate((b_parts, c_parts)):
                n = 5 * w
                dve.wait_ge(bc_ps, w + 1)
                if w:
                    dve.wait_ge(bc_step, 5)
                v.tensor_copy(parts[:, :, :], bank2(6)).then_inc(bc_step, 1)
                dve.wait_ge(bc_step, n + 1)
                v.scalar_tensor_tensor(hi, parts[:, :, :], cst[:, C_NEG:C_NEG + 1], bank2(6), ALU.mult, ALU.add)\
                    .then_inc(bc_step, 1)
                dve.wait_ge(bc_step, n + 2)
                v.tensor_copy(parts[:, :, :], hi).then_inc(bc_step, 1)
                dve.wait_ge(bc_step, n + 3)
                v.scalar_tensor_tensor(hi, parts[:, :, :], cst[:, C_NEG + 1:C_NEG + 2], hi, ALU.mult, ALU.add)\
                    .then_inc(bc_step, 1)
                dve.wait_ge(bc_step, n + 4)
                v.tensor_copy(parts[:, :, :], hi).then_inc(bc_step, 1)
                if w == 0:
                    dve.wait_ge(a_exp, 1)
                    v.tensor_scalar(a_neg[:, :, :], a_neg[:, :, :], -1.0, None, ALU.mult).then_inc(a_exp, 1)
                    for m, u in enumerate(US):
                        g = chan_group(u)
                        dve.wait_ge(sp_act, m + 1)
                        v.tensor_scalar(unit(dtu3, u), bank2(2 * u), chan[:, g, H_DTB:H_DTB + 1], 0.0,
                                        ALU.add, ALU.max).then_inc(sp_abs, 1)
            for n, u in enumerate(US):
                dve.wait_ge(sp_act, 4 + n)
                e, poly = unit(dt3, u), state[:, :, :]
                v.tensor_scalar(poly, e, LOG1P[-1], None, ALU.mult).then_inc(log_step, 1)
                for k, coefficient in enumerate(LOG1P[-2::-1]):
                    dve.wait_ge(log_step, len(LOG1P) * n + k + 1)
                    v.scalar_tensor_tensor(poly, poly, coefficient, e, ALU.add, ALU.mult).then_inc(log_step, 1)
                dve.wait_ge(log_step, len(LOG1P) * (n + 1))
                dve.wait_ge(sp_abs, n + 1)
                v.tensor_tensor(unit(dt3, u), poly, unit(dtu3, u), ALU.add).then_inc(sp_dve, 1)
                dve.wait_ge(sp_dve, 3 * n + 1)
                v.tensor_tensor(unit(dtu3, u), unit(dt3, u), unit(u3, u), ALU.mult).then_inc(sp_dve, 1)
                dve.wait_ge(sp_dve, 3 * n + 2)
                g = chan_group(u)
                v.tensor_scalar(unit(y3, u), unit(u3, u), chan[:, g, H_D:H_D + 1], None, ALU.mult).then_inc(sp_dve, 1)
            for p in range(2):
                v.memset(decay[:, p, :, 0:1], 0.0).then_inc(scanned, 1)
            dve.wait_ge(bc_step, 10)
            dve.wait_ge(sp_dve, 9)
            for n, u in enumerate(US):
                yb = 4 + 2 * (n % 2)
                def state_pass(m, p):
                    at = m * 2 + (S * n + p)
                    dve.wait_ge(b_wide, at + 1)
                    v.tensor_tensor(drive[:, :, :], unit(dtu3, u), bank2(0), ALU.mult).then_inc(driven, 1)
                    dve.wait_ge(driven, at + 1)
                    dve.wait_ge(decay_rdy, at + 1)
                    v.tensor_tensor_scan(state[:, :, :].rearrange("p a c -> p (a c)"),
                                         decay[:, p, :, :].rearrange("p a c -> p (a c)"),
                                         drive[:, :, :].rearrange("p a c -> p (a c)"), 0.0,
                                         ALU.mult, ALU.add).then_inc(scanned, 1)
                    dve.wait_ge(scanned, at + 3)
                    dve.wait_ge(c_wide, at + 1)
                    if is_at_least(at, 1):
                        dve.wait_ge(summed, at)
                    v.tensor_tensor(hc[:, :, :], state[:, :, :], bank2(2), ALU.mult).then_inc(hc_rdy, 1)

                state_pass(0, 0)
                state_pass(0, 1)
                with dve.Fori(1, S // 2) as m:
                    state_pass(m, 0)
                    state_pass(m, 1)
                dve.wait_ge(summed, S * (n + 1))
                v.tensor_tensor(unit(y3, u), bank2(yb), unit(y3, u), ALU.add).then_inc(y_step, 1)
                dve.wait_ge(y_step, 2 * n + 1)
                dve.wait_ge(z_ready, 1)
                v.tensor_tensor(unit(y3, u), unit(y3, u), unit(z3, u), ALU.mult).then_inc(y_step, 1)
            v.memset(zero, 0.0).then_inc(zeroed, 1)
            v.memset(xe_b[CB:CB + 1, :, :], 1.0).then_inc(dve_set, 1)
            g4 = ln_gb[:, 0:1, :].to_broadcast([P, NB, C])
            b4 = ln_gb[:, 1:2, :].to_broadcast([P, NB, C])
            at = 0

            def step(ins):
                nonlocal at
                at += 1
                ins.then_inc(post, 1)
                dve.wait_ge(post, at)

            ln_at = 9 * NJ
            for j in range(NJ):
                dve.wait_ge(attn_ps, j + 1)
                for h in range(2):
                    ins = v.tensor_tensor(rr[:, 2 * h:2 * h + 2, :],
                                          ps[:, h, :].rearrange("p (b c) -> p b c", b=2)[:, :, 0:C],
                                          xn[:, j, 2 * h:2 * h + 2, :], ALU.add)
                step(ins)
                norm_stats(rr, ln_step, ln_at)
                ln_at += 9
                for b in range(NB):
                    step(normalise(rr[:, b, :], rr[:, b, :], b))
                step(v.tensor_tensor(rr, rr, g4, ALU.mult))
                step(v.tensor_tensor(rr, rr, b4, ALU.add))
                step(v.tensor_tensor(h_tok[:, j, :, :], h_tok[:, j, :, :], rr, ALU.add))
                norm_stats(h_tok[:, j, :, :], ln_step, ln_at)
                ln_at += 9
                for b in range(NB):
                    ins = normalise(xf[:, NB * j + b, :], h_tok[:, j, b, :], b)
                    step(ins)
                step(v.memset(rstd[:, :], 0.0))
                v.memset(stats[:, 0, :], 0.0).then_inc(xf_rdy, 1)
                dve.wait_ge(xf_rdy, j + 1)
            dve.wait_ge(logit_ps, NJ)
            at_r = 0

            def rt(ins):
                nonlocal at_r
                at_r += 1
                ins.then_inc(route, 1)
                dve.wait_ge(route, at_r)

            v.tensor_copy(logit[:, :, :], ps[:, 4, 0:E * NT].rearrange("p (t e) -> p t e", t=NT)).then_inc(mixed_free, 1)
            dve.wait_ge(mixed_free, 1)
            for t in range(NT):
                v.max(top_v[:, t, :], logit[:, t, :]).then_inc(mixed_free, 1)
            dve.wait_ge(mixed_free, 1 + NT)
            for t in range(NT):
                ins = v.max_index(top_i[:, t, :], top_v[:, t, :], logit[:, t, :])
                ins.then_inc(route, 1)
            at_r = NT
            dve.wait_ge(route, NT)
            rt(v.tensor_copy(idf[:, :, :], top_i[:, :, 0:TOPK]))
            e8 = cst[:, C_E8:C_E8 + E].rearrange("p (o e) -> p o e", o=1).to_broadcast([P, NT, E])
            for k in range(TOPK):
                ins = v.tensor_tensor(hot[:, k, :, :], idf[:, :, k:k + 1].to_broadcast([P, NT, E]), e8, ALU.is_equal)
            rt(ins)
            rt(v.tensor_tensor(cnt[:, :, :].rearrange("p e t -> p t e"), hot[:, 0, :, :], hot[:, 1, :, :], ALU.add))
            rt(v.tensor_tensor(gtmp[:, 0, :], top_v[:, :, 1], top_v[:, :, 0], ALU.subtract))
            dve.wait_ge(gate_e, 1)
            rt(v.tensor_scalar(gtmp[:, 1, :], gtmp[:, 0, :], 1.0, None, ALU.add))
            rt(v.reciprocal(gate[:, 0, :], gtmp[:, 1, :]))
            rt(v.tensor_tensor(gate[:, 1, :], gtmp[:, 0, :], gate[:, 0, :], ALU.mult))
            dve.wait_ge(cnt_ps, 1)
            tot = ps[:, 6, 0:E * NT]
            runf = run[:, :, :].rearrange("p e t -> p (e t)")
            rt(v.tensor_tensor_scan(runf, cst[:, C_MASK:C_MASK + E * NT], tot, 0.0, ALU.mult, ALU.add))
            m12 = cst[:, C_M12:C_M12 + NT].rearrange("p (o m) -> p o m", o=1).to_broadcast([P, E, NT])
            rt(v.tensor_tensor(cmp12[:, :, :], run[:, :, NT - 1:NT].to_broadcast([P, E, NT]), m12, ALU.is_gt))
            rt(v.tensor_reduce(tiles[:, :], cmp12[:, :, :], AX_X, ALU.add))
            rt(v.tensor_tensor_scan(ends[:, :], ones_sq[:, 0:E], tiles[:, :], 0.0, ALU.mult, ALU.add))
            rt(v.tensor_tensor(first[:, :], ends[:, :], tiles[:, :], ALU.subtract))
            rt(v.tensor_tensor(runf, runf, tot, ALU.subtract))
            rt(v.tensor_tensor(runf, runf, ps[:, 5, 0:E * NT], ALU.add))
            rt(v.scalar_tensor_tensor(pos[:, :, :].rearrange("p t e -> p e t"),
                                      first[:, :].rearrange("p (e o) -> p e o", o=1).to_broadcast([P, E, NT]),
                                      float(P), run[:, :, :], ALU.mult, ALU.add))
            for k in range(TOPK):
                ins = v.tensor_tensor(pos_k[:, k, :, :], hot[:, k, :, :], pos[:, :, :], ALU.mult)
            rt(ins)
            rt(v.tensor_reduce(slot_f[:, :, :], pos_k[:, :, :, :], AX_X, ALU.add))
            t31 = cst[0:1, C_T31:C_T31 + MT].rearrange("p (m o) -> p m o", o=1).to_broadcast([1, MT, E])
            rt(v.tensor_tensor(tcmp[:, :, :], ends[0:1, :].rearrange("p (o e) -> p o e", o=1).to_broadcast([1, MT, E]),
                               t31, ALU.is_le))
            rt(v.tensor_reduce(tex[:, :], tcmp[:, :, :], AX_X, ALU.add))
            rt(v.tensor_copy(slot[:, :, :], slot_f[:, :, :]))
            assert at_r == ROUTE_SLOT, at_r
            rt(v.tensor_scalar(tex[:, :], tex[:, :], float(E - 1), None, ALU.min))
            rt(v.tensor_copy(texi[:, :], tex[:, :]))
            rt(v.memset(tcmp[:, 0, :], 0.0))

            def expert_tile(i, p):
                dve.wait_ge(xe_ps, i + 1)
                if is_at_least(i, 2):
                    dve.wait_ge(up_ps, i - 1)
                v.tensor_copy(xe_a[:, p, :], ps[:, p, 0:P]).then_inc(xe_rdy, 1)
                v.tensor_copy(xe_b[0:CB, p, :], ps[0:CB, p, P:2 * P]).then_inc(xe_rdy, 1)

            def hidden_tile(i):
                dve.wait_ge(hidt_ps, i + 1)
                if is_at_least(i, 1):
                    dve.wait_ge(down_ps, i)
                v.tensor_copy(hid_t.rearrange("p (h f) -> p h f", h=2), ps[:, 4:6, 0:FH]).then_inc(hidt_rdy, 1)

            expert_tile(0, 0)
            expert_tile(1, 1)

            def both(i, p):
                hidden_tile(i)
                if is_below(i, MT - 2):
                    expert_tile(i + 2, p)
            expert_loop(dve, both)
            for t in range(NT):
                j, b = t // NB, t % NB
                dve.wait_ge(fetched[t], 16 * TOPK)
                for k in range(TOPK):
                    if k:
                        dve.wait_ge(mixed, TOPK * t + k)
                    v.scalar_tensor_tensor(h_tok[:, j, b, :], got_y[k][:, t, :], gate[:, k, t:t + 1],
                                           h_tok[:, j, b, :], ALU.mult, ALU.add).then_inc(mixed, 1)


def kernel(**x):
    import numpy as _np
    import concourse.bacc as _bacc
    from concourse import mybir as _mybir
    from concourse.bass_utils import run_bass_kernel_spmd as _run

    a = {n: _np.asarray(v) for n, v in x.items()}
    cat = _np.concatenate

    def patches(p):
        h = 64 // p
        t = a["x"].reshape(4, 3, h, p, h, p).transpose(2, 4, 0, 3, 5, 1)
        return t.reshape(h * h, 4 * p * p * 3)

    def chunks(w):
        return _np.stack([w[0:128], cat([w[128:192], w[128:192]])], axis=1)

    def parts(w):
        return cat([w.T, w.T, w.T, _np.zeros_like(w.T)], axis=1)

    A, M, T = "L0_attn_", "L0_ffn_", "L0_tok_"
    wfT = a[T + "Wf"].T
    wiT = a[M + "Wi"].transpose(2, 0, 1)
    d = {
        "pix0": patches(1), "pix1": patches(2), "pix2": patches(4),
        "gidx": cat([a[T + "idx0"].reshape(2, 128, 16).transpose(1, 0, 2).reshape(128, 32),
                     a[T + "idx1"].reshape(64, 2, 8).transpose(1, 0, 2).reshape(128, 8),
                     a[T + "idx2"].reshape(16, 2, 8).transpose(2, 0, 1).reshape(128, 2)], axis=1),
        "txt": a["txt"], "cst": constants(),
        "w0T": a[T + "W0"].T, "w1T": a[T + "W1"].T.reshape(2, 96, 64).transpose(1, 0, 2),
        "w2T": a[T + "W2"].T.reshape(16, 48, 64).transpose(1, 0, 2),
        "b12": cat([a[T + "b1"], a[T + "b2"]])[:, None], "b0": a[T + "b0"][:, None],
        "wf_hi": wfT[64:192], "wf_lo": cat([wfT[0:64], a[T + "bf"][None]]),
        "i1": interpolation(64, 2).reshape(128, 512), "i2": interpolation(16, 4).reshape(64, 1024),
        "chan": chunks(cat([a[A + "conv_w"].reshape(192, 4), a[A + "conv_b"][:, None], a[A + "dt_b"][:, None],
                            a[A + "D_param"][:, None], a[A + "A_log"]], axis=1)),
        "ip_a": a[A + "in_proj_w"].T[0:128], "ip_b": a[A + "in_proj_w"].T[128:192],
        "dw": chunks(a[A + "dt_w"].T),
        "bc": chunks(_np.stack([parts(a[A + "B_w"]), parts(a[A + "C_w"])], axis=1)),
        "ow": chunks(a[A + "out_w"].T), "wr": chunks(a[M + "Wr"].T),
        "ln_gb": _np.stack([a[A + "ln_g"], a[A + "ln_b"]])[None],
        "wi_a": wiT[0:128].reshape(128, -1),
        "wi_b": cat([wiT[128:192].reshape(64, -1), a[M + "bi"].reshape(1, -1)]),
        "wo": a[M + "Wo"].transpose(0, 2, 1).reshape(8, 6, 128, 192).transpose(2, 0, 1, 3).reshape(128, -1),
        "bo": a[M + "bo"].reshape(1, -1),
    }
    nc = _bacc.Bacc("TRN2", target_bir_lowering=False, num_devices=1)
    arrays, args = {}, {}
    for name, v in d.items():
        v = _np.ascontiguousarray(v)
        arrays["in_" + name] = v
        args[name] = nc.dram_tensor("in_" + name, v.shape, _mybir.dt.from_np(v.dtype), kind="ExternalInput").ap()
    out = nc.dram_tensor("out_0", (4, 384, 192), F32, kind="ExternalOutput").ap()
    build(nc, args, out)
    r = _run(nc, [arrays], core_ids=[0])
    return r.results[0]["out_0"]
```

```python
from contextlib import ExitStack

import concourse.bass as bass
import numpy as np
from concourse import mybir

F32 = mybir.dt.float32
BF16 = mybir.dt.bfloat16
I32 = mybir.dt.int32
U32 = mybir.dt.uint32
ALU = mybir.AluOpType
ACT = mybir.ActivationFunctionType
AX_X = mybir.AxisListType.X

P = 128
NB = 4
C = 192
CB = C - P
NJ = 3
L = NJ * P
NT = NJ * NB
EMB = 64
GROUP = 16
PATCH = [3, 12, 48]
N_IMG = 256
G0, G1, G2 = 32, 8, 2
S = 16
K = 4
U = 2 * L
E = 8
F = 768
FC = F // P
FH = F // 2
W_UA, W_UB, W_BI = 0, F, F + FH
W_DN = W_BI + FC
W_E = W_DN + FC * C + 2
CW = C + CB
TOPK = 2
NTOK = NB * L
NX = 4
MT = (TOPK * NTOK + E * (P - 1)) // P
EPS = 1e-5
LOG1P = [0.9999999659255084, -0.4999944497632982, 0.33318121707353093, -0.2483539898720075, 0.19076880730853912,
         -0.13602247612385465, 0.0775160866235987, -0.029074064606579537, 0.0051261021233726485]

C_ID = 0
C_UP = C_ID + P
C_ROW = C_UP + P
C_NEG = C_ROW + 2 * S
C_E8 = C_NEG + 2
C_M12 = C_E8 + E
C_MASK = C_M12 + NT
C_IOTA = C_MASK + E * NT
C_TOK = C_IOTA + P
C_EPS = C_TOK + NT
N_CST = C_EPS + 1

H_W, H_CB, H_DTB, H_D, H_A = 0, 4, 5, 6, 7
N_CH = H_A + S


def constants():
    c = np.zeros((P, N_CST), np.float32)
    c[:, C_ID:C_ID + P] = np.eye(P)
    c[:, C_UP:C_UP + P] = np.triu(np.ones((P, P)), 1)
    for pair in range(2):
        for part in range(3):
            for s in range(S):
                c[64 * pair + S * part + s, C_ROW + S * pair + s] = 1
        c[64 * pair + S:64 * pair + 3 * S, C_NEG] = -1
        c[64 * pair + 2 * S:64 * pair + 3 * S, C_NEG + 1] = -1
    c[:, C_E8:C_E8 + E] = np.arange(E)
    c[:, C_M12:C_M12 + NT] = P * np.arange(NT)
    c[:, C_MASK:C_MASK + E * NT] = (np.arange(E * NT) % NT != 0)
    c[:, C_IOTA:C_IOTA + P] = np.arange(P)
    j, b = np.divmod(np.arange(NT), NB)
    c[:, C_TOK:C_TOK + NT] = np.arange(P)[:, None] + L * b + P * j + 1
    c[:, C_EPS] = EPS
    return c


def interpolation(n_in, copies):
    pos = np.clip((np.arange(N_IMG) + 0.5) * (n_in / N_IMG) - 0.5, 0, n_in - 1)
    lo = np.floor(pos).astype(int)
    hi = np.minimum(lo + 1, n_in - 1)
    m = np.zeros((n_in, N_IMG), np.float32)
    m[lo, np.arange(N_IMG)] += 1 - (pos - lo)
    m[hi, np.arange(N_IMG)] += pos - lo
    out = np.zeros((copies, n_in, copies, N_IMG), np.float32)
    for k in range(copies):
        out[k, :, k] = m
    return out.reshape(copies * n_in, copies, N_IMG)


def build(nc, d, out):
    with ExitStack() as ctx:
        def sb(name, shape, dt=F32):
            return ctx.enter_context(nc.sbuf_tensor(name, shape, dt))

        def sem(name):
            return ctx.enter_context(nc.semaphore(name))

        cst = sb("cst", [P, N_CST])
        gidx = sb("gidx", [P, G0 + G1 + G2], I32)
        chan = sb("chan", [P, 2, N_CH])
        ln_gb = sb("ln_gb", [P, 2, C])
        b12 = sb("b12", [P, 1])
        b0 = sb("b0", [EMB, 1])
        ip_a = sb("ip_a", [P, 2 * C])
        ip_b = sb("ip_b", [CB, 2 * C])
        dw = sb("dw", [P, 2, C])
        bc = sb("bc", [P, 2, 2, 64])
        ow = sb("ow", [P, 2, C])
        wr = sb("wr", [P, 2, E])
        bo = sb("bo", [P, C])
        w_all = sb("w_all", [P, E * W_E])

        h_tok = sb("h_tok", [P, NJ, NB, C])
        xn = sb("xn", [P, NJ, NB, C])
        x_cm = sb("x_cm", [P, 6 * (L + K - 1)])
        u_cm = sb("u_cm", [P, 6 * L])
        z_cm = sb("z_cm", [P, 6 * L])
        dt_cm = sb("dt_cm", [P, 6 * L])
        dtu_cm = sb("dtu_cm", [P, 6 * L])
        y_cm = sb("y_cm", [P, W_E])
        decay = sb("decay", [P, 2, 2, L])
        drive = sb("drive", [P, 2, L])
        state = sb("state", [P, 2, L])
        hc = sb("hc", [P, 2, L])
        pick = sb("pick", [P, 3, S, P], BF16)
        b_parts = sb("b_parts", [P, 2, L], BF16)
        c_parts = sb("c_parts", [P, 2, L], BF16)
        a_neg = sb("a_neg", [P, 2, S])
        ones_sq = sb("ones_sq", [P, P])
        stats = sb("stats", [P, NB, 6])
        mv = sb("mv", [P, NB, 2])
        std = sb("std", [P, NB])
        rstd = sb("rstd", [P, NB])
        gate = sb("gate", [P, TOPK, NT])
        gtmp = sb("gtmp", [P, 2, NT])
        tiles = sb("tiles", [P, E])
        ends = sb("ends", [P, E])
        first = sb("first", [P, E])
        tok_in = sb("tok_in", [P, MT], I32)
        tok_out = sb("tok_out", [P, MT], I32)
        gate_s = sb("gate_s", [P, MT])
        texi = sb("texi", [1, MT], I32)

        g0 = y_cm[:, 0:G0 * 12].rearrange("p (d r) -> p d r", d=G0)
        g1 = y_cm[:, 384:768].rearrange("p (d r) -> p d r", d=G1)
        g2 = y_cm[:, 768:1152].rearrange("p (d r) -> p d r", d=G2)
        r0 = y_cm[:, 1152:1536]
        r1 = y_cm[:, 1536:1920]
        t0 = dt_cm[0:48, 0:1024]
        t1 = dt_cm[0:96, 1024:1536]
        t2 = dtu_cm[0:48, 0:1024]
        y1 = dtu_cm[:, 1024:1152]
        y2 = dtu_cm[0:64, 1152:1216]
        i1 = u_cm[:, 0:512]
        i2 = u_cm[0:64, 512:1536]
        ycat_hi = decay[:, :, :, :].rearrange("p a b c -> p (a b c)")[:, 0:1024]
        ycat_lo = dt_cm[0:EMB + 1, 1536:2048]
        w2T = dtu_cm[0:PATCH[2], 1216:2240].rearrange("p (k e) -> p k e", k=GROUP)
        hcf = hc[:, :, :].rearrange("p a c -> p (a c)")
        w0T = hcf[0:PATCH[0] * GROUP, 0:EMB]
        w1T = hcf[0:96, EMB:3 * EMB].rearrange("p (k e) -> p k e", k=2)
        wf_hi = hcf[:, 192:384]
        wf_lo = hcf[0:EMB + 1, 384:576]
        xt_a = drive[:, :, :].rearrange("p a c -> p (a c)")[:, 0:512]
        xt_b = state[:, :, :].rearrange("p a c -> p (a c)")[0:CB, 0:512]
        free = [t[:, :, :, :].rearrange("p a b c -> p (a b c)") if t is decay else t[:, :, :].rearrange("p a c -> p (a c)")
                for t in (decay, state, drive)]
        used = 0

        def table(parts, *dims):
            nonlocal used
            size = int(np.prod(dims))
            if used + size > free[0].shape[1]:
                free.pop(0)
                used = 0
            t = free[0][0:parts, used:used + size]
            used += size
            if len(dims) == 1:
                return t
            names = "abc"[:len(dims)]
            return t.rearrange(f"p ({' '.join(names)}) -> p {' '.join(names)}", **dict(zip(names, dims)))

        logit = table(P, NT, E)
        top_v = table(P, NT, 8)
        top_i = table(P, NT, 8).bitcast(U32)
        idf = table(P, NT, TOPK)
        hot = table(P, TOPK, NT, E)
        cnt = table(P, E, NT)
        run = table(P, E, NT)
        cmp12 = table(P, E, NT)
        pos = table(P, NT, E)
        pos_k = table(P, TOPK, NT, E)
        slot_f = table(P, TOPK * NT)
        slot_i = table(P, 3, TOPK * NT).bitcast(I32)
        digit = table(P, 2, TOPK * NT)
        tex_s = table(P, 2, MT)
        tcmp = table(1, MT, E)
        tex = table(1, MT)
        xf = dt_cm[:, :].rearrange("p (t c) -> p t c", t=NT)
        rr = dtu_cm[:, 0:768].rearrange("p (t c) -> p t c", t=NB)
        xft_a = dtu_cm[:, 768:1280]
        xft_b = dtu_cm[0:CB, 1280:1792]
        x_in = dt_cm[:, 0:NX * CW].rearrange("p (n c) -> p n c", n=NX)
        xe = u_cm[:, 512:1024].rearrange("p (n c) -> p n c", n=2)
        hid = [u_cm[:, 1024:1792], z_cm[:, 0:F]]
        y_out = u_cm[:, 1792:1792 + 2 * C].rearrange("p (n c) -> p n c", n=2)
        w_now = [x_cm[:, 0:W_E], y_cm[:, 0:W_E]]
        at_lo = [z_cm[:, 0:NT * P].rearrange("p (t s) -> p t s", t=NT),
                 dtu_cm[:, 0:NT * P].rearrange("p (t s) -> p t s", t=NT)]
        at_hi = dtu_cm[:, 1536:1536 + TOPK * NT * MT].rearrange("p (k t m) -> p k t m", k=TOPK, t=NT)
        what = u_cm[:, 0:TOPK * NT * 2 * MT].rearrange("p (k t w m) -> p k t w m", k=TOPK, t=NT, w=2)
        gate_e8 = z_cm[:, 1536:1920].rearrange("p (t e) -> p t e", t=NT)
        gate_t = z_cm[:, 1920:2304]

        ps = ctx.enter_context(nc.psum_tensor("ps", [P, 8, 512], F32))

        def q3(t):
            return t.rearrange("p (q n) -> p q n", q=6)

        u3, z3, dt3, dtu3, y3 = (q3(t[:, 0:6 * L]) for t in (u_cm, z_cm, dt_cm, dtu_cm, y_cm))
        x3 = q3(x_cm[:, :])
        ident = cst[:, C_ID:C_ID + P]
        x_dram = nc.dram_tensor("x_dram", [NTOK, CW], F32, kind="Internal").ap()

        ld_idx = sem("ld_idx")
        ld_cst = sem("ld_cst")
        ld_tok = sem("ld_tok")
        ld_mix = sem("ld_mix")
        ld_exp = sem("ld_exp")
        gath12 = sem("gath12")
        gath0 = [sem("gath0_0"), sem("gath0_1")]
        dve_set = sem("dve_set")
        rearr = sem("rearr")
        pe_tok = sem("pe_tok")
        ev_tok = sem("ev_tok")
        h_ready = sem("h_ready")
        ln_step = sem("ln_step")
        std_rdy = sem("std_rdy")
        xn_ready = sem("xn_ready")
        xt_ps = sem("xt_ps")
        xt_ready = sem("xt_ready")
        xz_ps = sem("xz_ps")
        xz_out = sem("xz_out")
        conv_step = sem("conv_step")
        u_ready = sem("u_ready")
        z_ready = sem("z_ready")
        dt_ps = sem("dt_ps")
        bc_ps = sem("bc_ps")
        bc_step = sem("bc_step")
        sp_abs = sem("sp_abs")
        sp_act = sem("sp_act")
        sp_dve = sem("sp_dve")
        log_step = sem("log_step")
        a_exp = sem("a_exp")
        decay_rdy = sem("decay_rdy")
        b_wide = sem("b_wide")
        c_wide = sem("c_wide")
        driven = sem("driven")
        scanned = sem("scanned")
        hc_rdy = sem("hc_rdy")
        summed = sem("summed")
        y_step = sem("y_step")
        attn_ps = sem("attn_ps")
        post = sem("post")
        mixed_free = sem("tops")
        xf_rdy = sem("xf_rdy")
        xft_ps = sem("xft_ps")
        xft_rdy = sem("xft_rdy")
        logit_ps = sem("logit_ps")
        route = sem("route")
        gate_e = sem("gate_e")
        cnt_ps = sem("cnt_ps")
        tok_ps = sem("tok_ps")
        gt_ps = sem("gt_ps")
        gt_rdy = sem("gt_rdy")
        bo_ps = sem("bo_ps")
        h_final = sem("h_final")
        x_sent = sem("x_sent")
        xin_l = [sem(f"xin_l{q}") for q in range(NX)]
        xe_ps = sem("xe_ps")
        xe_rdy = sem("xe_rdy")
        up_rdy = sem("up_weights")
        dn_rdy = sem("down_weights")
        up_ps = sem("up_ps")
        hid_rdy = sem("hid_rdy")
        down_ps = sem("down_ps")
        y_rdy = sem("y_rdy")
        added = sem("added")
        out_st = sem("out_st")

        N_TOK, N_MIX, N_EXP = 10, 8, 4
        JS = [2, 0, 1]
        US = [2, 0, 1]

        def chan_group(u):
            return 1 if u == 2 else 0

        def unit(t, u, lo=0, n=L):
            return t[:, 2 * u:2 * u + 2, lo:lo + n]

        def bank2(b, n=L):
            return ps[:, b:b + 2, 0:n]

        block = ctx.enter_context(nc.Block())

        def expert_loop(eng, step):
            for i in range(NX):
                step(i, i)
            with eng.Fori(1, (MT - 2) // NX) as m:
                for q in range(NX):
                    step(m * NX + q, q)
            for i in range(NX * ((MT - 2) // NX), MT):
                step(i, i % NX)

        def is_at_least(i, n):
            return not isinstance(i, int) or i >= n

        def is_below(i, n):
            return not isinstance(i, int) or i < n

        T_T1, T_T2, T_L12, T_UP = 1, 2, 3, 4
        V_T1, V_T2, V_L12, V_UP = 1, 3, 4, 6
        ROUTE_TOP = NT
        ROUTE_CNT = NT + 3
        ROUTE_GATE = NT + 4
        ROUTE_SLOT = NT + 30
        ROUTE_TOKENS = NT + 35

        @block.sync
        def _(sp):
            sp.dma_start(gidx[:, :], d["gidx"]).then_inc(ld_idx, 16)
            sp.dma_start(h_tok[:, 2, :, :], d["txt"].rearrange("b p c -> p b c")).then_inc(h_ready, 16)
            sp.dma_start(cst[:, :], d["cst"]).then_inc(ld_cst, 16)
            for dst, name in ((w0T, "w0T"), (w1T, "w1T"), (w2T, "w2T"), (b12[:, :], "b12"),
                              (b0[:, :], "b0"), (wf_hi, "wf_hi"), (wf_lo, "wf_lo"), (i1, "i1"), (i2, "i2"),
                              (chan[:, :, :], "chan")):
                sp.dma_start(dst, d[name]).then_inc(ld_tok, 16)
            for dst, name in ((ip_a[:, :], "ip_a"), (ip_b[:, :], "ip_b"), (dw[:, :, :], "dw"), (bc[:, :, :, :], "bc"),
                              (ow[:, :, :], "ow"), (wr[:, :, :], "wr"), (bo[:, :], "bo")):
                sp.dma_start(dst, d[name]).then_inc(ld_mix, 16)
            sp.dma_start(ln_gb[:, :, :], d["ln_gb"].to_broadcast([P, 2, C])).then_inc(ld_mix, 16)
            sp.wait_ge(gath0[1], 16 * GROUP)
            for e in range(E):
                sp.dma_start(w_all[:, W_E * e:W_E * e + W_E], d["w_all"][:, W_E * e:W_E * e + W_E]).then_inc(ld_exp, 16)
            for j in range(NJ):
                sp.wait_ge(xf_rdy, j + 1)
                for c0, c1, src in ((0, C, 0), (C, CW, P)):
                    sp.dma_start(x_dram.rearrange("(b j p) c -> j p b c", b=NB, j=NJ)[j, :, :, c0:c1],
                                 xf[:, NB * j:NB * j + NB, src:C]).then_inc(x_sent, 16)
            sp.wait_ge(h_final, 1)
            for j in range(NJ):
                sp.dma_start(out.rearrange("b (j p) c -> j p b c", j=NJ)[j], h_tok[:, j, :, :]).then_inc(out_st, 16)
            sp.wait_ge(out_st, 16 * NJ)
            sp.wait_ge(added, 16 * MT)

        @block.gpsimd
        def _(pool):
            pool.wait_ge(ld_idx, 16)

            def gather(dst, table, col, signal):
                pool.indirect_dma_start(dst, None, d[table], bass.IndirectOffsetOnAxis(
                    ap=gidx[:, col:col + 1].bitcast(U32), axis=0)).then_inc(signal, 16)

            for n in range(G2):
                gather(g2[:, n, :], "pix2", G0 + G1 + n, gath12)
            for n in range(G1):
                gather(g1[:, n, :], "pix1", G0 + n, gath12)
            for n in range(G0):
                gather(g0[:, n, :], "pix0", n, gath0[n // GROUP])
            pool.wait_ge(route, ROUTE_TOKENS)
            pool.wait_ge(x_sent, 16 * 2 * NJ)
            out_rows = out.rearrange("b t c -> (b t) c")

            def fetch(i):
                pool.indirect_dma_start(x_in[:, i % NX, :], None, x_dram, bass.IndirectOffsetOnAxis(
                    ap=tok_in[:, i:i + 1].bitcast(U32), axis=0)).then_inc(xin_l[i % NX], 16)

            for i in range(NX):
                fetch(i)
            pool.wait_ge(out_st, 16 * NJ)
            for i in range(MT):
                if i + NX < MT:
                    pool.wait_ge(xe_ps, i + 1)
                    fetch(i + NX)
                pool.wait_ge(y_rdy, i + 1)
                if i:
                    pool.wait_ge(added, 16 * i)
                pool.indirect_dma_start(out_rows, bass.IndirectOffsetOnAxis(
                    ap=tok_out[:, i:i + 1].bitcast(U32), axis=0), y_out[:, i % 2, :], None,
                    bounds_check=NTOK - 1, oob_is_err=False, compute_op=ALU.add).then_inc(added, 16)

        @block.tensor
        def _(pe):
            pe.wait_ge(ld_cst, 16)
            pe.wait_ge(ld_tok, 16 * N_TOK)
            pe.wait_ge(rearr, 1)
            for b in range(NB):
                mm = nc.tensor.transpose(ps[0:96, 0, P * b:P * b + P], r1[:, 96 * b:96 * b + 96], ident)
            mm.then_inc(pe_tok, 1)
            for n in range(G2):
                for b in range(NB):
                    mm = nc.tensor.transpose(ps[0:48, 1 + n, P * b:P * b + P], g2[:, n, 48 * b:48 * b + 48], ident)
            mm.then_inc(pe_tok, 1)
            pe.wait_ge(ev_tok, V_T2)
            for half in range(2):
                for kh in range(2):
                    mm = nc.tensor.matmul(ps[:, 3, EMB * half:EMB * half + EMB], t1[:, 256 * kh + P * half:256 * kh + P * half + P],
                                          w1T[:, kh, :], start=(kh == 0), stop=(kh == 1))
            for k in range(GROUP):
                mm = nc.tensor.matmul(ps[0:64, 4, 0:EMB], t2[:, 64 * k:64 * k + 64], w2T[:, k, :],
                                      start=(k == 0), stop=(k == GROUP - 1))
            mm.then_inc(pe_tok, 1)
            pe.wait_ge(ev_tok, V_L12)
            for b in range(NB):
                o = ps[:, 5 + b // 2, N_IMG * (b % 2):N_IMG * (b % 2) + N_IMG]
                nc.tensor.matmul(o[0:64, :], y1[:, EMB * (b // 2):EMB * (b // 2) + EMB],
                                 i1[:, N_IMG * (b % 2):N_IMG * (b % 2) + N_IMG], start=True, stop=True)
                mm = nc.tensor.matmul(o[64:128, :], y2, i2[:, N_IMG * b:N_IMG * b + N_IMG], start=True, stop=True)
            mm.then_inc(pe_tok, 1)

            def tokens_from_patches(jt):
                base_v = 3 * jt
                pe.wait_ge(rearr, 2 + jt)
                for b in range(NB):
                    mm = nc.tensor.transpose(ps[0:48, 0, P * b:P * b + P],
                                             r0[:, 48 * (NB * jt + b):48 * (NB * jt + b) + 48], ident)
                mm.then_inc(pe_tok, 1)
                pe.wait_ge(ev_tok, V_UP + 1 + base_v)
                nc.tensor.matmul(ps[0:EMB, 1, :], w0T, t0[:, 512 * jt:512 * jt + 512],
                                 start=True, stop=True).then_inc(pe_tok, 1)
                pe.wait_ge(ev_tok, V_UP + 2 + base_v)
                for b in range(NB):
                    o = ps[:, 2 + b // 2, 256 * (b % 2):256 * (b % 2) + C]
                    c0 = N_IMG * b + P * jt
                    nc.tensor.matmul(o, ycat_hi[:, c0:c0 + P], wf_hi, start=True, stop=False)
                    mm = nc.tensor.matmul(o, ycat_lo[:, P * b:P * b + P], wf_lo,
                                          start=False, stop=True)
                mm.then_inc(pe_tok, 1)

            def in_projection(n):
                pe.wait_ge(xn_ready, n + 1)
                j = JS[n]
                if n >= 1:
                    pe.wait_ge(xt_ready, 2 * n)
                for b in range(NB):
                    nc.tensor.transpose(ps[:, 7, P * b:P * b + P], xn[:, j, b, 0:P], ident)
                mm = None
                for b in range(NB):
                    mm = nc.tensor.transpose(ps[0:CB, 4, P * b:P * b + P], xn[:, j, b, P:C], ident)
                mm.then_inc(xt_ps, 1)
                pe.wait_ge(xt_ready, 2 * n + 2)
                nc.tensor.matmul(ps[:, 5, :], ip_a[:, 0:P], xt_a, start=True, stop=False)
                nc.tensor.matmul(ps[:, 5, :], ip_b[:, 0:P], xt_b, start=False, stop=True).then_inc(xz_ps, 1)
                nc.tensor.matmul(ps[:, 6, :], ip_a[:, C:C + P], xt_a, start=True, stop=False)
                nc.tensor.matmul(ps[:, 6, :], ip_b[:, C:C + P], xt_b, start=False, stop=True).then_inc(xz_ps, 1)
                for half in range(2):
                    for xz in range(2):
                        o = ps[64 * half:64 * half + 64, 4, 256 * xz:256 * xz + 256]
                        w = slice(C * xz + P, C * xz + C)
                        c = slice(256 * half, 256 * half + 256)
                        nc.tensor.matmul(o, ip_a[:, w], xt_a[:, c], start=True, stop=False)
                        mm = nc.tensor.matmul(o, ip_b[:, w], xt_b[:, c], start=False, stop=True)
                mm.then_inc(xz_ps, 1)

            pe.wait_ge(ld_mix, 16 * N_MIX)
            pe.wait_ge(ev_tok, V_UP)
            in_projection(0)
            tokens_from_patches(0)
            pe.wait_ge(xz_out, 4)
            in_projection(1)
            tokens_from_patches(1)
            pe.wait_ge(xz_out, 8)
            in_projection(2)
            pe.wait_ge(xz_out, 12)

            def from_u(o, wa, wb, b, start_ok=True):
                hb = 64 * (b // 2)
                nc.tensor.matmul(o, wa, u3[:, b, :], start=True, stop=False)
                return nc.tensor.matmul(o, wb[hb:hb + 64], u3[hb:hb + 64, 4 + b % 2, :], start=False, stop=True)

            pe.wait_ge(u_ready, 3)
            for w in range(2):
                if w == 1:
                    pe.wait_ge(bc_step, 2)
                for b in range(NB):
                    mm = from_u(ps[64 * (b // 2):64 * (b // 2) + 64, 6 + b % 2, 0:L], bc[:, 0, w, :], bc[:, 1, w, :], b)
                mm.then_inc(bc_ps, 1)
                if w == 0:
                    for u in US:
                        if u == 2:
                            for b in range(NB):
                                mm = from_u(ps[64 * (b // 2):64 * (b // 2) + 64, 4 + b % 2, 0:L],
                                            dw[:, 0, P:C], dw[:, 1, P:C], b)
                        else:
                            for b in (2 * u, 2 * u + 1):
                                mm = from_u(ps[:, b, 0:L], dw[:, 0, 0:P], dw[:, 1, 0:P], b)
                        mm.then_inc(dt_ps, 1)
            pe.wait_ge(dve_set, 3)
            pe.wait_ge(bc_step, 10)
            pe.wait_ge(sp_dve, 9)
            for n, u in enumerate(US):
                yb = 4 + 2 * (n % 2)
                if n == 2:
                    pe.wait_ge(y_step, 2)

                def spread(s, parts, bank, signal):
                    for i in range(2):
                        mm = nc.tensor.matmul(ps[:, bank + i, 0:L], pick[:, u, bass.ds(s, 1), :].rearrange("p o c -> p (o c)"),
                                              parts[:, i, :], start=True, stop=True)
                    mm.then_inc(signal, 1)

                def sum_states(s, start, stop):
                    pe.wait_ge(hc_rdy, S * n + s + 1)
                    for i in range(2):
                        mm = nc.tensor.matmul(ps[:, yb + i, 0:L], ident, hc[:, i, :], start=start, stop=stop)
                    mm.then_inc(summed, 1)

                if n:
                    pe.wait_ge(driven, S * n)
                spread(0, b_parts, 0, b_wide)
                if n:
                    pe.wait_ge(hc_rdy, S * n)
                spread(0, c_parts, 2, c_wide)
                pe.wait_ge(driven, S * n + 1)
                spread(1, b_parts, 0, b_wide)
                pe.wait_ge(hc_rdy, S * n + 1)
                spread(1, c_parts, 2, c_wide)
                sum_states(0, True, False)
                with pe.Fori(2, S) as s:
                    pe.wait_ge(driven, s + S * n)
                    spread(s, b_parts, 0, b_wide)
                    pe.wait_ge(hc_rdy, s + S * n)
                    spread(s, c_parts, 2, c_wide)
                    sum_states(s - 1, False, False)
                sum_states(S - 1, False, True)
            pe.wait_ge(y_step, 6)
            for j in range(NJ):
                if j:
                    pe.wait_ge(post, 13 * (j - 1) + 1)
                for b in range(NB):
                    o = ps[:, b // 2, 256 * (b % 2):256 * (b % 2) + C]
                    hb = 64 * (b // 2)
                    nc.tensor.matmul(o, y3[:, b, P * j:P * j + P], ow[:, 0, :], start=True, stop=False)
                    mm = nc.tensor.matmul(o, y3[hb:hb + 64, 4 + b % 2, P * j:P * j + P], ow[hb:hb + 64, 1, :],
                                          start=False, stop=True)
                mm.then_inc(attn_ps, 1)
                pe.wait_ge(xf_rdy, j + 1)
                for b in range(NB):
                    nc.tensor.transpose(ps[:, 2, P * b:P * b + P], xf[:, NB * j + b, 0:P], ident)
                for b in range(NB):
                    mm = nc.tensor.transpose(ps[0:CB, 3, P * b:P * b + P], xf[:, NB * j + b, P:C], ident)
                mm.then_inc(xft_ps, 1)
                pe.wait_ge(xft_rdy, 2 * j + 2)
                for b in range(NB):
                    o = ps[:, 4, E * (NB * j + b):E * (NB * j + b) + E]
                    nc.tensor.matmul(o, xft_a[:, P * b:P * b + P], wr[:, 0, :], start=True, stop=False)
                    mm = nc.tensor.matmul(o, xft_b[:, P * b:P * b + P], wr[0:CB, 1, :], start=False, stop=True)
                mm.then_inc(logit_ps, 1)
            pe.wait_ge(route, ROUTE_CNT)
            cv = cnt[:, :, :].rearrange("p e t -> p (e t)")
            nc.tensor.matmul(ps[:, 5, 0:E * NT], cst[:, C_UP:C_UP + P], cv, start=True, stop=True)
            nc.tensor.matmul(ps[:, 6, 0:E * NT], ones_sq[:, :], cv, start=True, stop=True).then_inc(cnt_ps, 1)

            pe.wait_ge(route, ROUTE_SLOT)
            for k in range(TOPK):
                for t in range(NT):
                    mm = nc.tensor.matmul(ps[:, 7, 0:2 * MT], at_lo[k][:, t, :],
                                          what[:, k, t, :, :].rearrange("p w m -> p (w m)"),
                                          start=(k == 0 and t == 0), stop=(k == TOPK - 1 and t == NT - 1))
            mm.then_inc(tok_ps, 1)
            for j in range(NJ):
                mm = nc.tensor.transpose(ps[:, 0, P * j:P * j + P],
                                         gate_e8[:, NB * j:NB * j + NB, :].rearrange("p t e -> p (t e)"), ident)
            mm.then_inc(gt_ps, 1)
            pe.wait_ge(gt_rdy, 1)
            pe.wait_ge(route, ROUTE_TOKENS)
            for j in range(NJ):
                for b in range(NB):
                    o = ps[:, b, 256 * j:256 * j + C] if j < 2 else ps[:, 4 + b, 0:C]
                    mm = nc.tensor.matmul(o, gate_t[32 * b:32 * b + E, P * j:P * j + P], bo[32 * b:32 * b + E, :],
                                          start=True, stop=True)
            mm.then_inc(bo_ps, 1)
            pe.wait_ge(h_final, 1)

            def x_transposed(i, q):
                p = q % 2
                pe.wait_ge(xin_l[q], 16 * (i // NX + 1) if isinstance(i, int) else (i - q) * (16 // NX) + 16)
                if is_at_least(i, 2):
                    pe.wait_ge(xe_rdy, i - 1)
                for c in range(2):
                    mm = nc.tensor.transpose(ps[:, p, P * c:P * c + P], x_in[:, q, P * c:P * c + P], ident)
                mm.then_inc(xe_ps, 1)

            def up(i, p):
                pe.wait_ge(xe_rdy, i + 1)
                pe.wait_ge(up_rdy, i + 1)
                if is_at_least(i, 2):
                    pe.wait_ge(hid_rdy, i - 1)
                w = w_now[p]
                for f in range(FC):
                    nc.tensor.matmul(ps[:, 2 + 2 * p + f // 3, P * (f % 3):P * (f % 3) + P],
                                     w[:, W_UA + P * f:W_UA + P * f + P], xe[:, p, 0:P],
                                     start=(f % 3 == 0), stop=False, skip_group_check=True)
                for f in range(FC // 2):
                    for half in range(2):
                        r = slice(CB * half, CB * half + CB)
                        mm = nc.tensor.matmul(ps[:, 2 + 2 * p + half, P * f:P * f + P],
                                              w[r, W_UB + P * f:W_UB + P * f + P], xe[r, p, P:2 * P],
                                              start=False, stop=True, skip_group_check=True)
                mm.then_inc(up_ps, 1)

            def down(i, p):
                pe.wait_ge(hid_rdy, i + 1)
                pe.wait_ge(dn_rdy, i + 1)
                if is_at_least(i, 2):
                    pe.wait_ge(y_rdy, i - 1)
                for f in range(FC):
                    mm = nc.tensor.matmul(ps[:, 6 + p, 0:C], hid[p][:, P * f:P * f + P],
                                          w_now[p][:, W_DN + C * f:W_DN + C * f + C], start=(f == 0), stop=(f == FC - 1))
                mm.then_inc(down_ps, 1)

            x_transposed(0, 0)
            x_transposed(1, 1)
            up(0, 0)

            def expert_tile(i, q):
                p = q % 2
                if is_below(i, MT - 2):
                    x_transposed(i + 2, (q + 2) % NX)
                if is_below(i, MT - 1):
                    up(i + 1, 1 - p)
                down(i, p)
            expert_loop(pe, expert_tile)

        @block.scalar
        def _(act):
            act.wait_ge(gath12, 16 * (G2 + G1))
            nc.scalar.activation(r1.rearrange("p (b d c) -> p d b c", b=NB, d=G1),
                                 g1.rearrange("p d (b c) -> p d b c", b=NB), ACT.Copy).then_inc(rearr, 1)
            act.wait_ge(pe_tok, T_T1)
            nc.scalar.activation(t1.rearrange("p (k b t) -> p b k t", k=2, b=NB),
                                 ps[0:96, 0, :].rearrange("p (b k t) -> p b k t", b=NB, k=2), ACT.Copy).then_inc(ev_tok, 1)
            act.wait_ge(pe_tok, T_T2)
            for n in range(G2):
                nc.scalar.activation(t2[:, 512 * n:512 * n + 512].rearrange("p (k b t) -> p b k t", k=8, b=NB),
                                     ps[0:48, 1 + n, :].rearrange("p (b k t) -> p b k t", b=NB, k=8), ACT.Copy).then_inc(ev_tok, 1)
            act.wait_ge(pe_tok, T_L12)
            nc.scalar.activation(y1, ps[:, 3, 0:2 * EMB], ACT.Copy)
            nc.scalar.activation(y2, ps[0:64, 4, 0:EMB], ACT.Copy).then_inc(ev_tok, 1)
            act.wait_ge(pe_tok, T_UP)
            act.wait_ge(ld_tok, 16 * N_TOK)
            for h in range(2):
                nc.scalar.activation(ycat_hi[:, 512 * h:512 * h + 512], ps[:, 5 + h, :], ACT.Identity,
                                     bias=b12[:, 0:1]).then_inc(ev_tok, 1)

            def tokens_from_patches(jt):
                act.wait_ge(gath0[jt], 16 * GROUP)
                nc.scalar.activation(
                    r0[:, 192 * jt:192 * jt + 192].rearrange("p (b k c) -> p k b c", b=NB, k=GROUP),
                    g0[:, GROUP * jt:GROUP * jt + GROUP, :].rearrange("p k (b c) -> p k b c", b=NB),
                    ACT.Copy).then_inc(rearr, 1)
                act.wait_ge(pe_tok, T_UP + 1 + 3 * jt)
                nc.scalar.activation(t0[:, 512 * jt:512 * jt + 512], ps[0:48, 0, :], ACT.Copy).then_inc(ev_tok, 1)
                act.wait_ge(pe_tok, T_UP + 2 + 3 * jt)
                nc.scalar.activation(ycat_lo[0:EMB, :], ps[0:EMB, 1, :], ACT.Identity,
                                     bias=b0[:, 0:1]).then_inc(ev_tok, 1)
                act.wait_ge(pe_tok, T_UP + 3 + 3 * jt)
                for h in range(2):
                    ins = nc.scalar.activation(h_tok[:, jt, 2 * h:2 * h + 2, :],
                                               ps[:, 2 + h, :].rearrange("p (b c) -> p b c", b=2)[:, :, 0:C], ACT.Copy)
                ins.then_inc(ev_tok, 1)

            def deviation(n):
                act.wait_ge(ln_step, 9 * n + 8)
                nc.scalar.activation(std[:, :], mv[:, :, 1], ACT.Sqrt, bias=cst[:, C_EPS:C_EPS + 1]).then_inc(std_rdy, 1)

            def in_projection(n):
                j = JS[n]
                deviation(n)
                act.wait_ge(xt_ps, n + 1)
                nc.scalar.activation(xt_a, ps[:, 7, :], ACT.Copy).then_inc(xt_ready, 1)
                nc.scalar.activation(xt_b, ps[0:CB, 4, :], ACT.Copy).then_inc(xt_ready, 1)
                t = slice(K - 1 + P * j, K - 1 + P * j + P)
                act.wait_ge(xz_ps, 3 * n + 1)
                nc.scalar.activation(x3[:, 0:NB, t], ps[:, 5, :].rearrange("p (b t) -> p b t", b=NB),
                                     ACT.Copy).then_inc(xz_out, 1)
                act.wait_ge(xz_ps, 3 * n + 2)
                nc.scalar.activation(z3[:, 0:NB, P * j:P * j + P], ps[:, 6, :].rearrange("p (b t) -> p b t", b=NB),
                                     ACT.Copy).then_inc(xz_out, 1)
                act.wait_ge(xz_ps, 3 * n + 3)
                nc.scalar.activation(x3[:, NB:6, t], ps[:, 4, 0:256].rearrange("p (b t) -> p b t", b=2),
                                     ACT.Copy).then_inc(xz_out, 1)
                nc.scalar.activation(z3[:, NB:6, P * j:P * j + P], ps[:, 4, 256:512].rearrange("p (b t) -> p b t", b=2),
                                     ACT.Copy).then_inc(xz_out, 1)

            in_projection(0)
            tokens_from_patches(0)
            in_projection(1)
            tokens_from_patches(1)
            in_projection(2)
            act.wait_ge(xz_out, 12)
            nc.scalar.activation(z_cm[:, :], z_cm[:, :], ACT.Silu).then_inc(z_ready, 1)
            for n, u in enumerate(US):
                act.wait_ge(conv_step, K * (n + 1))
                g = chan_group(u)
                nc.scalar.activation(unit(u3, u), unit(y3, u), ACT.Silu, bias=chan[:, g, H_CB:H_CB + 1]).then_inc(u_ready, 1)
            act.wait_ge(bc_ps, 1)
            nc.scalar.activation(a_neg[:, :, :], chan[:, :, H_A:H_A + S], ACT.Exp).then_inc(a_exp, 1)
            for n, u in enumerate(US):
                g = chan_group(u)
                act.wait_ge(dt_ps, n + 1)
                nc.scalar.activation(unit(dt3, u), bank2(2 * u), ACT.Abs, bias=chan[:, g, H_DTB:H_DTB + 1]).then_inc(sp_act, 1)
            for n, u in enumerate(US):
                act.wait_ge(sp_act, 3 + n)
                nc.scalar.activation(unit(dt3, u), unit(dt3, u), ACT.Exp, scale=-1.0).then_inc(sp_act, 1)
            act.wait_ge(a_exp, 2)
            for n, u in enumerate(US):
                act.wait_ge(sp_dve, 3 * n + 3)
                g = chan_group(u)
                with act.Fori(0, S // 2) as m:
                    for p in range(2):
                        act.wait_ge(scanned, m * 2 + (S * n + p + 1))
                        nc.scalar.activation(decay[:, p, :, 1:L], unit(dt3, u, 1, L - 1), ACT.Exp,
                                             scale=a_neg[:, g, bass.ds(m * 2 + p, 1)]).then_inc(decay_rdy, 1)
            for j in range(NJ):
                deviation(NJ + 2 * j)
                deviation(NJ + 2 * j + 1)
                act.wait_ge(xft_ps, j + 1)
                if j:
                    act.wait_ge(logit_ps, j)
                nc.scalar.activation(xft_a, ps[:, 2, :], ACT.Copy).then_inc(xft_rdy, 1)
                nc.scalar.activation(xft_b, ps[0:CB, 3, :], ACT.Copy).then_inc(xft_rdy, 1)
            act.wait_ge(route, ROUTE_GATE)
            nc.scalar.activation(gtmp[:, 0, :], gtmp[:, 0, :], ACT.Exp).then_inc(gate_e, 1)

            act.wait_ge(gt_ps, 1)
            nc.scalar.activation(gate_t, ps[:, 0, 0:NJ * P], ACT.Copy).then_inc(gt_rdy, 1)

            def hidden(i, p):
                act.wait_ge(up_ps, i + 1)
                if is_at_least(i, 2):
                    act.wait_ge(down_ps, i - 1)
                for f in range(FC):
                    ins = nc.scalar.activation(hid[p][:, P * f:P * f + P],
                                               ps[:, 2 + 2 * p + f // 3, P * (f % 3):P * (f % 3) + P],
                                               ACT.Gelu, bias=w_now[p][:, W_BI + f:W_BI + f + 1])
                ins.then_inc(hid_rdy, 1)

            act.wait_ge(route, ROUTE_TOKENS)
            hidden(0, 0)

            def expert_tile(i, q):
                p = q % 2
                if is_below(i, MT - 1):
                    hidden(i + 1, 1 - p)
                act.wait_ge(down_ps, i + 1)
                if is_at_least(i, 2):
                    act.wait_ge(added, 16 * (i - 1))
                nc.scalar.activation(y_out[:, p, :], ps[:, 6 + p, 0:C], ACT.Copy,
                                     scale=gate_s[:, bass.ds(i, 1)]).then_inc(y_rdy, 1)
            expert_loop(act, expert_tile)

        @block.vector
        def _(dve):
            v = nc.vector
            dve.wait_ge(ld_cst, 16)
            rows = cst[:, C_ROW:C_ROW + 2 * S].rearrange("p (u s) -> p u s", u=2)
            v.tensor_copy(pick[:, 0:2, :, :].rearrange("p u s c -> p (u s) c"),
                          cst[:, C_ROW:C_ROW + 2 * S].rearrange("p (n o) -> p n o", o=1).to_broadcast([P, 2 * S, P]))\
                .then_inc(dve_set, 1)
            for half in range(2):
                v.tensor_copy(pick[:, 2, :, 64 * half:64 * half + 64],
                              rows[:, half, :].rearrange("p (s o) -> p s o", o=1).to_broadcast([P, S, 64]))\
                    .then_inc(dve_set, 1)
            v.memset(ones_sq[:, :], 1.0).then_inc(dve_set, 1)
            v.memset(ycat_lo[EMB:EMB + 1, :], 1.0).then_inc(dve_set, 1)
            v.memset(x3[:, :, 0:K - 1], 0.0).then_inc(dve_set, 1)

            def norm_stats(src, signal, at):
                for b in range(NB):
                    v.bn_stats(stats[:, b, :], src[:, b, :]).then_inc(signal, 1)
                dve.wait_ge(signal, at + 4)
                for b in range(NB):
                    v.bn_aggr(mv[:, b, :], stats[:, b, :]).then_inc(signal, 1)
                dve.wait_ge(signal, at + 8)
                dve.wait_ge(std_rdy, at // 9 + 1)
                v.reciprocal(rstd[:, :], std[:, :]).then_inc(signal, 1)
                dve.wait_ge(signal, at + 9)

            def normalise(dst, src, b):
                return v.tensor_scalar(dst, src, mv[:, b, 0:1], rstd[:, b:b + 1], ALU.subtract, ALU.mult)

            for n, j in enumerate(JS):
                if n == 0:
                    dve.wait_ge(h_ready, 16)
                else:
                    dve.wait_ge(ev_tok, V_UP + 3 * n)
                norm_stats(h_tok[:, j, :, :], ln_step, 9 * n)
                for b in range(NB):
                    ins = normalise(xn[:, j, b, :], h_tok[:, j, b, :], b)
                ins.then_inc(xn_ready, 1)
                dve.wait_ge(xn_ready, n + 1)

            dve.wait_ge(xz_out, 12)
            dve.wait_ge(dve_set, 6)
            for n, u in enumerate(US):
                g = chan_group(u)
                v.tensor_scalar(unit(y3, u), unit(x3, u, K - 1), chan[:, g, H_W + K - 1:H_W + K], None,
                                ALU.mult).then_inc(conv_step, 1)
                for k in range(K - 1):
                    dve.wait_ge(conv_step, K * n + k + 1)
                    v.scalar_tensor_tensor(unit(y3, u), unit(x3, u, k), chan[:, g, H_W + k:H_W + k + 1],
                                           unit(y3, u), ALU.mult, ALU.add).then_inc(conv_step, 1)
            hi = drive[:, :, :]
            for w, parts in enumerate((b_parts, c_parts)):
                n = 5 * w
                dve.wait_ge(bc_ps, w + 1)
                if w:
                    dve.wait_ge(bc_step, 5)
                v.tensor_copy(parts[:, :, :], bank2(6)).then_inc(bc_step, 1)
                dve.wait_ge(bc_step, n + 1)
                v.scalar_tensor_tensor(hi, parts[:, :, :], cst[:, C_NEG:C_NEG + 1], bank2(6), ALU.mult, ALU.add)\
                    .then_inc(bc_step, 1)
                dve.wait_ge(bc_step, n + 2)
                v.tensor_copy(parts[:, :, :], hi).then_inc(bc_step, 1)
                dve.wait_ge(bc_step, n + 3)
                v.scalar_tensor_tensor(hi, parts[:, :, :], cst[:, C_NEG + 1:C_NEG + 2], hi, ALU.mult, ALU.add)\
                    .then_inc(bc_step, 1)
                dve.wait_ge(bc_step, n + 4)
                v.tensor_copy(parts[:, :, :], hi).then_inc(bc_step, 1)
                if w == 0:
                    dve.wait_ge(a_exp, 1)
                    v.tensor_scalar(a_neg[:, :, :], a_neg[:, :, :], -1.0, None, ALU.mult).then_inc(a_exp, 1)
                    for m, u in enumerate(US):
                        g = chan_group(u)
                        dve.wait_ge(sp_act, m + 1)
                        v.tensor_scalar(unit(dtu3, u), bank2(2 * u), chan[:, g, H_DTB:H_DTB + 1], 0.0,
                                        ALU.add, ALU.max).then_inc(sp_abs, 1)
            for n, u in enumerate(US):
                dve.wait_ge(sp_act, 4 + n)
                e, poly = unit(dt3, u), state[:, :, :]
                v.tensor_scalar(poly, e, LOG1P[-1], None, ALU.mult).then_inc(log_step, 1)
                for k, coefficient in enumerate(LOG1P[-2::-1]):
                    dve.wait_ge(log_step, len(LOG1P) * n + k + 1)
                    v.scalar_tensor_tensor(poly, poly, coefficient, e, ALU.add, ALU.mult).then_inc(log_step, 1)
                dve.wait_ge(log_step, len(LOG1P) * (n + 1))
                dve.wait_ge(sp_abs, n + 1)
                v.tensor_tensor(unit(dt3, u), poly, unit(dtu3, u), ALU.add).then_inc(sp_dve, 1)
                dve.wait_ge(sp_dve, 3 * n + 1)
                v.tensor_tensor(unit(dtu3, u), unit(dt3, u), unit(u3, u), ALU.mult).then_inc(sp_dve, 1)
                dve.wait_ge(sp_dve, 3 * n + 2)
                g = chan_group(u)
                v.tensor_scalar(unit(y3, u), unit(u3, u), chan[:, g, H_D:H_D + 1], None, ALU.mult).then_inc(sp_dve, 1)
            for p in range(2):
                v.memset(decay[:, p, :, 0:1], 0.0).then_inc(scanned, 1)
            dve.wait_ge(bc_step, 10)
            dve.wait_ge(sp_dve, 9)
            for n, u in enumerate(US):
                yb = 4 + 2 * (n % 2)
                def state_pass(m, p):
                    at = m * 2 + (S * n + p)
                    dve.wait_ge(b_wide, at + 1)
                    v.tensor_tensor(drive[:, :, :], unit(dtu3, u), bank2(0), ALU.mult).then_inc(driven, 1)
                    dve.wait_ge(driven, at + 1)
                    dve.wait_ge(decay_rdy, at + 1)
                    v.tensor_tensor_scan(state[:, :, :].rearrange("p a c -> p (a c)"),
                                         decay[:, p, :, :].rearrange("p a c -> p (a c)"),
                                         drive[:, :, :].rearrange("p a c -> p (a c)"), 0.0,
                                         ALU.mult, ALU.add).then_inc(scanned, 1)
                    dve.wait_ge(scanned, at + 3)
                    dve.wait_ge(c_wide, at + 1)
                    if is_at_least(at, 1):
                        dve.wait_ge(summed, at)
                    v.tensor_tensor(hc[:, :, :], state[:, :, :], bank2(2), ALU.mult).then_inc(hc_rdy, 1)

                state_pass(0, 0)
                state_pass(0, 1)
                with dve.Fori(1, S // 2) as m:
                    state_pass(m, 0)
                    state_pass(m, 1)
                dve.wait_ge(summed, S * (n + 1))
                v.tensor_tensor(unit(y3, u), bank2(yb), unit(y3, u), ALU.add).then_inc(y_step, 1)
                dve.wait_ge(y_step, 2 * n + 1)
                dve.wait_ge(z_ready, 1)
                v.tensor_tensor(unit(y3, u), unit(y3, u), unit(z3, u), ALU.mult).then_inc(y_step, 1)
            g4 = ln_gb[:, 0:1, :].to_broadcast([P, NB, C])
            b4 = ln_gb[:, 1:2, :].to_broadcast([P, NB, C])
            at = 0

            def step(ins):
                nonlocal at
                at += 1
                ins.then_inc(post, 1)
                dve.wait_ge(post, at)

            ln_at = 9 * NJ
            for j in range(NJ):
                dve.wait_ge(attn_ps, j + 1)
                for h in range(2):
                    ins = v.tensor_tensor(rr[:, 2 * h:2 * h + 2, :],
                                          ps[:, h, :].rearrange("p (b c) -> p b c", b=2)[:, :, 0:C],
                                          xn[:, j, 2 * h:2 * h + 2, :], ALU.add)
                step(ins)
                norm_stats(rr, ln_step, ln_at)
                ln_at += 9
                for b in range(NB):
                    step(normalise(rr[:, b, :], rr[:, b, :], b))
                step(v.tensor_tensor(rr, rr, g4, ALU.mult))
                step(v.tensor_tensor(rr, rr, b4, ALU.add))
                step(v.tensor_tensor(h_tok[:, j, :, :], h_tok[:, j, :, :], rr, ALU.add))
                norm_stats(h_tok[:, j, :, :], ln_step, ln_at)
                ln_at += 9
                for b in range(NB):
                    ins = normalise(xf[:, NB * j + b, :], h_tok[:, j, b, :], b)
                    step(ins)
                step(v.memset(rstd[:, :], 0.0))
                v.memset(stats[:, 0, :], 0.0).then_inc(xf_rdy, 1)
                dve.wait_ge(xf_rdy, j + 1)
            dve.wait_ge(logit_ps, NJ)
            at_r = 0

            def rt(ins):
                nonlocal at_r
                at_r += 1
                ins.then_inc(route, 1)
                dve.wait_ge(route, at_r)

            v.tensor_copy(logit[:, :, :], ps[:, 4, 0:E * NT].rearrange("p (t e) -> p t e", t=NT)).then_inc(mixed_free, 1)
            dve.wait_ge(mixed_free, 1)
            for t in range(NT):
                v.max(top_v[:, t, :], logit[:, t, :]).then_inc(mixed_free, 1)
            dve.wait_ge(mixed_free, 1 + NT)
            for t in range(NT):
                ins = v.max_index(top_i[:, t, :], top_v[:, t, :], logit[:, t, :])
                ins.then_inc(route, 1)
            at_r = NT
            dve.wait_ge(route, NT)
            rt(v.tensor_copy(idf[:, :, :], top_i[:, :, 0:TOPK]))
            e8 = cst[:, C_E8:C_E8 + E].rearrange("p (o e) -> p o e", o=1).to_broadcast([P, NT, E])
            for k in range(TOPK):
                ins = v.tensor_tensor(hot[:, k, :, :], idf[:, :, k:k + 1].to_broadcast([P, NT, E]), e8, ALU.is_equal)
            rt(ins)
            rt(v.tensor_tensor(cnt[:, :, :].rearrange("p e t -> p t e"), hot[:, 0, :, :], hot[:, 1, :, :], ALU.add))
            rt(v.tensor_tensor(gtmp[:, 0, :], top_v[:, :, 1], top_v[:, :, 0], ALU.subtract))
            dve.wait_ge(gate_e, 1)
            rt(v.tensor_scalar(gtmp[:, 1, :], gtmp[:, 0, :], 1.0, None, ALU.add))
            rt(v.reciprocal(gate[:, 0, :], gtmp[:, 1, :]))
            rt(v.tensor_tensor(gate[:, 1, :], gtmp[:, 0, :], gate[:, 0, :], ALU.mult))
            dve.wait_ge(cnt_ps, 1)
            tot = ps[:, 6, 0:E * NT]
            runf = run[:, :, :].rearrange("p e t -> p (e t)")
            rt(v.tensor_tensor_scan(runf, cst[:, C_MASK:C_MASK + E * NT], tot, 0.0, ALU.mult, ALU.add))
            m12 = cst[:, C_M12:C_M12 + NT].rearrange("p (o m) -> p o m", o=1).to_broadcast([P, E, NT])
            rt(v.tensor_tensor(cmp12[:, :, :], run[:, :, NT - 1:NT].to_broadcast([P, E, NT]), m12, ALU.is_gt))
            rt(v.tensor_reduce(tiles[:, :], cmp12[:, :, :], AX_X, ALU.add))
            rt(v.tensor_tensor_scan(ends[:, :], ones_sq[:, 0:E], tiles[:, :], 0.0, ALU.mult, ALU.add))
            rt(v.tensor_tensor(first[:, :], ends[:, :], tiles[:, :], ALU.subtract))
            rt(v.tensor_tensor(runf, runf, tot, ALU.subtract))
            rt(v.tensor_tensor(runf, runf, ps[:, 5, 0:E * NT], ALU.add))
            rt(v.scalar_tensor_tensor(pos[:, :, :].rearrange("p t e -> p e t"),
                                      first[:, :].rearrange("p (e o) -> p e o", o=1).to_broadcast([P, E, NT]),
                                      float(P), run[:, :, :], ALU.mult, ALU.add))
            for k in range(TOPK):
                ins = v.tensor_tensor(pos_k[:, k, :, :], hot[:, k, :, :], pos[:, :, :], ALU.mult)
            rt(ins)
            rt(v.tensor_reduce(slot_f, pos_k[:, :, :, :].rearrange("p k t e -> p (k t) e"), AX_X, ALU.add))
            t31 = cst[0:P, C_IOTA:C_IOTA + MT].rearrange("p (m o) -> p m o", o=1)[0:1].to_broadcast([1, MT, E])
            rt(v.tensor_tensor(tcmp[:, :, :], ends[0:1, :].rearrange("p (o e) -> p o e", o=1).to_broadcast([1, MT, E]),
                               t31, ALU.is_le))
            rt(v.tensor_reduce(tex[:, :], tcmp[:, :, :], AX_X, ALU.add))
            rt(v.tensor_scalar(tex[:, :], tex[:, :], float(E - 1), None, ALU.min))
            rt(v.tensor_copy(texi[:, :], tex[:, :]))
            rt(v.tensor_copy(slot_i[:, 0, :], slot_f))
            rt(v.tensor_scalar(slot_i[:, 1, :], slot_i[:, 0, :], 7, None, ALU.logical_shift_right))
            rt(v.tensor_scalar(slot_i[:, 2, :], slot_i[:, 0, :], P - 1, None, ALU.bitwise_and))
            rt(v.tensor_copy(digit[:, :, :], slot_i[:, 1:3, :]))
            dig = digit[:, :, :].rearrange("p d (k t o) -> p d k t o", k=TOPK, o=1)
            iota_m = cst[:, C_IOTA:C_IOTA + MT].rearrange("p (o m) -> p o m", o=1).to_broadcast([P, NT, MT])
            iota_p = cst[:, C_IOTA:C_IOTA + P].rearrange("p (o m) -> p o m", o=1).to_broadcast([P, NT, P])
            tok1 = cst[:, C_TOK:C_TOK + NT].rearrange("p (t o) -> p t o", o=1).to_broadcast([P, NT, MT])
            for k in range(TOPK):
                ins = v.tensor_tensor(at_hi[:, k, :, :], dig[:, 0, k, :, :].to_broadcast([P, NT, MT]), iota_m, ALU.is_equal)
            rt(ins)
            for k in range(TOPK):
                v.tensor_tensor(at_lo[k], dig[:, 1, k, :, :].to_broadcast([P, NT, P]), iota_p, ALU.is_equal)
                v.tensor_tensor(what[:, k, :, 0, :], at_hi[:, k, :, :], tok1, ALU.mult)
                ins = v.tensor_tensor(what[:, k, :, 1, :], at_hi[:, k, :, :],
                                      gate[:, k, :].rearrange("p (t o) -> p t o", o=1).to_broadcast([P, NT, MT]), ALU.mult)
            rt(ins)
            rt(v.memset(gate_e8, 0.0))
            for k in range(TOPK):
                ins = v.tensor_tensor(pos_k[:, k, :, :], hot[:, k, :, :],
                                      gate[:, k, :].rearrange("p (t o) -> p t o", o=1).to_broadcast([P, NT, E]), ALU.mult)
            rt(ins)
            rt(v.tensor_tensor(gate_e8[:, :, 0:E], pos_k[:, 0, :, :], pos_k[:, 1, :, :], ALU.add))
            assert at_r == ROUTE_SLOT, at_r
            dve.wait_ge(tok_ps, 1)
            rt(v.tensor_scalar(tex_s[:, 0, :], ps[:, 7, 0:MT], -1.0, None, ALU.add))
            rt(v.tensor_scalar(tex_s[:, 1, :], tex_s[:, 0, :], 0.0, None, ALU.max))
            rt(v.tensor_copy(tok_out[:, :], tex_s[:, 0, :]))
            rt(v.tensor_copy(tok_in[:, :], tex_s[:, 1, :]))
            rt(v.tensor_copy(gate_s[:, :], ps[:, 7, MT:2 * MT]))
            assert at_r == ROUTE_TOKENS, at_r

            def up_weights(i, p):
                e = dve.value_load(texi[0:1, bass.ds(i, 1)], min_val=0, max_val=E - 1)
                if is_at_least(i, 2):
                    dve.wait_ge(hid_rdy, i - 1)
                v.tensor_copy(w_now[p][:, 0:W_DN], w_all[:, bass.ds(e * W_E, W_DN)]).then_inc(up_rdy, 1)
                return e

            def down_weights(i, p, e):
                if is_at_least(i, 2):
                    dve.wait_ge(down_ps, i - 1)
                v.tensor_copy(w_now[p][:, W_DN:W_E], w_all[:, bass.ds(e * W_E + W_DN, W_E - W_DN)]).then_inc(dn_rdy, 1)

            def tokens(i, p):
                dve.wait_ge(xe_ps, i + 1)
                if is_at_least(i, 2):
                    dve.wait_ge(up_ps, i - 1)
                v.tensor_copy(xe[:, p, :], ps[:, p, 0:2 * P]).then_inc(xe_rdy, 1)

            dve.wait_ge(ld_exp, 16 * E)
            e = up_weights(0, 0)
            dve.wait_ge(bo_ps, 1)
            for b in range(NB):
                v.tensor_tensor(h_tok[:, 0:2, b, :], h_tok[:, 0:2, b, :],
                                ps[:, b, :].rearrange("p (j c) -> p j c", j=2)[:, :, 0:C], ALU.add)
            for b in range(NB):
                ins = v.tensor_tensor(h_tok[:, 2, b, :], h_tok[:, 2, b, :], ps[:, 4 + b, 0:C], ALU.add)
            ins.then_inc(h_final, 1)
            tokens(0, 0)
            down_weights(0, 0, e)

            def expert_tile(i, q):
                p = q % 2
                if is_below(i, MT - 1):
                    tokens(i + 1, 1 - p)
                    e = up_weights(i + 1, 1 - p)
                    down_weights(i + 1, 1 - p, e)
            expert_loop(dve, expert_tile)


def kernel(**x):
    import numpy as _np
    import concourse.bacc as _bacc
    from concourse import mybir as _mybir
    from concourse.bass_utils import run_bass_kernel_spmd as _run

    a = {n: _np.asarray(v) for n, v in x.items()}
    cat = _np.concatenate

    def patches(p):
        h = 64 // p
        t = a["x"].reshape(4, 3, h, p, h, p).transpose(2, 4, 0, 3, 5, 1)
        return t.reshape(h * h, 4 * p * p * 3)

    def chunks(w):
        return _np.stack([w[0:128], cat([w[128:192], w[128:192]])], axis=1)

    def parts(w):
        return cat([w.T, w.T, w.T, _np.zeros_like(w.T)], axis=1)

    A, M, T = "L0_attn_", "L0_ffn_", "L0_tok_"
    wfT = a[T + "Wf"].T
    wiT = a[M + "Wi"].transpose(2, 0, 1)
    d = {
        "pix0": patches(1), "pix1": patches(2), "pix2": patches(4),
        "gidx": cat([a[T + "idx0"].reshape(2, 128, 16).transpose(1, 0, 2).reshape(128, 32),
                     a[T + "idx1"].reshape(64, 2, 8).transpose(1, 0, 2).reshape(128, 8),
                     a[T + "idx2"].reshape(16, 2, 8).transpose(2, 0, 1).reshape(128, 2)], axis=1),
        "txt": a["txt"], "cst": constants(),
        "w0T": a[T + "W0"].T, "w1T": a[T + "W1"].T.reshape(2, 96, 64).transpose(1, 0, 2),
        "w2T": a[T + "W2"].T.reshape(16, 48, 64).transpose(1, 0, 2),
        "b12": cat([a[T + "b1"], a[T + "b2"]])[:, None], "b0": a[T + "b0"][:, None],
        "wf_hi": wfT[64:192], "wf_lo": cat([wfT[0:64], a[T + "bf"][None]]),
        "i1": interpolation(64, 2).reshape(128, 512), "i2": interpolation(16, 4).reshape(64, 1024),
        "chan": chunks(cat([a[A + "conv_w"].reshape(192, 4), a[A + "conv_b"][:, None], a[A + "dt_b"][:, None],
                            a[A + "D_param"][:, None], a[A + "A_log"]], axis=1)),
        "ip_a": a[A + "in_proj_w"].T[0:128], "ip_b": a[A + "in_proj_w"].T[128:192],
        "dw": chunks(a[A + "dt_w"].T),
        "bc": chunks(_np.stack([parts(a[A + "B_w"]), parts(a[A + "C_w"])], axis=1)),
        "ow": chunks(a[A + "out_w"].T), "wr": chunks(a[M + "Wr"].T),
        "ln_gb": _np.stack([a[A + "ln_g"], a[A + "ln_b"]])[None],
        "w_all": cat([
            wiT[0:128],
            _np.stack([wiT[128:192, :, 0:384], wiT[128:192, :, 384:768]]).reshape(128, 8, 384),
            a[M + "bi"].reshape(8, 6, 128).transpose(2, 0, 1),
            a[M + "Wo"].transpose(0, 2, 1).reshape(8, 6, 128, 192).transpose(2, 0, 1, 3).reshape(128, 8, 1152),
            _np.zeros((128, 8, 2), _np.float32)], axis=2).reshape(128, -1),
        "bo": cat([cat([a[M + "bo"], _np.zeros((24, 192), _np.float32)])] * 4),
    }
    nc = _bacc.Bacc("TRN2", target_bir_lowering=False, num_devices=1)
    arrays, args = {}, {}
    for name, v in d.items():
        v = _np.ascontiguousarray(v)
        arrays["in_" + name] = v
        args[name] = nc.dram_tensor("in_" + name, v.shape, _mybir.dt.from_np(v.dtype), kind="ExternalInput").ap()
    out = nc.dram_tensor("out_0", (4, 384, 192), F32, kind="ExternalOutput").ap()
    build(nc, args, out)
    r = _run(nc, [arrays], core_ids=[0])
    return r.results[0]["out_0"]
```

```python
from contextlib import ExitStack

import concourse.bass as bass
import numpy as np
from concourse import mybir

F32 = mybir.dt.float32
BF16 = mybir.dt.bfloat16
I32 = mybir.dt.int32
U32 = mybir.dt.uint32
ALU = mybir.AluOpType
ACT = mybir.ActivationFunctionType
AX_X = mybir.AxisListType.X

P = 128
NB = 4
C = 192
CB = C - P
NJ = 3
L = NJ * P
NT = NJ * NB
EMB = 64
GROUP = 16
PATCH = [3, 12, 48]
N_IMG = 256
G0, G1, G2 = 32, 8, 2
S = 16
K = 4
U = 2 * L
E = 8
F = 768
FC = F // P
FH = F // 2
W_UA, W_UB, W_BI = 0, F, F + FH
W_DN = W_BI + FC
W_E = W_DN + FC * C + 2
LATE = 2
CHUNK = P + K - 1
CW = C + CB
TOPK = 2
NTOK = NB * L
NX = 4
MT = (TOPK * NTOK + E * (P - 1)) // P
EPS = 1e-5
LOG1P_SCALE = 0.0051261021233726485
LOG1P_PAIRS = [(-2.32946677, 0.4346165), (-0.08503787, 3.2738333), (-1.43055841, 2.7158022), (1.00917879, 1.1116931)]

C_ID = 0
C_UP = C_ID + P
C_ROW = C_UP + P
C_NEG = C_ROW + 2 * S
C_E8 = C_NEG + 2
C_M12 = C_E8 + E
C_MASK = C_M12 + NT
C_IOTA = C_MASK + E * NT
C_TOK = C_IOTA + P
C_PAD = C_TOK + TOPK * NT
C_EPS = C_PAD + 1
C_LOG = C_EPS + 1
N_CST = C_LOG + len(LOG1P_PAIRS)

H_W, H_CB, H_DTB, H_D, H_A = 0, 4, 5, 6, 7
N_CH = H_A + S


def constants():
    c = np.zeros((P, N_CST), np.float32)
    c[:, C_ID:C_ID + P] = np.eye(P)
    c[:, C_UP:C_UP + P] = np.triu(np.ones((P, P)), 1)
    for pair in range(2):
        for part in range(3):
            for s in range(S):
                c[64 * pair + S * part + s, C_ROW + S * pair + s] = 1
        c[64 * pair + S:64 * pair + 3 * S, C_NEG] = -1
        c[64 * pair + 2 * S:64 * pair + 3 * S, C_NEG + 1] = -1
    c[:, C_E8:C_E8 + E] = np.arange(E)
    c[:, C_M12:C_M12 + NT] = P * np.arange(NT)
    c[:, C_MASK:C_MASK + E * NT] = (np.arange(E * NT) % NT != 0)
    c[:, C_IOTA:C_IOTA + P] = np.arange(P)
    j, b = np.divmod(np.arange(NT), NB)
    for k in range(TOPK):
        c[:, C_TOK + NT * k:C_TOK + NT * (k + 1)] = TOPK * (np.arange(P)[:, None] + L * b + P * j) + k + 1
    c[:, C_PAD] = TOPK * NTOK + np.arange(P) + 1
    c[:, C_EPS] = EPS
    c[:, C_LOG:] = [a for a, _ in LOG1P_PAIRS]
    return c


def interpolation(n_in, copies):
    pos = np.clip((np.arange(N_IMG) + 0.5) * (n_in / N_IMG) - 0.5, 0, n_in - 1)
    lo = np.floor(pos).astype(int)
    hi = np.minimum(lo + 1, n_in - 1)
    m = np.zeros((n_in, N_IMG), np.float32)
    m[lo, np.arange(N_IMG)] += 1 - (pos - lo)
    m[hi, np.arange(N_IMG)] += pos - lo
    out = np.zeros((copies, n_in, copies, N_IMG), np.float32)
    for k in range(copies):
        out[k, :, k] = m
    return out.reshape(copies * n_in, copies, N_IMG)


def build(nc, d, out):
    with ExitStack() as ctx:
        def sb(name, shape, dt=F32):
            return ctx.enter_context(nc.sbuf_tensor(name, shape, dt))

        def sem(name):
            return ctx.enter_context(nc.semaphore(name))

        cst = sb("cst", [P, N_CST])
        gidx = sb("gidx", [P, G0 + G1 + G2], I32)
        chan = sb("chan", [P, 2, N_CH])
        ln_gb = sb("ln_gb", [P, 2, C])
        b12 = sb("b12", [P, 1])
        b0 = sb("b0", [EMB, 1])
        ip_a = sb("ip_a", [P, 2 * C])
        ip_b = sb("ip_b", [CB, 2 * C])
        dw = sb("dw", [P, 2, C])
        bc = sb("bc", [P, 2, 2, 64])
        ow = sb("ow", [P, 2, C])
        wr = sb("wr", [P, 2, E])
        bo = sb("bo", [P, C])
        w_all = sb("w_all", [P, E * W_E])

        h_tok = sb("h_tok", [P, NJ, NB, C])
        xn = sb("xn", [P, NJ, NB, C])
        x_cm = sb("x_cm", [P, 6 * (L + K - 1)])
        u_cm = sb("u_cm", [P, 6 * L])
        z_cm = sb("z_cm", [P, 6 * L])
        dt_cm = sb("dt_cm", [P, 6 * L])
        dtu_cm = sb("dtu_cm", [P, 6 * L])
        y_cm = sb("y_cm", [P, W_E])
        decay = sb("decay", [P, 2, 2, L])
        drive = sb("drive", [P, 2, L])
        state = sb("state", [P, 2, L])
        hc = sb("hc", [P, 2, L])
        pick = sb("pick", [P, 3, S, P], BF16)
        b_parts = sb("b_parts", [P, 2, L], BF16)
        c_parts = sb("c_parts", [P, 2, L], BF16)
        a_neg = sb("a_neg", [P, 2, S])
        ones_sq = sb("ones_sq", [P, P])
        stats = sb("stats", [P, NB, 6])
        mv = sb("mv", [P, 3, NT, 2])
        std = sb("std", [P, 3, NT])
        rstd = sb("rstd", [P, 3, NT])
        shift = sb("shift", [P, NB])
        gate = sb("gate", [P, TOPK, NT])
        gtmp = sb("gtmp", [P, 2, NT])
        tiles = sb("tiles", [P, E])
        ends = sb("ends", [P, E])
        first = sb("first", [P, E])
        tok_in = sb("tok_in", [P, MT], I32)
        tok_out = sb("tok_out", [P, MT], I32)
        gate_s = sb("gate_s", [P, MT])
        texi = sb("texi", [1, MT], I32)

        taken = 0

        def early(parts, n):
            nonlocal taken
            taken += n
            return w_all[0:parts, taken - n:taken]

        g0 = early(P, G0 * 12).rearrange("p (d r) -> p d r", d=G0)
        g1 = early(P, G1 * 48).rearrange("p (d r) -> p d r", d=G1)
        g2 = early(P, G2 * 192).rearrange("p (d r) -> p d r", d=G2)
        r0 = early(P, 384)
        r1 = early(P, 384)
        t0 = early(48, 1024)
        t1 = early(96, 512)
        t2 = early(48, 1024)
        y1 = early(P, 2 * EMB)
        y2 = early(64, EMB)
        i1 = early(P, 512)
        i2 = early(64, 1024)
        ycat_hi = early(P, NB * N_IMG)
        ycat_lo = early(EMB + 1, NB * P)
        w2T = early(PATCH[2], GROUP * EMB).rearrange("p (k e) -> p k e", k=GROUP)
        w0T = early(PATCH[0] * GROUP, EMB)
        w1T = early(96, 2 * EMB).rearrange("p (k e) -> p k e", k=2)
        wf_hi = early(P, C)
        wf_lo = early(EMB + 1, C)
        xt_a = drive[:, :, :].rearrange("p a c -> p (a c)")[:, 0:512]
        xt_b = state[:, :, :].rearrange("p a c -> p (a c)")[0:CB, 0:512]
        scan_w = (E - LATE) * W_E

        def halves(t):
            return t.rearrange("p (a c) -> p a c", a=2)

        drives = [drive[:, :, :], halves(w_all[:, scan_w:scan_w + U])]
        states = [state[:, :, :], halves(w_all[:, scan_w + U:scan_w + 2 * U])]
        hcs = [hc[:, :, :], halves(w_all[:, scan_w + 2 * U:scan_w + 3 * U])]
        c_sb = [halves(x_cm[:, 0:U]), halves(x_cm[:, U:2 * U])]
        squares = [w_all[:, scan_w + 6 * CHUNK * i:scan_w + 6 * CHUNK * (i + 1)] for i in range(len(LOG1P_PAIRS))]
        rest = [w_all[:, scan_w + (24 + 2 * i) * CHUNK:scan_w + (26 + 2 * i) * CHUNK] for i in range(2)]
        free = [t[:, :, :, :].rearrange("p a b c -> p (a b c)") if t is decay else t[:, :, :].rearrange("p a c -> p (a c)")
                for t in (decay, state, drive)]
        used = 0

        def table(parts, *dims):
            nonlocal used
            size = int(np.prod(dims))
            if used + size > free[0].shape[1]:
                free.pop(0)
                used = 0
            t = free[0][0:parts, used:used + size]
            used += size
            if len(dims) == 1:
                return t
            names = "abc"[:len(dims)]
            return t.rearrange(f"p ({' '.join(names)}) -> p {' '.join(names)}", **dict(zip(names, dims)))

        logit = table(P, NT, E)
        top_v = table(P, NT, 8)
        top_i = table(P, NT, 8).bitcast(U32)
        idf = table(P, NT, TOPK)
        pad_at = table(P, MT)
        hot = table(P, TOPK, NT, E)
        cnt = table(P, E, NT)
        run = table(P, E, NT)
        cmp12 = table(P, E, NT)
        pos = table(P, NT, E)
        pos_k = table(P, TOPK, NT, E)
        slot_f = table(P, TOPK * NT)
        slot_i = table(P, 3, TOPK * NT).bitcast(I32)
        digit = table(P, 2, TOPK * NT)
        tcmp = table(1, MT, E)
        tex = table(1, MT)
        xf = dt_cm[:, :].rearrange("p (t c) -> p t c", t=NT)
        rr = dtu_cm[:, :].rearrange("p (t c) -> p t c", t=NT)
        xft_a = [u_cm[:, 512 * n:512 * n + 512] for n in range(2)]
        xft_b = [u_cm[0:CB, 1024 + 512 * n:1536 + 512 * n] for n in range(2)]
        x_in = dt_cm[:, 0:NX * CW].rearrange("p (n c) -> p n c", n=NX)
        xe = u_cm[:, 512:1024].rearrange("p (n c) -> p n c", n=2)
        hid = [u_cm[:, 1024:1792], z_cm[:, 0:F]]
        y_out = u_cm[:, 1792:1792 + 2 * C].rearrange("p (n c) -> p n c", n=2)
        w_now = [x_cm[:, 0:W_E], y_cm[:, 0:W_E]]
        at_lo = [z_cm[:, 0:NT * P].rearrange("p (t s) -> p t s", t=NT),
                 dtu_cm[:, 0:NT * P].rearrange("p (t s) -> p t s", t=NT)]
        at_hi = dtu_cm[:, 1536:1536 + TOPK * NT * MT].rearrange("p (k t m) -> p k t m", k=TOPK, t=NT)
        what = u_cm[:, 0:TOPK * NT * 2 * MT].rearrange("p (k t w m) -> p k t w m", k=TOPK, t=NT, w=2)
        gate_e8 = z_cm[:, 1536:1920].rearrange("p (t e) -> p t e", t=NT)
        gate_t = z_cm[:, 1920:2304]
        y_two = w_all[:, 0:NT * TOPK * C].rearrange("p (t k c) -> p t k c", t=NT, k=TOPK)

        ps = ctx.enter_context(nc.psum_tensor("ps", [P, 8, 512], F32))

        def q3(t):
            return t.rearrange("p (q n) -> p q n", q=6)

        u3, z3, dt3, dtu3, y3 = (q3(t[:, 0:6 * L]) for t in (u_cm, z_cm, dt_cm, dtu_cm, y_cm))
        x3 = q3(x_cm[:, :])
        ident = cst[:, C_ID:C_ID + P]
        x_dram = nc.dram_tensor("x_dram", [NTOK, CW], F32, kind="Internal").ap()
        y_dram = nc.dram_tensor("y_dram", [TOPK * NTOK + P, C], F32, kind="Internal").ap()

        ld_idx = sem("ld_idx")
        ld_cst = sem("ld_cst")
        ld_tok = sem("ld_tok")
        ld_in = sem("ld_in")
        ld_mix = sem("ld_mix")
        ld_exp = sem("ld_exp")
        gath12 = sem("gath12")
        gath0 = [sem("gath0_0"), sem("gath0_1")]
        dve_set = sem("dve_set")
        rearr = sem("rearr")
        pe_tok = sem("pe_tok")
        ev_tok = sem("ev_tok")
        h_ready = sem("h_ready")
        ln_step = sem("ln_step")
        std_rdy = sem("std_rdy")
        rstd_rdy = sem("rstd_rdy")
        xn_ready = sem("xn_ready")
        xt_ps = sem("xt_ps")
        xt_ready = sem("xt_ready")
        u_ready = sem("u_ready")
        z_ready = sem("z_ready")
        dt_ps = sem("dt_ps")
        bc_ps = sem("bc_ps")
        a_exp = sem("a_exp")
        x_ps = sem("x_ps")
        z_ps = sem("z_ps")
        x_out = sem("x_out")
        conv_step = sem("conv_step")
        split_step = sem("split_step")
        linear_rdy = sem("linear_ready")
        abs_rdy = sem("abs_ready")
        exp_rdy = sem("exp_ready")
        square_rdy = sem("square_ready")
        log_step = sem("log_step")
        dt_rdy = sem("dt_ready")
        dtu_rdy = sem("dtu_ready")
        du_rdy = sem("du_ready")
        decay_rdy = sem("decay_rdy")
        b_wide = sem("b_wide")
        c_wide = sem("c_wide")
        c_copied = sem("c_copied")
        driven = sem("driven")
        scanned = sem("scanned")
        hc_rdy = sem("hc_rdy")
        summed = sem("summed")
        y_step = sem("y_step")
        attn_ps = sem("attn_ps")
        hb_rdy = sem("hb_ready")
        post = sem("post")
        mean_rdy = sem("mean_ready")
        logit_rdy = sem("logit_ready")
        whats = sem("whats")
        xf_rdy = sem("xf_rdy")
        shift_rdy = sem("shift_ready")
        xft_ps = sem("xft_ps")
        xft_rdy = sem("xft_rdy")
        logit_ps = sem("logit_ps")
        route = sem("route")
        gate_e = sem("gate_e")
        cnt_ps = sem("cnt_ps")
        tok_ps = sem("tok_ps")
        gt_ps = sem("gt_ps")
        gt_rdy = sem("gt_rdy")
        bo_ps = sem("bo_ps")
        h_final = sem("h_final")
        x_sent = sem("x_sent")
        xin_l = [sem(f"xin_l{q}") for q in range(NX)]
        xe_ps = sem("xe_ps")
        xe_rdy = sem("xe_rdy")
        up_rdy = sem("up_weights")
        dn_rdy = sem("down_weights")
        up_ps = sem("up_ps")
        hid_rdy = sem("hid_rdy")
        down_ps = sem("down_ps")
        y_rdy = sem("y_rdy")
        y_sent = sem("y_sent")
        y_back = [sem(f"y_back{j}") for j in range(NJ)]
        summed_up = sem("summed_up")
        summed_pool = sem("summed_pool")
        out_st = sem("out_st")

        N_TOK, N_IN, N_MIX = 10, 2, 6
        JS = [2, 0, 1]
        US = [2, 0, 1]
        RUNS = [(2 * P + K - 1, L), (0, P), (P, 2 * P + K - 1)]
        WARM = {"input weights": 10, "interpolated levels": 8, "fine tokens": 3, "last convolution": 10,
                "last steps": 24, "router's rows": 32, "later rows": 3, "last rows": 2, "slots": 8, "first tile": 4}
        NORMS = [(1, 0), (1, 1), (2, 0), (1, 2), (2, 1), (2, 2)]

        def chan_group(u):
            return 1 if u == 2 else 0

        def unit(t, u, lo=0, n=L):
            return t[:, 2 * u:2 * u + 2, lo:lo + n]

        def run_of(t3, n):
            lo, hi = RUNS[n]
            return (t3[:, 0:NB, lo:hi].rearrange("p (b k) n -> p b k n", b=2), t3[:, NB:6, lo:hi])

        def dt_bank(n):
            w = RUNS[n][1] - RUNS[n][0]
            return (ps[:, 5:7, 0:2 * CHUNK].rearrange("p b (k n) -> p b k n", k=2)[:, :, :, 0:w],
                    ps[:, 5:7, 2 * CHUNK:2 * CHUNK + w])

        def bc_bank(w, n):
            return ps[:, 1 + w, 0:2 * CHUNK].rearrange("p (i n) -> p i n", i=2)[:, :, 0:RUNS[n][1] - RUNS[n][0]]

        def packed(t, n, a):
            w = RUNS[n][1] - RUNS[n][0]
            return t[:, 0:a * w].rearrange("p (a n) -> p a n", a=a)

        def bank2(b, n=L):
            return ps[:, b:b + 2, 0:n]

        block = ctx.enter_context(nc.Block())

        def expert_loop(eng, step):
            for i in range(NX):
                step(i, i)
            with eng.Fori(1, (MT - 2) // NX) as m:
                for q in range(NX):
                    step(m * NX + q, q)
            for i in range(NX * ((MT - 2) // NX), MT):
                step(i, i % NX)

        def is_at_least(i, n):
            return not isinstance(i, int) or i >= n

        def is_below(i, n):
            return not isinstance(i, int) or i < n

        T_T1, T_T2, T_L12, T_UP = 1, 2, 3, 4
        V_T1, V_T2, V_L12, V_UP = 1, 3, 4, 6
        ROUTE_CNT = 3
        ROUTE_EXP = 4
        ROUTE_GATE = 9
        ROUTE_HI = 24
        ROUTE_LO = 25
        ROUTE_TOKENS = 34
        ROUTE_SCALES = 35

        @block.sync
        def _(sp):
            sp.dma_start(gidx[:, :], d["gidx"]).then_inc(ld_idx, 16)
            sp.dma_start(h_tok[:, 2, :, :], d["txt"].rearrange("b p c -> p b c")).then_inc(h_ready, 16)
            sp.dma_start(cst[:, :], d["cst"]).then_inc(ld_cst, 16)
            for dst, name in ((ip_a[:, :], "ip_a"), (ip_b[:, :], "ip_b")):
                sp.dma_start(dst, d[name]).then_inc(ld_in, 16)
            for dst, name in ((w0T, "w0T"), (w1T, "w1T"), (w2T, "w2T"), (b12[:, :], "b12"),
                              (b0[:, :], "b0"), (wf_hi, "wf_hi"), (wf_lo, "wf_lo"), (i1, "i1"), (i2, "i2"),
                              (chan[:, :, :], "chan")):
                sp.dma_start(dst, d[name]).then_inc(ld_tok, 16)
            for dst, name in ((dw[:, :, :], "dw"), (bc[:, :, :, :], "bc")):
                sp.dma_start(dst, d[name]).then_inc(ld_mix, 16)
            for dst, name in ((ow[:, :, :], "ow"), (wr[:, :, :], "wr"), (bo[:, :], "bo")):
                sp.dma_start(dst, d[name]).then_inc(ld_mix, 16)
            sp.dma_start(ln_gb[:, :, :], d["ln_gb"].to_broadcast([P, 2, C])).then_inc(ld_mix, 16)
            sp.wait_ge(ev_tok, V_UP + 6)
            for e in range(E):
                if e == E - LATE:
                    sp.wait_ge(y_step, 2 * 3)
                sp.dma_start(w_all[:, W_E * e:W_E * e + W_E], d["w_all"][:, W_E * e:W_E * e + W_E]).then_inc(ld_exp, 16)
            for j in range(NJ):
                sp.wait_ge(xf_rdy, j + 1)
                for c0, c1, src in ((0, C, 0), (C, CW, P)):
                    sp.dma_start(x_dram.rearrange("(b j p) c -> j p b c", b=NB, j=NJ)[j, :, :, c0:c1],
                                 xf[:, NB * j:NB * j + NB, src:C]).then_inc(x_sent, 16)
            sp.wait_ge(y_sent, 16 * MT)
            y_rows = y_dram[0:TOPK * NTOK, :].rearrange("(b j p k) c -> j p b (k c)", b=NB, j=NJ, k=TOPK)
            for j in range(NJ):
                sp.dma_start(y_two[:, NB * j:NB * j + NB, :, :].rearrange("p b k c -> p b (k c)"), y_rows[j])\
                    .then_inc(y_back[j], 16)
            for j in range(NJ):
                sp.wait_ge(summed_up, TOPK * (j + 1))
                sp.wait_ge(summed_pool, TOPK * (j + 1))
                sp.dma_start(out.rearrange("b (j p) c -> j p b c", j=NJ)[j], h_tok[:, j, :, :]).then_inc(out_st, 16)
            sp.wait_ge(out_st, 16 * NJ)

        @block.gpsimd
        def _(pool):
            pool.wait_ge(ld_idx, 16)

            def gather(dst, table, col, signal):
                pool.indirect_dma_start(dst, None, d[table], bass.IndirectOffsetOnAxis(
                    ap=gidx[:, col:col + 1].bitcast(U32), axis=0)).then_inc(signal, 16)

            for n in range(G2):
                gather(g2[:, n, :], "pix2", G0 + G1 + n, gath12)
            for n in range(G1):
                gather(g1[:, n, :], "pix1", G0 + n, gath12)
            for n in range(G0):
                gather(g0[:, n, :], "pix0", n, gath0[n // GROUP])
            pool.wait_ge(ld_mix, 16 * N_MIX)
            pool.wait_ge(xn_ready, NJ)
            for j in range(NJ):
                nc.gpsimd.tensor_tensor(h_tok[:, j, :, :], h_tok[:, j, :, :],
                                        ln_gb[:, 1:2, :].to_broadcast([P, NB, C]), ALU.add).then_inc(hb_rdy, 1)

            def state_output(n, s, p):
                at = s + S * n
                pool.wait_ge(scanned, s + (S * n + 3))
                pool.wait_ge(c_copied, s + (S * n + 1))
                if is_at_least(at, 2):
                    pool.wait_ge(summed, at - 1)
                nc.gpsimd.tensor_tensor(hcs[p], states[p], c_sb[p], ALU.mult).then_inc(hc_rdy, 1)

            for n in range(3):
                state_output(n, 0, 0)
                state_output(n, 1, 1)
                with pool.Fori(1, S // 2) as m:
                    for p in range(2):
                        state_output(n, m * 2 + p, p)
            pool.wait_ge(route, ROUTE_HI)
            for k in range(TOPK):
                nc.gpsimd.tensor_tensor(what[:, k, :, 0, :], at_hi[:, k, :, :],
                                        cst[:, C_TOK + NT * k:C_TOK + NT * (k + 1)].rearrange("p (t o) -> p t o", o=1)
                                        .to_broadcast([P, NT, MT]), ALU.mult)
                nc.gpsimd.tensor_tensor(what[:, k, :, 1, :], at_hi[:, k, :, :],
                                        gate[:, k, :].rearrange("p (t o) -> p t o", o=1).to_broadcast([P, NT, MT]),
                                        ALU.mult).then_inc(whats, 1)
            pool.wait_ge(route, ROUTE_TOKENS)
            pool.wait_ge(x_sent, 16 * 2 * NJ)

            def fetch(i):
                pool.indirect_dma_start(x_in[:, i % NX, :], None, x_dram, bass.IndirectOffsetOnAxis(
                    ap=tok_in[:, i:i + 1].bitcast(U32), axis=0)).then_inc(xin_l[i % NX], 16)

            for i in range(NX):
                fetch(i)
            for i in range(MT):
                if i + NX < MT:
                    pool.wait_ge(xe_ps, i + 1)
                    fetch(i + NX)
                pool.wait_ge(y_rdy, i + 1)
                if i:
                    pool.wait_ge(y_sent, 16 * i)
                pool.indirect_dma_start(y_dram, bass.IndirectOffsetOnAxis(
                    ap=tok_out[:, i:i + 1].bitcast(U32), axis=0), y_out[:, i % 2, :], None).then_inc(y_sent, 16)
            pool.wait_ge(h_final, 1)
            for j in range(NJ):
                pool.wait_ge(y_back[j], 16)
                for k in range(TOPK):
                    nc.gpsimd.tensor_tensor(h_tok[:, j, NB - 1, :], h_tok[:, j, NB - 1, :],
                                            y_two[:, NB * j + NB - 1, k, :], ALU.add).then_inc(summed_pool, 1)
                    pool.wait_ge(summed_pool, TOPK * j + k + 1)

        @block.tensor
        def _(pe):
            def coarse_levels():
                pe.wait_ge(ld_tok, 16 * N_TOK)
                pe.wait_ge(rearr, 1)
                for b in range(NB):
                    mm = nc.tensor.transpose(ps[0:96, 0, P * b:P * b + P], r1[:, 96 * b:96 * b + 96], ident)
                mm.then_inc(pe_tok, 1)
                for n in range(G2):
                    for b in range(NB):
                        mm = nc.tensor.transpose(ps[0:48, 1 + n, P * b:P * b + P], g2[:, n, 48 * b:48 * b + 48], ident)
                mm.then_inc(pe_tok, 1)
                pe.wait_ge(ev_tok, V_T2)
                pe.wait_ge(x_out, 2)
                pe.wait_ge(z_ready, 2)
                for half in range(2):
                    for kh in range(2):
                        nc.tensor.matmul(ps[:, 3, EMB * half:EMB * half + EMB],
                                         t1[:, 256 * kh + P * half:256 * kh + P * half + P],
                                         w1T[:, kh, :], start=(kh == 0), stop=(kh == 1))
                for k in range(GROUP):
                    mm = nc.tensor.matmul(ps[0:64, 4, 0:EMB], t2[:, 64 * k:64 * k + 64], w2T[:, k, :],
                                          start=(k == 0), stop=(k == GROUP - 1))
                mm.then_inc(pe_tok, 1)
                pe.wait_ge(ev_tok, V_L12)
                for b in range(NB):
                    o = ps[:, 5 + b // 2, N_IMG * (b % 2):N_IMG * (b % 2) + N_IMG]
                    nc.tensor.matmul(o[0:64, :], y1[:, EMB * (b // 2):EMB * (b // 2) + EMB],
                                     i1[:, N_IMG * (b % 2):N_IMG * (b % 2) + N_IMG], start=True, stop=True)
                    mm = nc.tensor.matmul(o[64:128, :], y2, i2[:, N_IMG * b:N_IMG * b + N_IMG], start=True, stop=True)
                mm.then_inc(pe_tok, 1)

            def tokens_from_patches(jt):
                base_v = 3 * jt
                pe.wait_ge(rearr, 2 + jt)
                for b in range(NB):
                    mm = nc.tensor.transpose(ps[0:48, 0, P * b:P * b + P],
                                             r0[:, 48 * (NB * jt + b):48 * (NB * jt + b) + 48], ident)
                mm.then_inc(pe_tok, 1)
                pe.wait_ge(ev_tok, V_UP + 1 + base_v)
                nc.tensor.matmul(ps[0:EMB, 0, :], w0T, t0[:, 512 * jt:512 * jt + 512],
                                 start=True, stop=True).then_inc(pe_tok, 1)
                pe.wait_ge(ev_tok, V_UP + 2 + base_v)
                if jt == 1:
                    pe.wait_ge(split_step, 10)
                for b in range(NB):
                    o = ps[:, 1 + b // 2, 256 * (b % 2):256 * (b % 2) + C]
                    c0 = N_IMG * b + P * jt
                    nc.tensor.matmul(o, ycat_hi[:, c0:c0 + P], wf_hi, start=True, stop=False)
                    mm = nc.tensor.matmul(o, ycat_lo[:, P * b:P * b + P], wf_lo,
                                          start=False, stop=True)
                mm.then_inc(pe_tok, 1)

            def others(xz):
                for half in range(2):
                    o = ps[64 * half:64 * half + 64, 4, 256 * xz:256 * xz + 256]
                    w = slice(C * xz + P, C * xz + C)
                    c = slice(256 * half, 256 * half + 256)
                    nc.tensor.matmul(o, ip_a[:, w], xt_a[:, c], start=True, stop=False)
                    mm = nc.tensor.matmul(o, ip_b[:, w], xt_b[:, c], start=False, stop=True)
                return mm

            def in_projection(n):
                pe.wait_ge(xn_ready, n + 1)
                j = JS[n]
                if n:
                    pe.wait_ge(z_ready, 2 * n)
                for b in range(NB):
                    nc.tensor.transpose(ps[:, 7, P * b:P * b + P], xn[:, j, b, 0:P], ident)
                for b in range(NB):
                    mm = nc.tensor.transpose(ps[0:CB, 4, P * b:P * b + P], xn[:, j, b, P:C], ident)
                mm.then_inc(xt_ps, 1)
                pe.wait_ge(xt_ready, 2 * n + 2)

                nc.tensor.matmul(ps[:, 3, :], ip_a[:, 0:P], xt_a, start=True, stop=False)
                nc.tensor.matmul(ps[:, 3, :], ip_b[:, 0:P], xt_b, start=False, stop=True)
                others(0).then_inc(x_ps, 1)

            def gate_projection(n):
                nc.tensor.matmul(ps[:, 7, :], ip_a[:, C:C + P], xt_a, start=True, stop=False)
                nc.tensor.matmul(ps[:, 7, :], ip_b[:, C:C + P], xt_b, start=False, stop=True)
                pe.wait_ge(x_out, 2 * n + 2)
                others(1).then_inc(z_ps, 1)

            def from_u(o, wa, wb, b, n):
                hb = 64 * (b // 2)
                t = slice(*RUNS[n])
                nc.tensor.matmul(o, wa, u3[:, b, t], start=True, stop=False)
                return nc.tensor.matmul(o, wb[hb:hb + 64], u3[hb:hb + 64, 4 + b % 2, t], start=False, stop=True)

            def scan_inputs(n):
                pe.wait_ge(u_ready, 2 * n + 2)
                if n:
                    pe.wait_ge(abs_rdy, 2 * n)
                    pe.wait_ge(linear_rdy, 2 * n)
                    pe.wait_ge(split_step, 10 * n)
                w = RUNS[n][1] - RUNS[n][0]
                for b in range(NB):
                    from_u(ps[:, 5 + b // 2, CHUNK * (b % 2):CHUNK * (b % 2) + w], dw[:, 0, 0:P], dw[:, 1, 0:P], b, n)
                for b in range(NB):
                    mm = from_u(ps[64 * (b // 2):64 * (b // 2) + 64, 5 + b % 2, 2 * CHUNK:2 * CHUNK + w],
                                dw[:, 0, P:C], dw[:, 1, P:C], b, n)
                mm.then_inc(dt_ps, 1)
                pe.wait_ge(ev_tok, V_UP + 3 * min(n + 1, 2))
                for m in range(2):
                    for b in range(NB):
                        mm = from_u(ps[64 * (b // 2):64 * (b // 2) + 64, 1 + m, CHUNK * (b % 2):CHUNK * (b % 2) + w],
                                    bc[:, 0, m, :], bc[:, 1, m, :], b, n)
                    mm.then_inc(bc_ps, 1)

            def keep_warm(n, bank):
                for _ in range(n):
                    nc.tensor.matmul(ps[:, bank, 0:256], ident, cst[:, 0:256], start=True, stop=True)

            pe.wait_ge(ld_cst, 16)
            keep_warm(WARM["input weights"], 0)
            pe.wait_ge(ld_in, 16 * N_IN)
            in_projection(0)
            gate_projection(0)
            coarse_levels()
            pe.wait_ge(ev_tok, V_UP)
            keep_warm(WARM["interpolated levels"], 0)
            tokens_from_patches(0)
            pe.wait_ge(ld_mix, 16 * N_MIX)
            scan_inputs(0)
            in_projection(1)
            keep_warm(WARM["fine tokens"], 0)
            tokens_from_patches(1)
            gate_projection(1)
            scan_inputs(1)
            in_projection(2)
            gate_projection(2)
            keep_warm(WARM["last convolution"], 0)
            scan_inputs(2)
            keep_warm(WARM["last steps"], 0)
            pe.wait_ge(dve_set, 5)
            pe.wait_ge(split_step, 10 * 3)
            pe.wait_ge(dtu_rdy, 3)
            pe.wait_ge(abs_rdy, 2 * 3)

            def spread_b(n, s, p):
                at = s + S * n
                if is_at_least(at, 2):
                    pe.wait_ge(driven, at - 1)
                for i in range(2):
                    mm = nc.tensor.matmul(ps[:, 2 * p + i, 0:L],
                                          pick[:, US[n], bass.ds(s, 1), :].rearrange("p o c -> p (o c)"),
                                          b_parts[:, i, :], start=True, stop=True)
                mm.then_inc(b_wide, 1)

            def spread_c(n, s):
                at = s + S * n
                if is_at_least(at, 1):
                    pe.wait_ge(c_copied, at)
                for i in range(2):
                    mm = nc.tensor.matmul(ps[:, 4 + i, 0:L],
                                          pick[:, US[n], bass.ds(s, 1), :].rearrange("p o c -> p (o c)"),
                                          c_parts[:, i, :], start=True, stop=True)
                mm.then_inc(c_wide, 1)

            def sum_states(n, s, p):
                if n and isinstance(s, int) and s == 0:
                    pe.wait_ge(y_step, 2 * n - 1)
                pe.wait_ge(hc_rdy, s + (S * n + 1))
                for i in range(2):
                    mm = nc.tensor.matmul(ps[:, 6 + i, 0:L], ident, hcs[p][:, i, :],
                                          start=isinstance(s, int) and s == 0, stop=isinstance(s, int) and s == S - 1)
                mm.then_inc(summed, 1)

            for n in range(3):
                for s in range(2):
                    spread_b(n, s, s)
                    spread_c(n, s)
                    if n:
                        sum_states(n - 1, S - 2 + s, s)
                spread_b(n, 2, 0)
                spread_c(n, 2)
                sum_states(n, 0, 0)
                spread_b(n, 3, 1)
                spread_c(n, 3)
                sum_states(n, 1, 1)
                with pe.Fori(2, S // 2) as m:
                    for p in range(2):
                        spread_b(n, m * 2 + p, p)
                        spread_c(n, m * 2 + p)
                        sum_states(n, m * 2 + (p - 2), p)
            for s in range(2):
                sum_states(2, S - 2 + s, s)
            pe.wait_ge(driven, 3 * S)
            pe.wait_ge(c_copied, 3 * S)
            for j in range(NJ):
                for h in range(2):
                    nc.tensor.matmul(ps[:, 2 * j + h, :].rearrange("p (b c) -> p b c", b=2)[:, :, 0:C], ident,
                                     xn[:, j, 2 * h:2 * h + 2, :], start=True, stop=False, skip_group_check=True)
            pe.wait_ge(y_step, 2 * 3)
            for j in range(NJ):
                for b in range(NB):
                    o = ps[:, 2 * j + b // 2, 256 * (b % 2):256 * (b % 2) + C]
                    hb = 64 * (b // 2)
                    nc.tensor.matmul(o, y3[:, b, P * j:P * j + P], ow[:, 0, :], start=False, stop=False,
                                     skip_group_check=True)
                    mm = nc.tensor.matmul(o, y3[hb:hb + 64, 4 + b % 2, P * j:P * j + P], ow[hb:hb + 64, 1, :],
                                          start=False, stop=True, skip_group_check=True)
                mm.then_inc(attn_ps, 1)
            keep_warm(WARM["router's rows"], 7)

            def router_transposes(j):
                pe.wait_ge(xf_rdy, j + 1)
                if j:
                    pe.wait_ge(xft_rdy, 2 * j)
                for b in range(NB):
                    nc.tensor.transpose(ps[:, 6, P * b:P * b + P], xf[:, NB * j + b, 0:P], ident)
                for b in range(NB):
                    mm = nc.tensor.transpose(ps[0:CB, 7, P * b:P * b + P], xf[:, NB * j + b, P:C], ident)
                mm.then_inc(xft_ps, 1)

            def router_logits(j):
                pe.wait_ge(xft_rdy, 2 * j + 2)
                for b in range(NB):
                    o = ps[:, 2 * j, E * b:E * b + E]
                    nc.tensor.matmul(o, xft_a[j % 2][:, P * b:P * b + P], wr[:, 0, :], start=True, stop=False)
                    mm = nc.tensor.matmul(o, xft_b[j % 2][:, P * b:P * b + P], wr[0:CB, 1, :], start=False, stop=True)
                mm.then_inc(logit_ps, 1)

            router_transposes(0)
            keep_warm(WARM["later rows"], 1)
            router_transposes(1)
            router_logits(0)
            keep_warm(WARM["last rows"], 1)
            router_transposes(2)
            router_logits(1)
            router_logits(2)
            pe.wait_ge(route, ROUTE_CNT)
            cv = cnt[:, :, :].rearrange("p e t -> p (e t)")
            nc.tensor.matmul(ps[:, 5, 0:E * NT], cst[:, C_UP:C_UP + P], cv, start=True, stop=True)
            nc.tensor.matmul(ps[:, 6, 0:E * NT], ones_sq[:, :], cv, start=True, stop=True).then_inc(cnt_ps, 1)
            pe.wait_ge(route, ROUTE_GATE)
            for j in range(NJ):
                mm = nc.tensor.transpose(ps[:, 7, P * j:P * j + P],
                                         gate_e8[:, NB * j:NB * j + NB, :].rearrange("p t e -> p (t e)"), ident)
            mm.then_inc(gt_ps, 1)
            keep_warm(WARM["slots"], 0)
            pe.wait_ge(gt_rdy, 1)
            for k in range(TOPK):
                pe.wait_ge(route, ROUTE_LO + k)
                pe.wait_ge(whats, k + 1)
                for t in range(NT):
                    mm = nc.tensor.matmul(ps[:, 7, 0:2 * MT], at_lo[k][:, t, :],
                                          what[:, k, t, :, :].rearrange("p w m -> p (w m)"),
                                          start=(k == 0 and t == 0), stop=(k == TOPK - 1 and t == NT - 1))
            mm.then_inc(tok_ps, 1)
            keep_warm(WARM["first tile"], 2)

            def x_transposed(i, q):
                p = q % 2
                pe.wait_ge(xin_l[q], 16 * (i // NX + 1) if isinstance(i, int) else (i - q) * (16 // NX) + 16)
                if is_at_least(i, 2):
                    pe.wait_ge(xe_rdy, i - 1)
                for c in range(2):
                    mm = nc.tensor.transpose(ps[:, p, P * c:P * c + P], x_in[:, q, P * c:P * c + P], ident)
                mm.then_inc(xe_ps, 1)

            def up(i, p):
                pe.wait_ge(xe_rdy, i + 1)
                pe.wait_ge(up_rdy, i + 1)
                if is_at_least(i, 2):
                    pe.wait_ge(hid_rdy, i - 1)
                w = w_now[p]
                for f in range(FC):
                    nc.tensor.matmul(ps[:, 2 + 2 * p + f // 3, P * (f % 3):P * (f % 3) + P],
                                     w[:, W_UA + P * f:W_UA + P * f + P], xe[:, p, 0:P],
                                     start=(f % 3 == 0), stop=False, skip_group_check=True)
                for f in range(FC // 2):
                    for half in range(2):
                        r = slice(CB * half, CB * half + CB)
                        mm = nc.tensor.matmul(ps[:, 2 + 2 * p + half, P * f:P * f + P],
                                              w[r, W_UB + P * f:W_UB + P * f + P], xe[r, p, P:2 * P],
                                              start=False, stop=True, skip_group_check=True)
                mm.then_inc(up_ps, 1)

            def down(i, p):
                pe.wait_ge(hid_rdy, i + 1)
                pe.wait_ge(dn_rdy, i + 1)
                if is_at_least(i, 2):
                    pe.wait_ge(y_rdy, i - 1)
                for f in range(FC):
                    mm = nc.tensor.matmul(ps[:, 6 + p, 0:C], hid[p][:, P * f:P * f + P],
                                          w_now[p][:, W_DN + C * f:W_DN + C * f + C], start=(f == 0), stop=(f == FC - 1))
                mm.then_inc(down_ps, 1)

            x_transposed(0, 0)
            x_transposed(1, 1)
            up(0, 0)

            def expert_tile(i, q):
                p = q % 2
                if is_below(i, MT - 2):
                    x_transposed(i + 2, (q + 2) % NX)
                if is_below(i, MT - 1):
                    up(i + 1, 1 - p)
                down(i, p)
            expert_loop(pe, expert_tile)
            pe.wait_ge(xe_rdy, MT)
            pe.wait_ge(hid_rdy, MT)
            for b in range(NB):
                for j in range(2):
                    mm = nc.tensor.matmul(ps[:, b, 256 * j:256 * j + C], gate_t[32 * b:32 * b + E, P * j:P * j + P],
                                          bo[32 * b:32 * b + E, :], start=True, stop=True)
            mm.then_inc(bo_ps, 1)
            for b in range(NB):
                if b >= 2:
                    pe.wait_ge(bo_ps, b)
                nc.tensor.matmul(ps[:, 4 + b % 2, 256 * (b // 2):256 * (b // 2) + C],
                                 gate_t[32 * b:32 * b + E, 2 * P:3 * P], bo[32 * b:32 * b + E, :],
                                 start=True, stop=True).then_inc(bo_ps, 1)

        @block.scalar
        def _(act):
            def coarse_levels():
                act.wait_ge(gath12, 16 * (G2 + G1))
                nc.scalar.activation(r1.rearrange("p (b d c) -> p d b c", b=NB, d=G1),
                                     g1.rearrange("p d (b c) -> p d b c", b=NB), ACT.Copy).then_inc(rearr, 1)
                act.wait_ge(pe_tok, T_T1)
                nc.scalar.activation(t1.rearrange("p (k b t) -> p b k t", k=2, b=NB),
                                     ps[0:96, 0, :].rearrange("p (b k t) -> p b k t", b=NB, k=2), ACT.Copy).then_inc(ev_tok, 1)
                act.wait_ge(pe_tok, T_T2)
                for n in range(G2):
                    nc.scalar.activation(t2[:, 512 * n:512 * n + 512].rearrange("p (k b t) -> p b k t", k=8, b=NB),
                                         ps[0:48, 1 + n, :].rearrange("p (b k t) -> p b k t", b=NB, k=8), ACT.Copy)\
                        .then_inc(ev_tok, 1)
                act.wait_ge(pe_tok, T_L12)
                nc.scalar.activation(y1, ps[:, 3, 0:2 * EMB], ACT.Copy)
                nc.scalar.activation(y2, ps[0:64, 4, 0:EMB], ACT.Copy).then_inc(ev_tok, 1)
                act.wait_ge(pe_tok, T_UP)
                act.wait_ge(ld_tok, 16 * N_TOK)
                for h in range(2):
                    nc.scalar.activation(ycat_hi[:, 512 * h:512 * h + 512], ps[:, 5 + h, :], ACT.Identity,
                                         bias=b12[:, 0:1]).then_inc(ev_tok, 1)

            def patch_order(jt):
                act.wait_ge(gath0[jt], 16 * GROUP)
                nc.scalar.activation(
                    r0[:, 192 * jt:192 * jt + 192].rearrange("p (b k c) -> p k b c", b=NB, k=GROUP),
                    g0[:, GROUP * jt:GROUP * jt + GROUP, :].rearrange("p k (b c) -> p k b c", b=NB),
                    ACT.Copy).then_inc(rearr, 1)

            def patches_transposed(jt):
                act.wait_ge(pe_tok, T_UP + 1 + 3 * jt)
                nc.scalar.activation(t0[:, 512 * jt:512 * jt + 512], ps[0:48, 0, :], ACT.Copy).then_inc(ev_tok, 1)

            def fine_level(jt):
                act.wait_ge(pe_tok, T_UP + 2 + 3 * jt)
                nc.scalar.activation(ycat_lo[0:EMB, :], ps[0:EMB, 0, :], ACT.Identity,
                                     bias=b0[:, 0:1]).then_inc(ev_tok, 1)

            def fused_tokens(jt):
                act.wait_ge(pe_tok, T_UP + 3 + 3 * jt)
                for h in range(2):
                    ins = nc.scalar.activation(h_tok[:, jt, 2 * h:2 * h + 2, :],
                                               ps[:, 1 + h, :].rearrange("p (b c) -> p b c", b=2)[:, :, 0:C], ACT.Copy)
                ins.then_inc(ev_tok, 1)

            def deviation(norm, j, n):
                act.wait_ge(mean_rdy, n + 1)
                t = slice(NB * j, NB * j + NB)
                nc.scalar.activation(std[:, norm, t], mv[:, norm, t, 1], ACT.Sqrt, bias=cst[:, C_EPS:C_EPS + 1])\
                    .then_inc(std_rdy, 1)

            def transposed(n):
                act.wait_ge(xt_ps, n + 1)
                nc.scalar.activation(xt_a, ps[:, 7, :], ACT.Copy).then_inc(xt_ready, 1)
                nc.scalar.activation(xt_b, ps[0:CB, 4, :], ACT.Copy).then_inc(xt_ready, 1)

            def x_of(n):
                j = JS[n]
                t = slice(K - 1 + P * j, K - 1 + P * j + P)
                act.wait_ge(x_ps, n + 1)
                nc.scalar.activation(x3[:, NB:6, t], ps[:, 4, 0:256].rearrange("p (b t) -> p b t", b=2),
                                     ACT.Copy).then_inc(x_out, 1)
                nc.scalar.activation(x3[:, 0:NB, t], ps[:, 3, :].rearrange("p (b t) -> p b t", b=NB),
                                     ACT.Copy).then_inc(x_out, 1)

            def z_of(n):
                j = JS[n]
                return ((z3[:, 0:NB, P * j:P * j + P], ps[:, 7, :].rearrange("p (b t) -> p b t", b=NB)),
                        (z3[:, NB:6, P * j:P * j + P], ps[:, 4, 256:512].rearrange("p (b t) -> p b t", b=2)))

            def gate_of(n):
                act.wait_ge(z_ps, n + 1)
                for dst, src in z_of(n):
                    nc.scalar.activation(dst, src, ACT.Silu).then_inc(z_ready, 1)

            def convolved(n):
                for g in range(2):
                    act.wait_ge(conv_step, 8 * n + K * (g + 1))
                    nc.scalar.activation(run_of(u3, n)[g], run_of(y3, n)[g], ACT.Silu,
                                         bias=chan[:, g, H_CB:H_CB + 1]).then_inc(u_ready, 1)

            def exponentials(n):
                act.wait_ge(dt_ps, n + 1)
                for g in range(2):
                    nc.scalar.activation(run_of(dt3, n)[g], dt_bank(n)[g], ACT.Abs,
                                         bias=chan[:, g, H_DTB:H_DTB + 1]).then_inc(abs_rdy, 1)
                act.wait_ge(abs_rdy, 2 * n + 2)
                e = dt3[:, :, RUNS[n][0]:RUNS[n][1]]
                nc.scalar.activation(e, e, ACT.Exp, scale=-1.0).then_inc(exp_rdy, 1)

            def squares_of(n, start=0, stop=len(LOG1P_PAIRS)):
                act.wait_ge(exp_rdy, n + 1)
                if n:
                    act.wait_ge(log_step, 4 * n)
                for i in range(start, stop):
                    nc.scalar.activation(packed(squares[i], n, 6), dt3[:, :, RUNS[n][0]:RUNS[n][1]], ACT.Square,
                                         bias=cst[:, C_LOG + i:C_LOG + i + 1]).then_inc(square_rdy, 1)

            def skip_term(n):
                act.wait_ge(dt_rdy, n + 1)
                for g in range(2):
                    nc.scalar.activation(run_of(y3, n)[g], run_of(u3, n)[g], ACT.Copy,
                                         scale=chan[:, g, H_D:H_D + 1]).then_inc(du_rdy, 1)

            act.wait_ge(ld_cst, 16)
            deviation(0, JS[0], 0)
            transposed(0)
            x_of(0)
            gate_of(0)
            coarse_levels()
            act.wait_ge(ld_tok, 16 * N_TOK)
            convolved(0)
            patch_order(0)
            patches_transposed(0)
            fine_level(0)
            fused_tokens(0)
            deviation(0, JS[1], 1)
            transposed(1)
            exponentials(0)
            x_of(1)
            patch_order(1)
            squares_of(0, 0, 2)
            patches_transposed(1)
            squares_of(0, 2, 4)
            fine_level(1)
            convolved(1)
            fused_tokens(1)
            deviation(0, JS[2], 2)
            act.wait_ge(z_ps, 2)
            for dst, src in z_of(1):
                nc.scalar.activation(dst, src, ACT.Copy).then_inc(z_ready, 1)
            transposed(2)
            exponentials(1)
            nc.scalar.activation(a_neg[:, :, :], chan[:, :, H_A:H_A + S], ACT.Exp).then_inc(a_exp, 1)
            x_of(2)
            squares_of(1)
            skip_term(0)
            gate_of(2)
            convolved(2)
            act.wait_ge(z_ready, 2 * NJ)
            for dst, _ in z_of(1):
                nc.scalar.activation(dst, dst, ACT.Silu).then_inc(z_ready, 1)
            exponentials(2)
            squares_of(2)
            skip_term(1)
            act.wait_ge(a_exp, 2)

            def decay_of(n, s, p):
                g = chan_group(US[n])
                act.wait_ge(scanned, s + (S * n + 1))
                nc.scalar.activation(decay[:, p, :, 1:L], unit(dt3, US[n], 1, L - 1), ACT.Exp,
                                     scale=a_neg[:, g, bass.ds(s, 1)]).then_inc(decay_rdy, 1)

            def copy_c(n, s, p):
                at = s + S * n
                act.wait_ge(c_wide, s + (S * n + 1))
                if is_at_least(at, 2):
                    act.wait_ge(hc_rdy, at - 1)
                nc.scalar.activation(c_sb[p], bank2(4), ACT.Copy).then_inc(c_copied, 1)

            act.wait_ge(dt_rdy, 3)
            decay_of(0, 0, 0)
            for n in range(3):
                decay_of(n, 1, 1)
                copy_c(n, 0, 0)
                if n == 0:
                    skip_term(2)
                with act.Fori(1, S // 2) as m:
                    for p in range(2):
                        decay_of(n, m * 2 + p, p)
                        copy_c(n, m * 2 + (p - 1), 1 - p)
                if n < 2:
                    decay_of(n + 1, 0, 0)
                copy_c(n, S - 1, 1)

            def router_input(j):
                act.wait_ge(xft_ps, j + 1)
                if j == 2:
                    act.wait_ge(logit_ps, 1)
                nc.scalar.activation(xft_a[j % 2], ps[:, 6, :], ACT.Copy).then_inc(xft_rdy, 1)
                nc.scalar.activation(xft_b[j % 2], ps[0:CB, 7, :], ACT.Copy).then_inc(xft_rdy, 1)

            def logits(j):
                act.wait_ge(logit_ps, j + 1)
                nc.scalar.activation(logit[:, NB * j:NB * j + NB, :],
                                     ps[:, 2 * j, 0:NB * E].rearrange("p (t e) -> p t e", t=NB), ACT.Copy).then_inc(logit_rdy, 1)

            act.wait_ge(y_step, 2 * 3)

            def first_router_rows():
                j = 0
                act.wait_ge(shift_rdy, 1)
                for t in range(NB * j, NB * j + NB):
                    ins = nc.scalar.activation(xf[:, t, :], h_tok[:, j, t % NB, :], ACT.Identity,
                                               scale=rstd[:, 2, t:t + 1], bias=shift[:, t:t + 1])
                ins.then_inc(xf_rdy, 1)

            for n, (norm, j) in enumerate(NORMS):
                if n == 5:
                    first_router_rows()
                    router_input(0)
                deviation(norm, j, NJ + n)
            router_input(1)
            logits(0)
            router_input(2)
            logits(1)
            logits(2)
            act.wait_ge(route, ROUTE_EXP)
            nc.scalar.activation(gtmp[:, 0, :], gtmp[:, 0, :], ACT.Exp).then_inc(gate_e, 1)
            act.wait_ge(gt_ps, 1)
            nc.scalar.activation(gate_t, ps[:, 7, 0:NJ * P], ACT.Copy).then_inc(gt_rdy, 1)
            nc.scalar.activation(std[:, 0, 0:1], std[:, 0, 1:2], ACT.Gelu)

            def hidden(i, p):
                act.wait_ge(up_ps, i + 1)
                if is_at_least(i, 2):
                    act.wait_ge(down_ps, i - 1)
                for f in range(FC):
                    ins = nc.scalar.activation(hid[p][:, P * f:P * f + P],
                                               ps[:, 2 + 2 * p + f // 3, P * (f % 3):P * (f % 3) + P],
                                               ACT.Gelu, bias=w_now[p][:, W_BI + f:W_BI + f + 1])
                ins.then_inc(hid_rdy, 1)

            act.wait_ge(route, ROUTE_SCALES)
            hidden(0, 0)

            def expert_tile(i, q):
                p = q % 2
                if is_below(i, MT - 1):
                    hidden(i + 1, 1 - p)
                act.wait_ge(down_ps, i + 1)
                if is_at_least(i, 2):
                    act.wait_ge(y_sent, 16 * (i - 1))
                nc.scalar.activation(y_out[:, p, :], ps[:, 6 + p, 0:C], ACT.Copy,
                                     scale=gate_s[:, bass.ds(i, 1)]).then_inc(y_rdy, 1)
            expert_loop(act, expert_tile)

        @block.vector
        def _(dve):
            v = nc.vector
            dve.wait_ge(ld_cst, 16)
            v.memset(ycat_lo[EMB:EMB + 1, :], 1.0).then_inc(dve_set, 1)
            v.memset(x3[:, :, 0:K - 1], 0.0).then_inc(dve_set, 1)

            def scan_constants():
                rows = cst[:, C_ROW:C_ROW + 2 * S].rearrange("p (u s) -> p u s", u=2)
                v.tensor_copy(pick[:, 0:2, :, :].rearrange("p u s c -> p (u s) c"),
                              cst[:, C_ROW:C_ROW + 2 * S].rearrange("p (n o) -> p n o", o=1)
                              .to_broadcast([P, 2 * S, P])).then_inc(dve_set, 1)
                for half in range(2):
                    v.tensor_copy(pick[:, 2, :, 64 * half:64 * half + 64],
                                  rows[:, half, :].rearrange("p (s o) -> p s o", o=1).to_broadcast([P, S, 64]))\
                        .then_inc(dve_set, 1)
                v.memset(ones_sq[:, :], 1.0).then_inc(dve_set, 1)

            groups = 0
            inverses = 0

            def means(norm, j, src):
                nonlocal groups
                for b in range(NB):
                    ins = v.bn_stats(stats[:, b, :], src[b])
                ins.then_inc(ln_step, 1)
                groups += 1
                dve.wait_ge(ln_step, groups)
                for b in range(NB):
                    ins = v.bn_aggr(mv[:, norm, NB * j + b, :], stats[:, b, :])
                ins.then_inc(mean_rdy, 1)
                dve.wait_ge(mean_rdy, groups)

            def inverse(norm, j, n):
                nonlocal inverses
                inverses += 1
                dve.wait_ge(std_rdy, n + 1)
                t = slice(NB * j, NB * j + NB)
                v.reciprocal(rstd[:, norm, t], std[:, norm, t]).then_inc(rstd_rdy, 1)
                dve.wait_ge(rstd_rdy, inverses)

            def normalise(norm, dst, src, t):
                return v.tensor_scalar(dst, src, mv[:, norm, t, 0:1], rstd[:, norm, t:t + 1], ALU.subtract, ALU.mult)

            def input_norm(n):
                j = JS[n]
                if n == 0:
                    dve.wait_ge(h_ready, 16)
                else:
                    dve.wait_ge(ev_tok, V_UP + 3 * n)
                means(0, j, [h_tok[:, j, b, :] for b in range(NB)])
                inverse(0, j, n)
                for b in range(NB):
                    ins = normalise(0, xn[:, j, b, :], h_tok[:, j, b, :], NB * j + b)
                ins.then_inc(xn_ready, 1)

            def convolution(n):
                dve.wait_ge(x_out, 2 * n + 2)
                lo, hi = RUNS[n]
                for g, q in ((0, slice(0, NB)), (1, slice(NB, 6))):
                    at = 8 * n + K * g
                    y = y3[:, q, lo:hi]
                    v.tensor_scalar(y, x3[:, q, lo + K - 1:hi + K - 1], chan[:, g, H_W + K - 1:H_W + K], None,
                                    ALU.mult).then_inc(conv_step, 1)
                    for k in range(K - 1):
                        dve.wait_ge(conv_step, at + k + 1)
                        v.scalar_tensor_tensor(y, x3[:, q, lo + k:hi + k], chan[:, g, H_W + k:H_W + k + 1], y,
                                               ALU.mult, ALU.add).then_inc(conv_step, 1)

            def split(n):
                lo, hi = RUNS[n]
                part = [b_parts[:, :, lo:hi], c_parts[:, :, lo:hi]]
                hi_lo = [packed(rest[w], n, 2) for w in range(2)]
                for w in range(2):
                    dve.wait_ge(bc_ps, 2 * n + w + 1)
                    v.tensor_copy(part[w], bc_bank(w, n)).then_inc(split_step, 1)
                for w in range(2):
                    dve.wait_ge(split_step, 10 * n + w + 1)
                    v.scalar_tensor_tensor(hi_lo[w], part[w], cst[:, C_NEG:C_NEG + 1], bc_bank(w, n), ALU.mult, ALU.add)\
                        .then_inc(split_step, 1)
                for w in range(2):
                    dve.wait_ge(split_step, 10 * n + w + 3)
                    v.tensor_copy(part[w], hi_lo[w]).then_inc(split_step, 1)
                for w in range(2):
                    dve.wait_ge(split_step, 10 * n + w + 5)
                    v.scalar_tensor_tensor(hi_lo[w], part[w], cst[:, C_NEG + 1:C_NEG + 2], hi_lo[w], ALU.mult, ALU.add)\
                        .then_inc(split_step, 1)
                for w in range(2):
                    dve.wait_ge(split_step, 10 * n + w + 7)
                    v.tensor_copy(part[w], hi_lo[w]).then_inc(split_step, 1)

            def linear(n):
                dve.wait_ge(abs_rdy, 2 * n + 2)
                for g in range(2):
                    v.tensor_scalar(run_of(dtu3, n)[g], dt_bank(n)[g], chan[:, g, H_DTB:H_DTB + 1], 0.0,
                                    ALU.add, ALU.max).then_inc(linear_rdy, 1)

            def softplus(n):
                lo, hi = RUNS[n]
                e, poly, dtu = dt3[:, :, lo:hi], y3[:, :, lo:hi], dtu3[:, :, lo:hi]
                for i, (_, b) in enumerate(LOG1P_PAIRS):
                    dve.wait_ge(square_rdy, 4 * n + i + 1)
                    if i:
                        dve.wait_ge(log_step, 4 * n + i)
                    v.scalar_tensor_tensor(poly, packed(squares[i], n, 6), b, e if i == 0 else poly,
                                           ALU.add, ALU.mult).then_inc(log_step, 1)
                dve.wait_ge(log_step, 4 * n + 4)
                dve.wait_ge(linear_rdy, 2 * n + 2)
                v.scalar_tensor_tensor(e, poly, LOG1P_SCALE, dtu, ALU.mult, ALU.add).then_inc(dt_rdy, 1)
                dve.wait_ge(dt_rdy, n + 1)
                v.tensor_tensor(dtu, e, u3[:, :, lo:hi], ALU.mult).then_inc(dtu_rdy, 1)

            input_norm(0)
            scan_constants()
            dve.wait_ge(ld_tok, 16 * N_TOK)
            dve.wait_ge(dve_set, 2)
            convolution(0)
            input_norm(1)
            split(0)
            linear(0)
            convolution(1)
            softplus(0)
            input_norm(2)
            split(1)
            linear(1)
            dve.wait_ge(a_exp, 1)
            v.tensor_scalar(a_neg[:, :, :], a_neg[:, :, :], -1.0, None, ALU.mult).then_inc(a_exp, 1)
            convolution(2)
            for p in range(2):
                v.memset(decay[:, p, :, 0:1], 0.0).then_inc(scanned, 1)
            softplus(1)
            linear(2)
            softplus(2)
            split(2)
            dve.wait_ge(dtu_rdy, 3)

            def drive_step(n, s, p):
                at = s + S * n
                dve.wait_ge(b_wide, s + (S * n + 1))
                if is_at_least(at, 2):
                    dve.wait_ge(scanned, at + 1)
                v.tensor_tensor(drives[p], unit(dtu3, US[n]), bank2(2 * p), ALU.mult).then_inc(driven, 1)

            def scan_step(n, s, p):
                at = s + S * n
                dve.wait_ge(driven, s + (S * n + 1))
                dve.wait_ge(decay_rdy, s + (S * n + 1))
                if is_at_least(at, 2):
                    dve.wait_ge(hc_rdy, at - 1)
                v.tensor_tensor_scan(states[p].rearrange("p a c -> p (a c)"),
                                     decay[:, p, :, :].rearrange("p a c -> p (a c)"),
                                     drives[p].rearrange("p a c -> p (a c)"), 0.0,
                                     ALU.mult, ALU.add).then_inc(scanned, 1)

            def unit_output(n):
                u = US[n]
                dve.wait_ge(summed, S * (n + 1))
                dve.wait_ge(du_rdy, 2 * NJ)
                v.tensor_tensor(unit(y3, u), bank2(6), unit(y3, u), ALU.add).then_inc(y_step, 1)
                dve.wait_ge(y_step, 2 * n + 1)
                dve.wait_ge(z_ready, 2 * NJ + 2)
                v.tensor_tensor(unit(y3, u), unit(y3, u), unit(z3, u), ALU.mult).then_inc(y_step, 1)

            def state_pass(n, s, p):
                drive_step(n, s, p)
                scan_step(n, s, p)

            for n in range(3):
                state_pass(n, 0, 0)
                state_pass(n, 1, 1)
                if n:
                    unit_output(n - 1)
                with dve.Fori(1, S // 2) as m:
                    state_pass(n, m * 2, 0)
                    state_pass(n, m * 2 + 1, 1)
            unit_output(2)
            at = 0

            def step(ins):
                nonlocal at
                at += 1
                ins.then_inc(post, 1)
                dve.wait_ge(post, at)

            def residual(j):
                dve.wait_ge(attn_ps, j + 1)
                both = [ps[:, 2 * j + b // 2, 256 * (b % 2):256 * (b % 2) + C] for b in range(NB)]
                means(1, j, both)
                for b in range(NB):
                    t = NB * j + b
                    ins = v.scalar_tensor_tensor(rr[:, t, :], both[b], mv[:, 1, t, 0:1], ln_gb[:, 0, :],
                                                 ALU.subtract, ALU.mult)
                ins.then_inc(post, 1)

            def new_h(j):
                inverse(1, j, NJ + NORMS.index((1, j)))
                for b in range(NB):
                    t = NB * j + b
                    ins = v.scalar_tensor_tensor(h_tok[:, j, b, :], rr[:, t, :], rstd[:, 1, t:t + 1], h_tok[:, j, b, :],
                                                 ALU.mult, ALU.add)
                step(ins)
                means(2, j, [h_tok[:, j, b, :] for b in range(NB)])

            def router_shift():
                inverse(2, 0, NJ + NORMS.index((2, 0)))
                t = slice(0, NB)
                v.scalar_tensor_tensor(shift[:, t], mv[:, 2, t, 0], -1.0, rstd[:, 2, t], ALU.mult, ALU.mult)\
                    .then_inc(shift_rdy, 1)

            def router_rows(j):
                inverse(2, j, NJ + NORMS.index((2, j)))
                if j == 1:
                    dve.wait_ge(xf_rdy, 1)
                for b in range(NB):
                    ins = normalise(2, xf[:, NB * j + b, :], h_tok[:, j, b, :], NB * j + b)
                ins.then_inc(xf_rdy, 1)

            def largest(j):
                dve.wait_ge(logit_rdy, j + 1)
                for t in range(NB * j, NB * j + NB):
                    ins = v.max(top_v[:, t, :], logit[:, t, :])
                step(ins)
                for t in range(NB * j, NB * j + NB):
                    ins = v.max_index(top_i[:, t, :], top_v[:, t, :], logit[:, t, :])
                ins.then_inc(post, 1)

            dve.wait_ge(hb_rdy, NJ)
            v.memset(gate_e8, 0.0).then_inc(dve_set, 1)
            residual(0)
            at += 1
            residual(1)
            at += 1
            dve.wait_ge(post, at)
            new_h(0)
            residual(2)
            at += 1
            router_shift()
            dve.wait_ge(post, at)
            new_h(1)
            new_h(2)
            router_rows(1)
            router_rows(2)
            for j in range(NJ):
                largest(j)
                at += 1
            dve.wait_ge(post, at)
            at_r = 0

            def rt(ins):
                nonlocal at_r
                at_r += 1
                ins.then_inc(route, 1)
                dve.wait_ge(route, at_r)

            rt(v.tensor_copy(idf[:, :, :], top_i[:, :, 0:TOPK]))
            e8 = cst[:, C_E8:C_E8 + E].rearrange("p (o e) -> p o e", o=1).to_broadcast([P, NT, E])
            for k in range(TOPK):
                ins = v.tensor_tensor(hot[:, k, :, :], idf[:, :, k:k + 1].to_broadcast([P, NT, E]), e8, ALU.is_equal)
            rt(ins)
            rt(v.tensor_tensor(cnt[:, :, :].rearrange("p e t -> p t e"), hot[:, 0, :, :], hot[:, 1, :, :], ALU.add))
            rt(v.tensor_tensor(gtmp[:, 0, :], top_v[:, :, 1], top_v[:, :, 0], ALU.subtract))
            assert at_r == ROUTE_EXP
            dve.wait_ge(gate_e, 1)
            rt(v.tensor_scalar(gtmp[:, 1, :], gtmp[:, 0, :], 1.0, None, ALU.add))
            rt(v.reciprocal(gate[:, 0, :], gtmp[:, 1, :]))
            rt(v.tensor_tensor(gate[:, 1, :], gtmp[:, 0, :], gate[:, 0, :], ALU.mult))
            for k in range(TOPK):
                ins = v.tensor_tensor(pos_k[:, k, :, :], hot[:, k, :, :],
                                      gate[:, k, :].rearrange("p (t o) -> p t o", o=1).to_broadcast([P, NT, E]), ALU.mult)
            rt(ins)
            dve.wait_ge(dve_set, 6)
            rt(v.tensor_tensor(gate_e8[:, :, 0:E], pos_k[:, 0, :, :], pos_k[:, 1, :, :], ALU.add))
            assert at_r == ROUTE_GATE, at_r
            dve.wait_ge(cnt_ps, 1)
            tot = ps[:, 6, 0:E * NT]
            runf = run[:, :, :].rearrange("p e t -> p (e t)")
            rt(v.tensor_tensor_scan(runf, cst[:, C_MASK:C_MASK + E * NT], tot, 0.0, ALU.mult, ALU.add))
            m12 = cst[:, C_M12:C_M12 + NT].rearrange("p (o m) -> p o m", o=1).to_broadcast([P, E, NT])
            rt(v.tensor_tensor(cmp12[:, :, :], run[:, :, NT - 1:NT].to_broadcast([P, E, NT]), m12, ALU.is_gt))
            rt(v.tensor_reduce(tiles[:, :], cmp12[:, :, :], AX_X, ALU.add))
            rt(v.tensor_tensor_scan(ends[:, :], ones_sq[:, 0:E], tiles[:, :], 0.0, ALU.mult, ALU.add))
            rt(v.tensor_tensor(first[:, :], ends[:, :], tiles[:, :], ALU.subtract))
            rt(v.tensor_tensor(runf, runf, tot, ALU.subtract))
            rt(v.tensor_tensor(runf, runf, ps[:, 5, 0:E * NT], ALU.add))
            rt(v.scalar_tensor_tensor(pos[:, :, :].rearrange("p t e -> p e t"),
                                      first[:, :].rearrange("p (e o) -> p e o", o=1).to_broadcast([P, E, NT]),
                                      float(P), run[:, :, :], ALU.mult, ALU.add))
            for k in range(TOPK):
                ins = v.tensor_tensor(pos_k[:, k, :, :], hot[:, k, :, :], pos[:, :, :], ALU.mult)
            rt(ins)
            rt(v.tensor_reduce(slot_f, pos_k[:, :, :, :].rearrange("p k t e -> p (k t) e"), AX_X, ALU.add))
            rt(v.tensor_copy(slot_i[:, 0, :], slot_f))
            rt(v.tensor_scalar(slot_i[:, 1, :], slot_i[:, 0, :], 7, None, ALU.logical_shift_right))
            rt(v.tensor_scalar(slot_i[:, 2, :], slot_i[:, 0, :], P - 1, None, ALU.bitwise_and))
            rt(v.tensor_copy(digit[:, :, :], slot_i[:, 1:3, :]))
            dig = digit[:, :, :].rearrange("p d (k t o) -> p d k t o", k=TOPK, o=1)
            iota_m = cst[:, C_IOTA:C_IOTA + MT].rearrange("p (o m) -> p o m", o=1).to_broadcast([P, NT, MT])
            iota_p = cst[:, C_IOTA:C_IOTA + P].rearrange("p (o m) -> p o m", o=1).to_broadcast([P, NT, P])
            for k in range(TOPK):
                ins = v.tensor_tensor(at_hi[:, k, :, :], dig[:, 0, k, :, :].to_broadcast([P, NT, MT]), iota_m, ALU.is_equal)
            rt(ins)
            assert at_r == ROUTE_HI, at_r
            for k in range(TOPK):
                rt(v.tensor_tensor(at_lo[k], dig[:, 1, k, :, :].to_broadcast([P, NT, P]), iota_p, ALU.is_equal))
            t31 = cst[0:P, C_IOTA:C_IOTA + MT].rearrange("p (m o) -> p m o", o=1)[0:1].to_broadcast([1, MT, E])
            rt(v.tensor_tensor(tcmp[:, :, :], ends[0:1, :].rearrange("p (o e) -> p o e", o=1).to_broadcast([1, MT, E]),
                               t31, ALU.is_le))
            rt(v.tensor_reduce(tex[:, :], tcmp[:, :, :], AX_X, ALU.add))
            rt(v.tensor_scalar(tex[:, :], tex[:, :], float(E - 1), None, ALU.min))
            rt(v.tensor_copy(texi[:, :], tex[:, :]))
            dve.wait_ge(tok_ps, 1)
            rt(v.tensor_scalar(pad_at, ps[:, 7, 0:MT], 0.0, cst[:, C_PAD:C_PAD + 1], ALU.is_equal, ALU.mult))
            rt(v.scalar_tensor_tensor(tok_out[:, :], ps[:, 7, 0:MT], -1.0, pad_at, ALU.add, ALU.add))
            rt(v.tensor_scalar(tok_in[:, :], tok_out[:, :], 1, None, ALU.logical_shift_right))
            rt(v.tensor_scalar(tok_in[:, :], tok_in[:, :], NTOK - 1, None, ALU.min))
            rt(v.tensor_copy(gate_s[:, :], ps[:, 7, MT:2 * MT]))
            assert at_r == ROUTE_SCALES, at_r

            def up_weights(i, p):
                e = dve.value_load(texi[0:1, bass.ds(i, 1)], min_val=0, max_val=E - 1)
                if is_at_least(i, 2):
                    dve.wait_ge(hid_rdy, i - 1)
                v.tensor_copy(w_now[p][:, 0:W_DN], w_all[:, bass.ds(e * W_E, W_DN)]).then_inc(up_rdy, 1)
                return e

            def down_weights(i, p, e):
                if is_at_least(i, 2):
                    dve.wait_ge(down_ps, i - 1)
                v.tensor_copy(w_now[p][:, W_DN:W_E], w_all[:, bass.ds(e * W_E + W_DN, W_E - W_DN)]).then_inc(dn_rdy, 1)

            def tokens(i, p):
                dve.wait_ge(xe_ps, i + 1)
                if is_at_least(i, 2):
                    dve.wait_ge(up_ps, i - 1)
                v.tensor_copy(xe[:, p, :], ps[:, p, 0:2 * P]).then_inc(xe_rdy, 1)

            dve.wait_ge(ld_exp, 16 * E)
            e = up_weights(0, 0)
            tokens(0, 0)
            down_weights(0, 0, e)

            def expert_tile(i, q):
                p = q % 2
                if is_below(i, MT - 1):
                    tokens(i + 1, 1 - p)
                    e = up_weights(i + 1, 1 - p)
                    down_weights(i + 1, 1 - p, e)
            expert_loop(dve, expert_tile)
            dve.wait_ge(bo_ps, 1)
            for b in range(NB):
                v.tensor_tensor(h_tok[:, 0:2, b, :], h_tok[:, 0:2, b, :],
                                ps[:, b, :].rearrange("p (j c) -> p j c", j=2)[:, :, 0:C], ALU.add)
            dve.wait_ge(bo_ps, 1 + NB)
            for h in range(2):
                ins = v.tensor_tensor(h_tok[:, 2, 2 * h:2 * h + 2, :], h_tok[:, 2, 2 * h:2 * h + 2, :],
                                      ps[:, 4:6, 256 * h:256 * h + C], ALU.add)
            ins.then_inc(h_final, 1)
            dve.wait_ge(h_final, 1)
            for j in range(NJ):
                dve.wait_ge(y_back[j], 16)
                for k in range(TOPK):
                    v.tensor_tensor(h_tok[:, j, 0:NB - 1, :], h_tok[:, j, 0:NB - 1, :],
                                    y_two[:, NB * j:NB * j + NB - 1, k, :],
                                    ALU.add).then_inc(summed_up, 1)
                    dve.wait_ge(summed_up, TOPK * j + k + 1)


def kernel(**x):
    import numpy as _np
    import concourse.bacc as _bacc
    from concourse import mybir as _mybir
    from concourse.bass_utils import run_bass_kernel_spmd as _run

    a = {n: _np.asarray(v) for n, v in x.items()}
    cat = _np.concatenate

    def patches(p):
        h = 64 // p
        t = a["x"].reshape(4, 3, h, p, h, p).transpose(2, 4, 0, 3, 5, 1)
        return t.reshape(h * h, 4 * p * p * 3)

    def chunks(w):
        return _np.stack([w[0:128], cat([w[128:192], w[128:192]])], axis=1)

    def parts(w):
        return cat([w.T, w.T, w.T, _np.zeros_like(w.T)], axis=1)

    A, M, T = "L0_attn_", "L0_ffn_", "L0_tok_"
    wfT = a[T + "Wf"].T
    wiT = a[M + "Wi"].transpose(2, 0, 1)
    d = {
        "pix0": patches(1), "pix1": patches(2), "pix2": patches(4),
        "gidx": cat([a[T + "idx0"].reshape(2, 128, 16).transpose(1, 0, 2).reshape(128, 32),
                     a[T + "idx1"].reshape(64, 2, 8).transpose(1, 0, 2).reshape(128, 8),
                     a[T + "idx2"].reshape(16, 2, 8).transpose(2, 0, 1).reshape(128, 2)], axis=1),
        "txt": a["txt"], "cst": constants(),
        "w0T": a[T + "W0"].T, "w1T": a[T + "W1"].T.reshape(2, 96, 64).transpose(1, 0, 2),
        "w2T": a[T + "W2"].T.reshape(16, 48, 64).transpose(1, 0, 2),
        "b12": cat([a[T + "b1"], a[T + "b2"]])[:, None], "b0": a[T + "b0"][:, None],
        "wf_hi": wfT[64:192], "wf_lo": cat([wfT[0:64], a[T + "bf"][None]]),
        "i1": interpolation(64, 2).reshape(128, 512), "i2": interpolation(16, 4).reshape(64, 1024),
        "chan": chunks(cat([a[A + "conv_w"].reshape(192, 4), a[A + "conv_b"][:, None], a[A + "dt_b"][:, None],
                            a[A + "D_param"][:, None], a[A + "A_log"]], axis=1)),
        "ip_a": a[A + "in_proj_w"].T[0:128], "ip_b": a[A + "in_proj_w"].T[128:192],
        "dw": chunks(a[A + "dt_w"].T),
        "bc": chunks(_np.stack([parts(a[A + "B_w"]), parts(a[A + "C_w"])], axis=1)),
        "ow": chunks(a[A + "out_w"].T), "wr": chunks(a[M + "Wr"].T),
        "ln_gb": _np.stack([a[A + "ln_g"], a[A + "ln_b"]])[None],
        "w_all": cat([
            wiT[0:128],
            _np.stack([wiT[128:192, :, 0:384], wiT[128:192, :, 384:768]]).reshape(128, 8, 384),
            a[M + "bi"].reshape(8, 6, 128).transpose(2, 0, 1),
            a[M + "Wo"].transpose(0, 2, 1).reshape(8, 6, 128, 192).transpose(2, 0, 1, 3).reshape(128, 8, 1152),
            _np.zeros((128, 8, 2), _np.float32)], axis=2).reshape(128, -1),
        "bo": cat([cat([a[M + "bo"], _np.zeros((24, 192), _np.float32)])] * 4),
    }
    nc = _bacc.Bacc("TRN2", target_bir_lowering=False, num_devices=1)
    arrays, args = {}, {}
    for name, v in d.items():
        v = _np.ascontiguousarray(v)
        arrays["in_" + name] = v
        args[name] = nc.dram_tensor("in_" + name, v.shape, _mybir.dt.from_np(v.dtype), kind="ExternalInput").ap()
    out = nc.dram_tensor("out_0", (4, 384, 192), F32, kind="ExternalOutput").ap()
    build(nc, args, out)
    r = _run(nc, [arrays], core_ids=[0])
    return r.results[0]["out_0"]
```
